# Optimizing a Trainium2 kernel written in Bass

```python
import numpy as np
import jax
import jax.numpy as jnp

def _softmax(x, axis=-1):
    return jax.nn.softmax(x, axis=axis)

def _gelu(x):
    return jax.nn.gelu(x, approximate=True)

def _silu(x):
    return jax.nn.silu(x)

def _sigmoid(x):
    return jax.nn.sigmoid(x)

def _layernorm(x, axis=-1, eps=1e-05):
    m = jnp.mean(x, axis=axis, keepdims=True)
    v = jnp.var(x, axis=axis, keepdims=True)
    return (x - m) / jnp.sqrt(v + eps)

def _scatter_add(tgt, idx, src, axis=0):
    return tgt.at[idx].add(src)

def _segment_sum(src, seg, n):
    return jax.ops.segment_sum(src, seg, n)
kernel_name = 'mk_adaln_attn_ffn_d1_seqx_r4_29d3b2'

def setup_inputs(seed: int=0):
    np.random.seed(seed)
    _w = jnp.asarray

    def _rec_inputs():
        import jax
        import jax.numpy as jnp
        _rk = jax.random.key(seed)
        x = -0.0003929 + 0.9999 * jax.random.normal(jax.random.fold_in(_rk, 1), (8, 256, 256), jnp.float32)
        _lenS = 256 - jax.random.randint(jax.random.fold_in(_rk, 7), (8,), 0, max(1, 256 // 4) + 1, jnp.int32)
        _lenS2 = 256 - jax.random.randint(jax.random.fold_in(_rk, 8), (8,), 0, max(1, 256 // 4) + 1, jnp.int32)
        itok_B_0_7 = jax.random.randint(jax.random.fold_in(_rk, 11), (8,), 0, 8, jnp.int32)
        itok_B_0_2 = jax.random.randint(jax.random.fold_in(_rk, 12), (8,), 0, 3, jnp.int32)
        return (x, itok_B_0_7, itok_B_0_2)
    x, itok_B_0_7, itok_B_0_2 = _rec_inputs()

    def _L0_cond_setup():
        import jax, jax.numpy as jnp
        import numpy as np
        B, S, D, F = (32, 128, 256, 1024)
        R_COMMON, R_DOMAIN, E = (16, 16, 8)
        ALPHA = 2.0

        def _expert_lora(x, expert_ids, Wa, Wb):
            Ab = Wa[expert_ids]
            Bb = Wb[expert_ids]
            low = jnp.einsum('bsd,brd->bsr', x, Ab)
            return ALPHA * jnp.einsum('bsr,bor->bso', low, Bb)
        key = jax.random.key(seed)
        ks = jax.random.split(key, 12)
        sd = lambda k, shape: jax.random.normal(k, shape, dtype=jnp.float32) * (1.0 / np.sqrt(shape[-1]))
        return {'hidden_states': jax.random.normal(ks[0], (B, S, D), dtype=jnp.float32), 'expert_ids': jax.random.randint(ks[1], (B,), 0, E, dtype=jnp.int32), 'wi': sd(ks[2], (F, D)), 'wo': sd(ks[3], (D, F)), 'common_wi_a': sd(ks[4], (R_COMMON, D)), 'common_wi_b': sd(ks[5], (F, R_COMMON)), 'common_wo_a': sd(ks[6], (R_COMMON, F)), 'common_wo_b': sd(ks[7], (D, R_COMMON)), 'experts_wi_a': sd(ks[8], (E, R_DOMAIN, D)), 'experts_wi_b': sd(ks[9], (F, R_DOMAIN)) * jnp.ones((E, 1, 1)) * 0.0 + sd(ks[9], (E, F, R_DOMAIN)), 'experts_wo_a': sd(ks[10], (E, R_DOMAIN, F)), 'experts_wo_b': sd(ks[11], (E, D, R_DOMAIN))}
    _L0_cond_all = _L0_cond_setup()
    _L0_cond_in = {k: v for k, v in _L0_cond_all.items() if k in ('wi', 'wo', 'common_wi_a', 'common_wi_b', 'common_wo_a', 'common_wo_b', 'experts_wi_a', 'experts_wi_b', 'experts_wo_a', 'experts_wo_b')}
    del _L0_cond_all

    def _L0_attn_setup():
        import jax, jax.numpy as jnp
        import numpy as np
        H = 256
        I = 512
        E = 8
        TOP_K = 2
        CAP_FACTOR = 1.25
        RMS_EPS = 1e-06
        BIT_EPS = 1e-08

        def rmsnorm(x, eps):
            return x * jax.lax.rsqrt(jnp.mean(x * x, axis=-1, keepdims=True) + eps)

        def activation_quant(x):
            scale = 127.0 / jnp.clip(jnp.max(jnp.abs(x), axis=-1, keepdims=True), 1e-05)
            return jnp.clip(jnp.round(x * scale), -128, 127) / scale

        def weight_quant(w):
            scale = 1.0 / jnp.clip(jnp.mean(jnp.abs(w)), 1e-05)
            return jnp.clip(jnp.round(w * scale), -1, 1) / scale

        def bitlinear(x, w):
            xn = rmsnorm(x, BIT_EPS)
            xq = xn + jax.lax.stop_gradient(activation_quant(xn) - xn)
            wq = w + jax.lax.stop_gradient(weight_quant(w) - w)
            return xq @ wq.T

        def bit_mlp(x, gate_proj_w, down_proj_w):
            gy = bitlinear(x, gate_proj_w)
            gate, y = jnp.split(gy, 2, axis=-1)
            return bitlinear(jax.nn.silu(gate) * y, down_proj_w)
        key = jax.random.key(seed)
        ks = jax.random.split(key, 7)
        s = 0.02
        return {'x': jax.random.normal(ks[0], (4, 512, H), dtype=jnp.float32), 'gate_norm_w': jnp.ones((H,), dtype=jnp.float32), 'gate_w': jax.random.normal(ks[1], (E, H), dtype=jnp.float32) * s, 'shared_gate_w': jax.random.normal(ks[2], (2 * I, H), dtype=jnp.float32) * s, 'shared_down_w': jax.random.normal(ks[3], (H, I), dtype=jnp.float32) * s, 'expert_gate_w': jax.random.normal(ks[4], (E, 2 * I, H), dtype=jnp.float32) * s, 'expert_down_w': jax.random.normal(ks[5], (E, H, I), dtype=jnp.float32) * s}
    _L0_attn_all = _L0_attn_setup()
    _L0_attn_in = {k: v for k, v in _L0_attn_all.items() if k in ('gate_norm_w', 'gate_w', 'shared_gate_w', 'shared_down_w', 'expert_gate_w', 'expert_down_w')}
    del _L0_attn_all

    def _L0_cond2_setup():
        import jax, jax.numpy as jnp
        import numpy as np
        B, S, D, F, E = (8, 512, 256, 1024, 5)

        def _dense(x, wi_, wo_):
            return jax.nn.relu(x @ wi_) @ wo_
        key = jax.random.key(seed)
        ks = jax.random.split(key, 9)
        sc = 0.02
        return {'hidden_states': jax.random.normal(ks[0], (B, S, D), jnp.float32), 'type_label': jax.random.randint(ks[1], (B,), 0, E, jnp.int32), 'wi': jax.random.normal(ks[2], (E, D, F), jnp.float32) * sc, 'wo': jax.random.normal(ks[3], (E, F, D), jnp.float32) * sc, 'swi': jax.random.normal(ks[4], (2, D, F), jnp.float32) * sc, 'swo': jax.random.normal(ks[5], (2, F, D), jnp.float32) * sc, 'g1': jax.random.normal(ks[6], (3 * D, D), jnp.float32) * sc, 'g2': jax.random.normal(ks[7], (D, 3), jnp.float32) * sc}
    _L0_cond2_all = _L0_cond2_setup()
    _L0_cond2_in = {k: v for k, v in _L0_cond2_all.items() if k in ('wi', 'wo', 'swi', 'swo', 'g1', 'g2')}
    del _L0_cond2_all

    def _L0_ffn_setup():
        import jax, jax.numpy as jnp
        import numpy as np
        B, N, D = (4, 512, 256)
        SPARSITY = 0.01
        key = jax.random.key(seed)
        k1, k2, k3 = jax.random.split(key, 3)
        x = jax.random.normal(k1, (B, N, D), dtype=jnp.float32)
        spatial = jax.random.normal(k2, (D, D), dtype=jnp.float32) * 0.02
        freq = jnp.fft.fft(spatial, axis=-1)
        k = int(D * SPARSITY)
        mag = jnp.abs(freq)
        kth = jax.lax.top_k(mag, k)[0][:, -1:]
        w_sparse = jnp.where(mag >= kth, freq, 0.0 + 0j)
        bias = jax.random.normal(k3, (D,), dtype=jnp.float32) * 0.01
        return {'x': x, 'w_freq_real': jnp.real(w_sparse).astype(jnp.float32), 'w_freq_imag': jnp.imag(w_sparse).astype(jnp.float32), 'bias': bias}
    _L0_ffn_all = _L0_ffn_setup()
    _L0_ffn_in = {k: v for k, v in _L0_ffn_all.items() if k in ('w_freq_real', 'w_freq_imag', 'bias')}
    del _L0_ffn_all
    return {'x': x, 'itok_B_0_7': itok_B_0_7, 'itok_B_0_2': itok_B_0_2, 'L0_cond_wi': _L0_cond_in['wi'], 'L0_cond_wo': _L0_cond_in['wo'], 'L0_cond_common_wi_a': _L0_cond_in['common_wi_a'], 'L0_cond_common_wi_b': _L0_cond_in['common_wi_b'], 'L0_cond_common_wo_a': _L0_cond_in['common_wo_a'], 'L0_cond_common_wo_b': _L0_cond_in['common_wo_b'], 'L0_cond_experts_wi_a': _L0_cond_in['experts_wi_a'], 'L0_cond_experts_wi_b': _L0_cond_in['experts_wi_b'], 'L0_cond_experts_wo_a': _L0_cond_in['experts_wo_a'], 'L0_cond_experts_wo_b': _L0_cond_in['experts_wo_b'], 'L0_attn_gate_norm_w': _L0_attn_in['gate_norm_w'], 'L0_attn_gate_w': _L0_attn_in['gate_w'], 'L0_attn_shared_gate_w': _L0_attn_in['shared_gate_w'], 'L0_attn_shared_down_w': _L0_attn_in['shared_down_w'], 'L0_attn_expert_gate_w': _L0_attn_in['expert_gate_w'], 'L0_attn_expert_down_w': _L0_attn_in['expert_down_w'], 'L0_cond2_wi': _L0_cond2_in['wi'], 'L0_cond2_wo': _L0_cond2_in['wo'], 'L0_cond2_swi': _L0_cond2_in['swi'], 'L0_cond2_swo': _L0_cond2_in['swo'], 'L0_cond2_g1': _L0_cond2_in['g1'], 'L0_cond2_g2': _L0_cond2_in['g2'], 'L0_ffn_w_freq_real': _L0_ffn_in['w_freq_real'], 'L0_ffn_w_freq_imag': _L0_ffn_in['w_freq_imag'], 'L0_ffn_bias': _L0_ffn_in['bias']}

def reference(x, itok_B_0_7, itok_B_0_2, L0_cond_wi, L0_cond_wo, L0_cond_common_wi_a, L0_cond_common_wi_b, L0_cond_common_wo_a, L0_cond_common_wo_b, L0_cond_experts_wi_a, L0_cond_experts_wi_b, L0_cond_experts_wo_a, L0_cond_experts_wo_b, L0_attn_gate_norm_w, L0_attn_gate_w, L0_attn_shared_gate_w, L0_attn_shared_down_w, L0_attn_expert_gate_w, L0_attn_expert_down_w, L0_cond2_wi, L0_cond2_wo, L0_cond2_swi, L0_cond2_swo, L0_cond2_g1, L0_cond2_g2, L0_ffn_w_freq_real, L0_ffn_w_freq_imag, L0_ffn_bias):
    import jax
    import jax.numpy as jnp

    def _L0_cond_ref(hidden_states, expert_ids, wi, wo, common_wi_a, common_wi_b, common_wo_a, common_wo_b, experts_wi_a, experts_wi_b, experts_wo_a, experts_wo_b):
        import jax, jax.numpy as jnp
        import numpy as np
        B, S, D, F = (32, 128, 256, 1024)
        R_COMMON, R_DOMAIN, E = (16, 16, 8)
        ALPHA = 2.0

        def _expert_lora(x, expert_ids, Wa, Wb):
            Ab = Wa[expert_ids]
            Bb = Wb[expert_ids]
            low = jnp.einsum('bsd,brd->bsr', x, Ab)
            return ALPHA * jnp.einsum('bsr,bor->bso', low, Bb)
        x = hidden_states
        hidden_i = jnp.einsum('bsd,fd->bsf', x, wi)
        hidden_i += ALPHA * jnp.einsum('bsr,fr->bsf', jnp.einsum('bsd,rd->bsr', x, common_wi_a), common_wi_b)
        hidden_i += _expert_lora(x, expert_ids, experts_wi_a, experts_wi_b)
        hidden_i = jax.nn.relu(hidden_i)
        hidden_o = jnp.einsum('bsf,df->bsd', hidden_i, wo)
        hidden_o += ALPHA * jnp.einsum('bsr,dr->bsd', jnp.einsum('bsf,rf->bsr', hidden_i, common_wo_a), common_wo_b)
        hidden_o += _expert_lora(hidden_i, expert_ids, experts_wo_a, experts_wo_b)
        return hidden_o

    def _L0_attn_ref(x, gate_norm_w, gate_w, shared_gate_w, shared_down_w, expert_gate_w, expert_down_w):
        import jax, jax.numpy as jnp
        import numpy as np
        H = 256
        I = 512
        E = 8
        TOP_K = 2
        CAP_FACTOR = 1.25
        RMS_EPS = 1e-06
        BIT_EPS = 1e-08

        def rmsnorm(x, eps):
            return x * jax.lax.rsqrt(jnp.mean(x * x, axis=-1, keepdims=True) + eps)

        def activation_quant(x):
            scale = 127.0 / jnp.clip(jnp.max(jnp.abs(x), axis=-1, keepdims=True), 1e-05)
            return jnp.clip(jnp.round(x * scale), -128, 127) / scale

        def weight_quant(w):
            scale = 1.0 / jnp.clip(jnp.mean(jnp.abs(w)), 1e-05)
            return jnp.clip(jnp.round(w * scale), -1, 1) / scale

        def bitlinear(x, w):
            xn = rmsnorm(x, BIT_EPS)
            xq = xn + jax.lax.stop_gradient(activation_quant(xn) - xn)
            wq = w + jax.lax.stop_gradient(weight_quant(w) - w)
            return xq @ wq.T

        def bit_mlp(x, gate_proj_w, down_proj_w):
            gy = bitlinear(x, gate_proj_w)
            gate, y = jnp.split(gy, 2, axis=-1)
            return bitlinear(jax.nn.silu(gate) * y, down_proj_w)
        B, S, _ = x.shape
        N = B * S
        capacity = int(N / E * CAP_FACTOR)
        x_flat = x.reshape(N, H)
        shared_out = bit_mlp(x_flat, shared_gate_w, shared_down_w)
        x_norm = rmsnorm(x_flat, RMS_EPS) * gate_norm_w
        gate_logits = x_norm @ gate_w.T
        router_probs = jax.nn.softmax(gate_logits, axis=-1)
        top_k_weights, top_k_indices = jax.lax.top_k(router_probs, TOP_K)
        expert_mask = jnp.zeros((N, E), dtype=top_k_weights.dtype)
        expert_mask = expert_mask.at[jnp.arange(N)[:, None], top_k_indices].set(top_k_weights)
        routed = jnp.zeros_like(x_flat)
        for e in range(E):
            w_e = expert_mask[:, e]
            sel = w_e > 0
            keep = sel & (jnp.cumsum(sel.astype(jnp.int32)) <= capacity)
            w_keep = jnp.where(keep, w_e, 0.0)
            expert_out = bit_mlp(x_flat, expert_gate_w[e], expert_down_w[e])
            routed = routed + w_keep[:, None] * expert_out
        return (routed + shared_out).reshape(B, S, H)

    def _L0_cond2_ref(hidden_states, type_label, wi, wo, swi, swo, g1, g2):
        import jax, jax.numpy as jnp
        import numpy as np
        B, S, D, F, E = (8, 512, 256, 1024, 5)

        def _dense(x, wi_, wo_):
            return jax.nn.relu(x @ wi_) @ wo_
        x = hidden_states
        s0 = _dense(x, swi[0], swo[0])
        s1 = _dense(x, swi[1], swo[1])
        wi_sel = wi[type_label]
        wo_sel = wo[type_label]
        h = jax.nn.relu(jnp.einsum('bsd,bdf->bsf', x, wi_sel))
        eo = jnp.einsum('bsf,bfd->bsd', h, wo_sel)
        gate_in = jnp.concatenate([eo[:, 0], s0[:, 0], s1[:, 0]], axis=-1)
        w = jax.nn.softmax(jax.nn.relu(gate_in @ g1) @ g2, axis=-1)
        w = w[:, :, None, None]
        return eo * w[:, 0] + s0 * w[:, 1] + s1 * w[:, 2]

    def _L0_ffn_ref(x, w_freq_real, w_freq_imag, bias):
        import jax, jax.numpy as jnp
        import numpy as np
        B, N, D = (4, 512, 256)
        SPARSITY = 0.01
        w = jax.lax.complex(w_freq_real, w_freq_imag)
        x_freq = jnp.fft.fft(x, axis=-1)
        y_freq = jnp.einsum('bnd,do->bno', x_freq, w)
        y = jnp.real(jnp.fft.ifft(y_freq, axis=-1))
        return y + bias
    x = x + _L0_attn_ref(_L0_cond_ref(x, itok_B_0_7, L0_cond_wi, L0_cond_wo, L0_cond_common_wi_a, L0_cond_common_wi_b, L0_cond_common_wo_a, L0_cond_common_wo_b, L0_cond_experts_wi_a, L0_cond_experts_wi_b, L0_cond_experts_wo_a, L0_cond_experts_wo_b), L0_attn_gate_norm_w, L0_attn_gate_w, L0_attn_shared_gate_w, L0_attn_shared_down_w, L0_attn_expert_gate_w, L0_attn_expert_down_w)
    x = x + _L0_ffn_ref(_L0_cond2_ref(x, itok_B_0_2, L0_cond2_wi, L0_cond2_wo, L0_cond2_swi, L0_cond2_swo, L0_cond2_g1, L0_cond2_g2), L0_ffn_w_freq_real, L0_ffn_w_freq_imag, L0_ffn_bias)
    return x

_drawn_inputs = setup_inputs


def setup_inputs(seed=0):
    import zlib

    import numpy as np

    out = dict(_drawn_inputs(seed))
    spreads = {'L0_attn_gate_norm_w': (1.0, 0.6)}
    factors = {'L0_cond2_g1': 8.0, 'L0_cond2_g2': 8.0, 'L0_ffn_bias': 5.802}
    for name, (base, spread) in spreads.items():
        noise = np.random.default_rng([zlib.crc32(name.encode()), seed]).standard_normal(out[name].shape)
        drawn = base * np.exp(spread * noise) if base else spread * noise
        out[name] = jnp.asarray(drawn.astype(out[name].dtype))
    for name, factor in factors.items():
        out[name] = (out[name] * factor).astype(out[name].dtype)
    return out
```

```python
import math
from contextlib import ExitStack
from collections import namedtuple

import concourse.bass as bass
from concourse import mybir

F32 = mybir.dt.float32
F32R = mybir.dt.float32r
BF16 = mybir.dt.bfloat16
F16 = mybir.dt.float16
U32 = mybir.dt.uint32
ALU = mybir.AluOpType
ACT = mybir.ActivationFunctionType
X = mybir.AxisListType.X
RADD = bass.bass_isa.ReduceOp.add
ds = bass.ds

P = 128
B, S, D = 8, 256, 256
N = B * S
F = 1024
KD, KF = D // P, F // P
PR = 2 * S
NP = N // PR
TP = PR // P
NT = N // P
R = 16
R2 = 2 * R
R3 = 3 * R2
E = 8
I = 512
KI = I // P
CAP = int(N / E * 1.25)
NS = E * CAP
ST = NS // P
TE = 2 * CAP // P
MID = TE // 2
HALF = CAP - MID * P
QW = D + 2
GW = KD * 2 * I
DW = KI * D
W2C = 3 * R + D
ROUND = 1.5 * 2.0 ** 23
DUMP = NS


def need(eng, sem, value):
    if not (isinstance(value, int) and value <= 0):
        eng.wait_ge(sem, value)


def build(nc, a):
    ctx = ExitStack()
    with ctx:
        _program(nc, a, ctx)


def _program(nc, a, ctx):
    base = -(-nc.sbuf_base // 32) * 32

    class Area:
        def __init__(self, at):
            self.at = at

        def put(self, name, shape, dt):
            size = math.prod(shape[1:]) * mybir.dt.size(dt)
            t = nc.alloc_sbuf_tensor_at(name, shape, dt, offset=self.at)
            self.at += -(-size // 32) * 32
            return t

    keep = Area(base)
    xs = keep.put("xs", [P, NT, D], F32)
    x_hi = keep.put("x_hi", [P, KD, PR], F32R)
    x_lo = keep.put("x_lo", [P, KD, PR], F32R)
    id_f = keep.put("id_f", [P, P], F32)
    id_b = keep.put("id_b", [P, P], BF16)
    wts = keep.put("wts", [P, 2, NT], F32)
    slots = keep.put("slots", [P, 2, NT], U32)
    m_hi = keep.put("m_hi", [P, KD, D], F32R)
    m_lo = keep.put("m_lo", [P, KD, D], F32R)
    consts = keep.put("consts", [P, 4], F32)
    MHALF, MONE, I127, RND = (consts[:, k:k + 1] for k in range(4))

    r1 = Area(keep.at)
    w1_hi = r1.put("w1_hi", [P, KD, F], F32R)
    w1_lo = r1.put("w1_lo", [P, KD, F], F32R)
    w2_hi = r1.put("w2_hi", [P, KF, W2C], F32R)
    w2_lo = r1.put("w2_lo", [P, KF, W2C], F32R)
    h_hi = r1.put("h_hi", [P, KF, PR], F32R)
    h_lo = r1.put("h_lo", [P, KF, PR], F32R)
    r1b = Area(keep.at)
    sw1, sw2 = [], []
    for n in range(2):
        sw1.append([r1b.put(f"sw1_{q}{n}", [P, KD, F], F32R) for q in ("hi", "lo")])
        sw2.append([r1b.put(f"sw2_{q}{n}", [P, KF, D], F32R) for q in ("hi", "lo")])

    r2 = Area(max(r1.at, r1b.at + 2 * PR * 4))
    r2_at = r2.at
    wq = r2.put("wq", [P, E, GW + DW], BF16)
    w_raw = r2.put("w_raw", [P, GW + DW], F32)
    per = (GW + DW) * 2
    s_a = Area(r2_at + 2 * per)
    w1_raw = s_a.put("w1_raw", [P, KD, F], F32)
    w2_raw = s_a.put("w2_raw", [P, KF, R + D], F32)
    assert s_a.at <= r2_at + 5 * per
    s_b = Area(r2_at + 5 * per)
    fr = s_b.put("fr", [P, KD, D], F32)
    fi = s_b.put("fi", [P, KD, D], F32)
    dft = s_b.put("dft", [P, 3, KD, D], F32)
    a_re = s_b.put("a_re", [P, KD, D], F32)
    a_im = s_b.put("a_im", [P, KD, D], F32)
    assert s_b.at <= r2_at + 8 * per
    r2b = Area(r2_at)
    tw1, tw2 = [], []
    for n in range(2):
        tw1.append([r2b.put(f"tw1_{q}{n}", [P, KD, F], F32R) for q in ("hi", "lo")])
        tw2.append([r2b.put(f"tw2_{q}{n}", [P, KF, D], F32R) for q in ("hi", "lo")])

    r3 = Area(r2.at)
    q_all = r3.put("q_all", [P, NT, QW], BF16)
    wq_s = r3.put("wq_s", [P, GW + DW], BF16)
    logits = r3.put("logits", [P, NT, E], F32)
    gw = r3.put("gw", [P, KD, E], F32)
    gnorm = r3.put("gnorm", [P, KD], F32)
    wsum = r3.put("wsum", [P, 4], F32)
    wscale = r3.put("wscale", [P, E + 1, 2], F32)
    wrec = r3.put("wrec", [P, 2], F32)
    tscale = r3.put("tscale", [P, ST, 2], F32)
    triu = r3.put("triu", [P, P], BF16)
    ones = r3.put("ones", [P, P], BF16)
    r3_at = r3.at
    x_raw = r3.put("x_raw", [P, KD, PR], F32)
    a_raw = r3.put("a_raw", [P, 2, KD, R2], F32)
    a_hi = r3.put("a_hi", [P, 2, KD, R3], F32R)
    a_lo = r3.put("a_lo", [P, 2, KD, R3], F32R)
    b_raw = r3.put("b_raw", [R3, F], F32)
    b_st = r3.put("b_st", [R3, 2, F], F32R)
    e2a_raw = r3.put("e2a_raw", [P, 2, KF, R], F32)
    b2_raw = r3.put("b2_raw", [R3, 2, D], F32)
    b2_st = r3.put("b2_st", [R3, 2, D], F32R)
    low = r3.put("low", [R3, PR], F32R)
    low2 = r3.put("low2", [P, 3, R2], F32)
    low2t = r3.put("low2t", [R3, P], F32R)
    c_sb = r3.put("c_sb", [P, TP, D], F32)
    c_tmp = r3.put("c_tmp", [P, D], F32)
    c_t = r3.put("c_t", [P, KD, P], F32)
    cst = r3.put("cst", [P, TP, 12], F32)
    c_junk = r3.put("c_junk", [P, D], BF16)
    end1 = r3.at
    rr = Area(keep.at)
    rt = [rr.put(f"rt{k}", [P, NT, E], F32) for k in range(8)]
    cum = [rr.put(f"cum{k}", [P, NT + 1, E], F32) for k in range(2)]
    sel_b = rr.put("sel_b", [P, NT, E], BF16)
    c16 = [rr.put(f"c16_{k}", [P, NT], F32) for k in range(10)]
    rev8 = rr.put("rev8", [P, E], F32)
    e_off = rr.put("e_off", [P, E], F32)
    iota_p = rr.put("iota_p", [P, P], F32)
    iota_c = rr.put("iota_c", [P, ST], F32)
    tokid = rr.put("tokid", [P, NT], F32)
    oh_p = rr.put("oh_p", [P, 2, P], F16)
    oh_c = rr.put("oh_c", [P, 2, ST], F16)
    inv = rr.put("inv", [P, ST], U32)
    rr = Area(keep.at + 3 * 16384)
    xg = rr.put("xg", [P, ST, QW], BF16)
    ys = rr.put("ys", [P, TE, D], F32)
    r3 = Area(r3_at)
    q_t = r3.put("q_t", [P, 2, KD, P], BF16)
    q_ta = r3.put("q_ta", [P, KD, P], BF16)
    q_tb = r3.put("q_tb", [P, KD, P], BF16)
    g_sb = r3.put("g_sb", [P, I], F32)
    hf = r3.put("hf", [P, 3, I], F32)
    hq = r3.put("hq", [P, 3, I], BF16)
    h_t = r3.put("h_t", [P, KI, P], BF16)
    h_ta = r3.put("h_ta", [P, KI, P], BF16)
    h_tb = r3.put("h_tb", [P, KI, P], BF16)
    mst = r3.put("mst", [P, 3, 12], F32)
    m_junk = r3.put("m_junk", [P, I], BF16)
    top = Area(nc.sbuf_usable_end // 32 * 32 - 2 * 4096)
    assert r3.at <= top.at
    raw = [top.put(f"raw{k}", [P, F], F32) for k in range(2)]
    end3 = r3.at
    r4 = Area(r2b.at)
    gat = r4.put("gat", [P, 2 * TP, D], F32)
    nets = r4.put("nets", [P, 3, KD, PR], F32)
    z_hi = Area(r4.at - 2 * KD * PR * 4).put("z_hi", [P, KD, PR], F32R)
    z_lo = Area(r4.at - KD * PR * 4).put("z_lo", [P, KD, PR], F32R)
    spare = Area(r1b.at)
    ring = [(r4.put(f"ring_hi{k}", [P, PR], F32R), r4.put(f"ring_lo{k}", [P, PR], F32R)) for k in range(2)]
    ring.append((spare.put("ring_hi2", [P, PR], F32R), spare.put("ring_lo2", [P, PR], F32R)))
    assert spare.at <= r2_at
    g1_sb = r4.put("g1_sb", [P, 3 * KD, D], F32)
    g2_sb = r4.put("g2_sb", [P, KD, 3], F32)
    bias_b = r4.put("bias_b", [P, D], F32)
    gidx = r4.put("gidx", [P, 2 * TP], U32)
    gh = r4.put("gh", [P, KD, 2], F32)
    gh_b = r4.put("gh_b", [P, KD, 2, P], F32)
    gl = r4.put("gl", [P, 8, 2, 3], F32)
    assert r4.at <= top.at

    bank = [ctx.enter_context(nc.psum_tensor(f"bank{k}", [P, 512], F32)) for k in range(8)]
    bank_b = [b[:, :].bitcast(BF16) for b in bank]

    def scratch(name, shape, dt):
        return nc.dram_tensor(name, shape, dt, kind="Internal").ap()

    q_d = scratch("q_d", (N, QW // 2), U32)
    y_d = scratch("y_d", (NS + 1, D), F32)

    def sem(name):
        return ctx.enter_context(nc.semaphore(name))

    names = """x_in a_in b_in e2_in w_in c_in m_in w1_in w2_in gw_in xs_in ids_ok q_out zrow
        built id0 gwok xh xl w1h w1l w2h w2l m1 m1e m2 mh ml a_sp b_sp w2_sp b2_sp
        w_abs w_m w_rec w_rnd w_clip w_out low_ps lowh lowl h_ps hh hl l2_ps low2s low2t_ps low2h low2l
        c_ps c_done csq camax cch cq1 cq2 ct_ps ct_sb lg_ps lg_sb
        route r_sub r_exp cnt_rd r_ps r_inv oh_ok oh_used built2 tsc rows_ok
        q_tp q_tc gu msg silu hmul hsq hmax mch hq1 hq2 h_tp h_tc dn y_ok
        s_hi s_lo gix comb xb rows_in xt_ps x4h x4l hp gath inv_ok h4h h4l l2d ne_a ne_d tsp g1_ps gh_ok gt_ok g2_ps
        gch gexp pool_held sync_held zh zl f_ps f_ok o_out g1_in""".split()
    q = namedtuple("Signals", names)(*[sem(n) for n in names])
    g_in = [sem(f"g_in{k}") for k in range(E // 2)]
    y_out = [sem(f"y_out{k}") for k in range(TE)]
    s_in = [sem(f"s_in{k}") for k in range(2)]
    t_in = [sem(f"t_in{k}") for k in range(2)]



    HB = (0, 1, 2)
    OB = (3, 4, 5)
    LT, CT, LG, LOW = 6, 7, 6, 7
    QT, GB, YB, HT, DN, RB = 7, (0, 2), (1, 3), 4, 5, 6
    AC, GT, XT = (4, 5), 3, (6, 7)

    block = ctx.enter_context(nc.Block())

    def hlh(w, x):
        return ((w[0], x[0]), (w[0], x[1]), (w[1], x[0]))

    COLS = ((0, slice(2 * R, 2 * R + D), slice(0, R), slice(R, 2 * R)),
            (R, slice(R, R + D), slice(R + D, 2 * R + D), slice(0, R)))
    UP = 2 * R + D

    def ring_of(kind, j):
        return j % 2 if kind == "shared" or j < 4 else 2

    def turned_of(kind, j):
        return j % 2 if kind == "shared" or j < MID else (j - MID - 1) % 2

    SECTION = {"shared": (0, TP, NP), "expert": (NT, TE, E // 2)}

    def tile_at(kind, i, j, lag):
        first, n, _ = SECTION[kind]
        if isinstance(i, int) and n * i + j - lag < 0:
            if kind == "shared":
                return None
            return tile_at("shared", NP, j - lag, 0)
        ii, jj = (i, j - lag) if j >= lag else (i - 1, j - lag + n)
        if isinstance(ii, int) and ii >= 0 and jj < 0:
            ii, jj = ii - 1, jj + n
        if kind == "shared" and isinstance(ii, int) and (ii > NP - 1 or jj < 0):
            ii, jj = NP - 1, (j - lag) % n
            return kind, ii, jj, first + n * ii + jj
        return kind, ii, jj, n * ii + (jj + first)

    def steps(eng, kind, step):
        _, n, count = SECTION[kind]
        for j in range(n):
            step(kind, 0, j)
        with eng.Fori(1, count) as i:
            for j in range(n):
                step(kind, i, j)

    def flat(ap):
        return ap.rearrange("p a c -> p (a c)")

    def w_dst(n):
        if isinstance(n, int) and n == 0:
            return wq_s[:, :]
        return flat(wq[:, ds(n - 1, 1), :])

    def split_dst(w1, w2, n, part, which):
        if part < 2:
            return w1[n][which][:, part, :]
        return w2[n][which][:, 4 * (part - 2):4 * (part - 2) + 4, :].rearrange("p k d -> p (k d)")

    @block.sync
    def _(sp):
        def lora_loads(p, part, half=0):
            for b in ((half,) if part == "b" else (0, 1)):
                sp.sem_inc(q.sync_held, 1)
                e = sp.value_load(a["ids"][0:1, ds(2 * p + b, 1)], min_val=0, max_val=E - 1)
                if part == "a":
                    sp.dma_start(a_raw[:, b, :, 0:R], a["ea1"][ds(e, 1)].rearrange("e p k r -> (e p) k r")).then_inc(q.a_in, 16)
                if part == "b":
                    for k in range(3):
                        sp.dma_start(b_raw[k * R2:k * R2 + R, :], a["eb1"][ds(e, 1)].rearrange("e r f -> (e r) f")).then_inc(q.b_in, 16)
                if part == "2":
                    sp.dma_start(e2a_raw[:, b, :, :], a["ea2"][ds(e, 1)].rearrange("e p k r -> (e p) k r")).then_inc(q.e2_in, 16)
                    for k in range(3):
                        sp.dma_start(b2_raw[k * R2:k * R2 + R, b, :], a["eb2"][ds(e, 1)].rearrange("e r d -> (e r) d")).then_inc(q.e2_in, 16)

        def w_load(n):
            need(sp, q.w_out, n)
            sp.dma_start(w_raw[:, 0:GW], a["gT"][ds(n, 1)].rearrange("e p k f -> (e p) (k f)")).then_inc(q.w_in, 16)
            sp.dma_start(w_raw[:, GW:], a["dT"][ds(n, 1)].rearrange("e p k f -> (e p) (k f)")).then_inc(q.w_in, 16)

        def x_load(p):
            sp.dma_start(x_raw[:, :, :], a["xT"][:, :, ds(p * PR, PR)]).then_inc(q.x_in, 16)

        x_load(0)
        sp.dma_start(w1_raw[:, :, :], a["w1T"]).then_inc(q.w1_in, 16)
        for t, n in ((fr, "fr"), (fi, "fi"), (dft, "dft")):
            sp.dma_start(t[:, :], a[n]).then_inc(q.m_in, 16)
        for b in range(2):
            sp.dma_start(a_raw[:, b, :, R:R2], a["ca1"]).then_inc(q.c_in, 16)
        for k in range(3):
            sp.dma_start(b_raw[k * R2 + R:(k + 1) * R2, :], a["cb1"]).then_inc(q.c_in, 16)
            for b in range(2):
                sp.dma_start(b2_raw[k * R2 + R:(k + 1) * R2, b, :], a["cb2"]).then_inc(q.c_in, 16)
        lora_loads(0, "a")
        lora_loads(0, "b", 0)
        sp.dma_start(w2_raw[:, :, 0:R], a["ca2"]).then_inc(q.w2_in, 16)
        sp.dma_start(w2_raw[:, :, R:], a["w2T"]).then_inc(q.w2_in, 16)
        lora_loads(0, "2")
        w_load(0)
        sp.dma_start(gw[:, :, :], a["gate_wT"]).then_inc(q.gw_in, 16)
        sp.dma_start(gnorm[:, :], a["gnorm"]).then_inc(q.gw_in, 16)
        sp.wait_ge(q.b_sp, 2)
        lora_loads(0, "b", 1)

        def feed(p, pre):
            w_load(2 * p + 1)
            if pre:
                sp.wait_ge(q.xl, p + 1)
                x_load(p + 1)
                sp.wait_ge(q.a_sp, 2 * p + 2)
                lora_loads(p + 1, "a")
                sp.wait_ge(q.b_sp, 4 * p + 4)
                lora_loads(p + 1, "b", 0)
                sp.wait_ge(q.w2_sp, 4 * p + 4)
                sp.wait_ge(q.b2_sp, 2 * p + 2)
                lora_loads(p + 1, "2")
            w_load(2 * p + 2)
            if pre:
                sp.wait_ge(q.b_sp, 4 * p + 6)
                lora_loads(p + 1, "b", 1)
            sp.wait_ge(q.cq2, TP * p + TP)
            sp.sem_inc(q.sync_held, 1)
            sp.wait_ge(q.cch, 8 * (TP * p + TP))
            sp.dma_start(q_d[ds(p * PR, PR), :].rearrange("(t p) c -> p t c", p=P), q_all[:, ds(p * TP, TP), :].bitcast(U32)).then_inc(q.q_out, 16)

        feed(0, True)
        sp.dma_start(xs[:, :, :], a["x"].rearrange("(t p) d -> p t d", p=P)).then_inc(q.xs_in, 16)
        with sp.Fori(1, NP - 1) as p:
            feed(p, True)
        feed(NP - 1, False)
        sp.wait_ge(q.q_out, 16 * NP)

        sp.wait_ge(q.built2, 2)
        sp.dma_start(y_d[DUMP:DUMP + 1, :].rearrange("a (b c) -> (a b) c", b=2), q_ta[0:2, :, :].rearrange("p k c -> p (k c)").bitcast(F32)).then_inc(q.zrow, 16)
        sp.wait_ge(q.zrow, 16)
        sp.sem_inc(q.rows_ok, 1)

        def s_load(c):
            n, part, k = c // 4, c // 2 % 2, c % 2
            need(sp, q.s_lo, c - 1)
            src = a["swi"][n, :, k, :] if part == 0 else a["swo"][n, :, 4 * k:4 * k + 4, :].rearrange("p k d -> p (k d)")
            sp.dma_start(raw[c % 2][:, :], src).then_inc(s_in[c % 2], 16)

        def y_store(kind, i, j):
            t = tile_at(kind, i, j, 0)
            sp.wait_ge(q.y_ok, t[3] + 1)
            sp.dma_start(y_d[ds(P * (t[3] - NT), P), :], ys[:, j, :]).then_inc(y_out[j], 16)

        sp.wait_ge(q.lg_sb, NT)
        s_load(0)
        s_load(1)
        with sp.Fori(0, E // 2) as i:
            for j in range(TE):
                y_store("expert", i, j)
        for c in range(2, 8):
            s_load(c)
        sp.dma_start(g1_sb[:, :, :], a["g1"]).then_inc(q.g1_in, 16)
        sp.dma_start(g2_sb[:, :, :], a["g2"]).then_inc(q.g1_in, 16)
        sp.dma_start(bias_b[:, :], a["bias"].partition_broadcast(P)).then_inc(q.g1_in, 16)

        def types(p):
            for b in range(2):
                sp.sem_inc(q.sync_held, 1)
                v = sp.value_load(a["types"][0:1, ds(2 * p + b, 1)], min_val=0, max_val=4)
                for m in range(4):
                    c = 4 * b + m
                    if c >= 2:
                        sp.wait_ge(q.tsp, 16 * p + 2 * (c - 1))
                    elif isinstance(p, int) and p == 0:
                        sp.wait_ge(q.s_lo, 7 + c)
                    else:
                        sp.wait_ge(q.tsp, 16 * p + 2 * (c - 1))
                    if m < 2:
                        src = a["wi"][ds(v, 1), :, m, :].rearrange("e p f -> (e p) f")
                    else:
                        src = a["wo"][ds(v, 1), :, 4 * (m - 2):4 * (m - 2) + 4, :].rearrange("e p k d -> (e p) (k d)")
                    sp.dma_start(raw[c % 2][:, :], src).then_inc(t_in[c % 2], 16)

        def store(p):
            for h in range(2):
                sp.wait_ge(q.f_ok, 2 * p + h + 1)
                sp.dma_start(a["out"][ds(p * PR + h * S, S), :].rearrange("(t p) d -> p t d", p=P), xs[:, ds(p * TP + 2 * h, 2), :]).then_inc(q.o_out, 16)

        types(0)
        with sp.Fori(1, NP) as p:
            types(p)
            store(p - 1)
        store(NP - 1)
        sp.wait_ge(q.o_out, 2 * 16 * NP)

    @block.tensor
    def _(pe):
        mm = nc.tensor.matmul

        pe.wait_ge(q.m_in, 48)
        for o in range(KD):
            for out_bank, terms in ((0, ((fr, 0), (fi, 1))), (1, ((fi, 0), (fr, 2)))):
                seq = [(w, t, k) for w, t in terms for k in range(KD)]
                for n, (w, t, k) in enumerate(seq):
                    last = mm(bank[out_bank][:, o * D:(o + 1) * D], w[:, k, o * P:(o + 1) * P], dft[:, t, k, :],
                              start=n == 0, stop=n == len(seq) - 1)
        last.then_inc(q.m1, 1)
        pe.wait_ge(q.m1e, 2)
        for m in range(KD):
            seq = [(w, t, k) for w, t in ((a_re, 0), (a_im, 2)) for k in range(KD)]
            for n, (w, t, k) in enumerate(seq):
                last = mm(bank[2][:, m * D:(m + 1) * D], w[:, k, m * P:(m + 1) * P], dft[:, t, k, :],
                          start=n == 0, stop=n == len(seq) - 1)
        last.then_inc(q.m2, 1)

        def low_rank(p):
            pe.wait_ge(q.xl, p + 1)
            pe.wait_ge(q.a_sp, 2 * p + 2)
            for b in range(2):
                seq = [(w, x, k) for k in range(KD) for w, x in hlh((a_hi, a_lo), (x_hi, x_lo))]
                for n, (w, x, k) in enumerate(seq):
                    last = mm(bank[LOW][0:R3, b * S:(b + 1) * S], w[:, b, k, :], x[:, k, b * S:(b + 1) * S],
                              start=n == 0, stop=n == len(seq) - 1)
            last.then_inc(q.low_ps, 1)

        def turn_c(p, j):
            t = TP * p + j
            pe.wait_ge(q.c_done, t + 1)
            if j == 0:
                need(pe, q.lowl, p + 2 if isinstance(p, int) and p == NP - 2 else p + 1)
            need(pe, q.ct_sb, t)
            for k in range(KD):
                last = nc.tensor.transpose(bank[CT][:, k * P:(k + 1) * P], c_sb[:, j, k * P:(k + 1) * P], id_f[:, :])
            last.then_inc(q.ct_ps, 1)

        def router(p, j):
            t = TP * p + j
            pe.wait_ge(q.ct_sb, t + 1)
            need(pe, q.lg_sb, t)
            pe.wait_ge(q.low2l, TP * p + TP)
            for k in range(KD):
                last = mm(bank[LG][:, 0:E], c_t[:, k, :], gw[:, k, :], start=k == 0, stop=k == KD - 1)
            last.then_inc(q.lg_ps, 1)

        def feed(p, prev, pre):
            for f in range(KF):
                if f == 0:
                    pe.wait_ge(q.lowl, p + 1)
                    pe.wait_ge(q.b_sp, 4 * p + 4)
                need(pe, q.hl, KF * p + f - 2)
                fs = slice(f * P, (f + 1) * P)
                seq = [(w, x, k) for k in range(KD) for w, x in hlh((w1_hi, w1_lo), (x_hi, x_lo))]
                for n, (w, x, k) in enumerate(seq):
                    mm(bank[HB[f % 3]][:, :], w[:, k, fs], x[:, k, :], start=n == 0, stop=False, skip_group_check=True)
                for b in range(2):
                    last = mm(bank[HB[f % 3]][:, b * S:(b + 1) * S], b_st[:, b, fs], low[:, b * S:(b + 1) * S],
                              start=False, stop=b == 1, skip_group_check=True)
                last.then_inc(q.h_ps, 1)
                if prev:
                    (turn_c if f % 2 == 0 else router)(p - 1, f // 2)

            def down(j):
                c0 = COLS[j // 2][0]
                need(pe, q.c_done, TP * p if j < 3 else TP * p + 1)
                for f in range(KF):
                    for n, (h, w) in enumerate(((h_hi, w2_hi), (h_hi, w2_lo), (h_lo, w2_hi))):
                        last = mm(bank[OB[j % 3]][:, 0:UP], h[:, f, j * P:(j + 1) * P], w[:, f, c0:c0 + UP],
                                  start=f == 0 and n == 0, stop=False, skip_group_check=True)
                last.then_inc(q.l2_ps, 1)

            def turn_low(j):
                pe.wait_ge(q.low2s, 2 * (TP * p + j + 1))
                need(pe, q.low2l, TP * p + j)
                if j == 0 and prev:
                    pe.wait_ge(q.lg_sb, TP * p)
                nc.tensor.transpose(bank[LT][0:R3, 0:P], low2[:, :, :].rearrange("p a b -> p (a b)"), id_f[:, :]).then_inc(q.low2t_ps, 1)

            def finish(j):
                pe.wait_ge(q.low2l, TP * p + j + 1)
                mm(bank[OB[j % 3]][:, COLS[j // 2][1]], low2t[:, :], b2_st[:, j // 2, :],
                   start=False, stop=True, skip_group_check=True).then_inc(q.c_ps, 1)

            pe.wait_ge(q.hl, KF * p + KF)
            pe.wait_ge(q.w2_sp, 4 * p + 4)
            pe.wait_ge(q.b2_sp, 2 * p + 2)
            if isinstance(p, int) and p == 0:
                pe.wait_ge(q.w2l, 1)
            down(0)
            down(1)
            turn_low(0)
            down(2)
            finish(0)
            turn_low(1)
            down(3)
            finish(1)
            turn_low(2)
            finish(2)
            turn_low(3)
            if pre:
                if prev:
                    pe.wait_ge(q.ct_sb, TP * p)
                low_rank(p + 1)
            finish(3)

        pe.wait_ge(q.w1l, 1)
        low_rank(0)
        pe.wait_ge(q.ml, 1)
        pe.wait_ge(q.id0, 4)
        feed(0, False, True)
        pe.wait_ge(q.gwok, 2)
        with pe.Fori(1, NP - 1) as p:
            feed(p, True, True)
        feed(NP - 1, True, False)
        for j in range(TP):
            turn_c(NP - 1, j)
            router(NP - 1, j)

        pe.wait_ge(q.r_ps, 1)
        sel = sel_b[:, :, :].rearrange("p t e -> p (t e)")
        mm(bank[RB][:, 0:NT * E], triu[:, :], sel, start=True, stop=True)
        mm(bank[RB][:, NT * E:2 * NT * E], ones[:, :], sel, start=True, stop=True).then_inc(q.r_inv, 1)

        def place(t, first, last):
            for k in range(2):
                pe.wait_ge(q.oh_ok, 4 * t + 2 * k + 2)
                mm(bank[RB][:, 0:ST], oh_p[:, k, :], oh_c[:, k, :], start=first and k == 0, stop=last and k == 1,
                   skip_group_check=True).then_inc(q.oh_used, 1)

        pe.wait_ge(q.cnt_rd, 1)
        place(0, True, False)
        with pe.Fori(1, NT - 1) as t:
            place(t, False, False)
        place(NT - 1, False, True)

        def rows_of(kind, i, j, c):
            if kind == "shared":
                return q_all[:, ds(TP * i + j, 1), c].rearrange("p a c -> p (a c)")
            return xg[:, ds(TE * i + j, 1), c].rearrange("p a c -> p (a c)")

        def weights(kind, i, j):
            if kind == "shared":
                return [(None, wq_s[:, :])]
            if j == MID:
                return [(0, wq[:, ds(2 * i, 1), :].rearrange("p e c -> p (e c)")),
                        (1, wq[:, ds(2 * i + 1, 1), :].rearrange("p e c -> p (e c)"))]
            return [(None, wq[:, ds(2 * i + (1 if j > MID else 0), 1), :].rearrange("p e c -> p (e c)"))]

        def mlp_step(kind, i, j, t1=True):
            if t1:
                _, ii, jj, g = tile_at(kind, i, j, 0)
                need(pe, q.q_tc, g)
                if kind == "expert" and j == 0:
                    pe.wait_ge(q.rows_in, i + 1)
                for k in range(KD):
                    last = nc.tensor.transpose(bank_b[QT][:, k * P:(k + 1) * P], rows_of(kind, i, j, slice(k * P, (k + 1) * P)), id_b[:, :])
                last.then_inc(q.q_tp, 1)
            back3 = tile_at(kind, i, j, 3)
            if back3:
                kd, ii, jj, g = back3
                pe.wait_ge(q.hq2, g + 1)
                need(pe, q.h_tc, g)
                for k in range(KI):
                    last = nc.tensor.transpose(bank_b[HT][:, k * P:(k + 1) * P], hq[:, ring_of(kd, jj), k * P:(k + 1) * P], id_b[:, :])
                last.then_inc(q.h_tp, 1)
            back1 = tile_at(kind, i, j, 1) if t1 or j == 0 else None
            if back1:
                kd, ii, jj, g = back1
                pe.wait_ge(q.q_tc, g + 1)
                r = jj % 2
                same = kd == "expert" and jj == 0 and not (isinstance(ii, int) and ii == 0)
                need(pe, q.hmul, g if same else g - 1)
                for out_bank, c0 in ((GB[r], 0), (YB[r], I)):
                    seq = [(m, w, k) for m, w in weights(kd, ii, jj) for k in range(KD)]
                    for n, (m, w, k) in enumerate(seq):
                        lhs = q_t[:, turned_of(kd, jj), k, :] if m is None else (q_ta, q_tb)[m][:, k, :]
                        last = mm(bank[out_bank][:, :], lhs, w[:, k * 2 * I + c0:k * 2 * I + c0 + I],
                                  start=n == 0, stop=n == len(seq) - 1)
                last.then_inc(q.gu, 1)
            if back3:
                kd, ii, jj, g = back3
                pe.wait_ge(q.h_tc, g + 1)
                need(pe, q.y_ok, g)
                seq = [(m, w, k) for m, w in weights(kd, ii, jj) for k in range(KI)]
                for n, (m, w, k) in enumerate(seq):
                    lhs = h_t[:, k, :] if m is None else (h_ta, h_tb)[m][:, k, :]
                    last = mm(bank[DN][:, 0:D], lhs, w[:, GW + k * D:GW + (k + 1) * D], start=n == 0, stop=n == len(seq) - 1)
                last.then_inc(q.dn, 1)

        pe.wait_ge(q.w_out, E + 1)
        pe.wait_ge(q.built2, 4)
        steps(pe, "shared", mlp_step)
        steps(pe, "expert", mlp_step)
        for j in range(3):
            mlp_step("expert", E // 2, j, t1=False)

        def turn_x(p):
            need(pe, q.f_ok, 2 * (p - 1))
            for k in range(KD):
                for j in range(TP):
                    pe.wait_ge(q.comb, 2 * (TP * p + j + 1))
                    last = nc.tensor.transpose(bank[XT[k]][:, j * P:(j + 1) * P], gat[:, 2 * j, k * P:(k + 1) * P], id_f[:, :])
                last.then_inc(q.xt_ps, 1)

        def up(p, st):
            n, f = st // KF, st % KF
            fs = slice(f * P, (f + 1) * P)
            out = bank[HB[st % 3]]
            need(pe, q.h4l, 3 * KF * p + st - 2)
            if st == 0:
                pe.wait_ge(q.x4l, KD * p + KD)
            if n < 2:
                if f == 0 and isinstance(p, int) and p == 0:
                    pe.wait_ge(q.s_lo, 4 * n + 2)
                seq = [(w, x, k) for k in range(KD) for w, x in hlh(sw1[n], (x_hi, x_lo))]
                for m, (w, x, k) in enumerate(seq):
                    last = mm(out[:, :], w[:, k, fs], x[:, k, :], start=m == 0, stop=m == len(seq) - 1)
            else:
                if f == 0:
                    pe.wait_ge(q.tsp, 16 * p + 16)
                for b in range(2):
                    seq = [(w, x, k) for k in range(KD) for w, x in hlh(tw1[b], (x_hi, x_lo))]
                    for m, (w, x, k) in enumerate(seq):
                        last = mm(out[:, b * S:(b + 1) * S], w[:, k, fs], x[:, k, b * S:(b + 1) * S],
                                  start=b == 0 and m == 0, stop=m == len(seq) - 1, skip_group_check=True)
            last.then_inc(q.hp, 1)

        def down4(p, st):
            n, f = st // KF, st % KF
            pe.wait_ge(q.h4l, 3 * KF * p + st + 1)
            if f == 0:
                need(pe, q.ne_a, 3 * p + n)
                need(pe, q.ne_d, 3 * p + n)
                if n < 2 and isinstance(p, int) and p == 0:
                    pe.wait_ge(q.s_lo, 4 * n + 4)
            h = ring[st % 3]
            for m in range(KD):
                ms = slice(m * P, (m + 1) * P)
                for b in ((None,) if n < 2 else (0, 1)):
                    cs = slice(0, PR) if b is None else slice(b * S, (b + 1) * S)
                    w2 = sw2[n] if b is None else tw2[b]
                    for t, (w, x) in enumerate(hlh(w2, h)):
                        last = mm(bank[AC[m]][:, cs], w[:, f, ms], x[:, cs], start=f == 0 and t == 0 and b != 1,
                                  stop=f == KF - 1 and t == 2, skip_group_check=True)
            last.then_inc(q.l2d, 1)

        def gate1(p):
            pe.wait_ge(q.ne_d, 3 * p + 3)
            pe.wait_ge(q.ne_a, 3 * p + 3)
            need(pe, q.gch, 12 * p)
            for m in range(KD):
                for n, net in enumerate((2, 0, 1)):
                    for k in range(KD):
                        last = mm(bank[GT][:, 2 * m:2 * m + 2], g1_sb[:, n * KD + k, m * P:(m + 1) * P], nets[:, net, k, 0:PR:S],
                                  start=n == 0 and k == 0, stop=n == 2 and k == KD - 1)
            last.then_inc(q.g1_ps, 1)

        def gate2(p):
            pe.wait_ge(q.gt_ok, p + 1)
            for b in range(2):
                for m in range(KD):
                    last = mm(bank[GT][:, 8 + 3 * b:11 + 3 * b], gh_b[:, m, b, :], g2_sb[:, m, :], start=m == 0, stop=m == KD - 1)
            last.then_inc(q.g2_ps, 1)

        def fourier(p, last_pair=False):
            pe.wait_ge(q.zl, p + 1)
            pe.wait_ge(q.x4l, KD * p + KD if last_pair else KD * p + 2 * KD)
            for j in range(TP):
                seq = [(z, w, k) for k in range(KD) for z, w in ((z_hi, m_hi), (z_hi, m_lo), (z_lo, m_hi))]
                for n, (z, w, k) in enumerate(seq):
                    last = mm(bank[XT[j // 2]][:, (j % 2) * D:(j % 2 + 1) * D], z[:, k, j * P:(j + 1) * P], w[:, k, :],
                              start=n == 0, stop=n == len(seq) - 1)
                if j % 2:
                    last.then_inc(q.f_ps, 1)

        def mix(p, prev, pre):
            for st in range(3 * KF):
                up(p, st)
                if st >= 2:
                    down4(p, st - 2)
                if prev:
                    if st == 2:
                        gate1(p - 1)
                    if st == 4:
                        gate2(p - 1)
                    if st == 13:
                        fourier(p - 1)
                if pre and st == 20:
                    turn_x(p + 1)
            down4(p, 3 * KF - 2)
            down4(p, 3 * KF - 1)

        pe.wait_ge(q.g1_in, 48)
        turn_x(0)
        mix(0, False, True)
        with pe.Fori(1, NP - 1) as p:
            mix(p, True, True)
        mix(NP - 1, True, False)
        gate1(NP - 1)
        gate2(NP - 1)
        fourier(NP - 1, True)

    @block.scalar
    def _(act):
        fn = nc.scalar.activation
        cp = nc.scalar.copy

        def x_high(p):
            act.wait_ge(q.x_in, 16 * (p + 1))
            need(act, q.h_ps, KF * p)
            cp(x_hi[:, :, :], x_raw[:, :, :]).then_inc(q.xh, 1)

        def low_high(p):
            act.wait_ge(q.low_ps, p + 1)
            need(act, q.h_ps, KF * p)
            fn(low[:, :], bank[LOW][0:R3, :], ACT.Copy, scale=2.0).then_inc(q.lowh, 1)

        def w_abs(n):
            act.wait_ge(q.w_in, 32 * (n + 1))
            dst = w_dst(n)
            fn(dst[:, 0:GW], w_raw[:, 0:GW], ACT.Abs, accum_out=wsum[:, 0:1]).then_inc(q.w_abs, 1)
            fn(dst[:, GW:], w_raw[:, GW:], ACT.Abs, accum_out=wsum[:, 1:2]).then_inc(q.w_abs, 1)

        def w_round(n):
            act.wait_ge(q.w_rec, 2 * n + 1)
            for c, k in ((slice(0, GW), 0), (slice(GW, GW + DW), 1)):
                fn(w_raw[:, c], w_raw[:, c], ACT.Identity, scale=wrec[:, k:k + 1], bias=RND).then_inc(q.w_rnd, 1)

        act.wait_ge(q.built, 7)
        x_high(0)
        act.wait_ge(q.w1_in, 16)
        cp(w1_hi[:, :, :], w1_raw[:, :, :]).then_inc(q.w1h, 1)
        act.wait_ge(q.m1, 1)
        cp(a_re[:, :, :].rearrange("p k d -> p (k d)"), bank[0][:, :]).then_inc(q.m1e, 1)
        cp(a_im[:, :, :].rearrange("p k d -> p (k d)"), bank[1][:, :]).then_inc(q.m1e, 1)
        low_high(0)
        act.wait_ge(q.m2, 1)
        fn(m_hi[:, :, :].rearrange("p k d -> p (k d)"), bank[2][:, :], ACT.Copy, scale=1.0 / D).then_inc(q.mh, 1)
        act.wait_ge(q.w2_in, 32)
        cp(w2_hi[:, :, R:R2 + D], w2_raw[:, :, :]).then_inc(q.w2h, 1)
        w_abs(0)
        w_round(0)

        def feed(p, prev, pre):
            for f in range(KF):
                act.wait_ge(q.h_ps, KF * p + f + 1)
                if f == 0:
                    need(act, q.l2_ps, TP * p)
                fn(h_hi[:, f, :], bank[HB[f % 3]][:, :], ACT.Relu).then_inc(q.hh, 1)
                if f == 2:
                    w_abs(2 * p + 1)
                if f == 4:
                    w_round(2 * p + 1)
                if prev and f % 2 == 0:
                    turned(p - 1, f // 2)
            if pre:
                x_high(p + 1)

            def low_out(j):
                t = TP * p + j
                act.wait_ge(q.l2_ps, t + 1)
                need(act, q.low2t_ps, t)
                for c, dst in ((COLS[j // 2][2], slice(0, R)), (COLS[j // 2][3], slice(R, R2))):
                    src = bank[OB[j % 3]][:, c].rearrange("p (a r) -> p a r", a=1).broadcast_to([P, 3, R])
                    fn(low2[:, :, dst], src, ACT.Copy, scale=2.0).then_inc(q.low2s, 1)

            def low_turned(j):
                t = TP * p + j
                act.wait_ge(q.low2t_ps, t + 1)
                need(act, q.c_ps, t)
                cp(low2t[:, :], bank[LT][0:R3, 0:P]).then_inc(q.low2h, 1)

            def c_out(j):
                t = TP * p + j
                act.wait_ge(q.c_ps, t + 1)
                need(act, q.cch, 8 * (t - TP + 1))
                need(act, q.ct_ps, t - TP + 1)
                need(act, q.csq, t)
                src = bank[OB[j % 3]][:, COLS[j // 2][1]]
                fn(c_junk[:, :], src, ACT.Square, accum_out=cst[:, j, 0:1]).then_inc(q.csq, 1)
                cp(c_sb[:, j, :], src).then_inc(q.c_done, 1)

            def c_round(j):
                t = TP * p + j
                act.wait_ge(q.cch, 8 * t + 5)
                need(act, q.cq2, t)
                fn(c_tmp[:, :], c_sb[:, j, :], ACT.Identity, scale=cst[:, j, 6:7], bias=RND).then_inc(q.cq1, 1)

            low_out(0)
            low_out(1)
            low_turned(0)
            low_out(2)
            c_out(0)
            low_turned(1)
            low_out(3)
            c_out(1)
            w_abs(2 * p + 2)
            low_turned(2)
            c_out(2)
            low_turned(3)
            if pre:
                low_high(p + 1)
            c_out(3)
            for j in range(TP):
                c_round(j)
            w_round(2 * p + 2)

        def turned(p, j):
            t = TP * p + j
            act.wait_ge(q.ct_ps, t + 1)
            need(act, q.lg_ps, t)
            cp(c_t[:, :, :].rearrange("p k d -> p (k d)"), bank[CT][:, 0:D]).then_inc(q.ct_sb, 1)

        feed(0, False, True)
        with act.Fori(1, NP - 1) as p:
            feed(p, True, True)
        feed(NP - 1, True, False)
        for j in range(TP):
            turned(NP - 1, j)

        act.wait_ge(q.r_sub, 1)
        fn(rt[1][:, :, :], rt[0][:, :, :], ACT.Exp).then_inc(q.r_exp, 1)

        def mlp_step(kind, i, j, t1=True):
            def at(lag):
                return tile_at(kind, i, j, lag) if t1 or j < lag else None
            if at(2):
                kd, ii, jj, g = at(2)
                r = ring_of(kd, jj)
                act.wait_ge(q.mch, 7 * g + 5)
                fn(hf[:, r, :], hf[:, r, :], ACT.Identity, scale=mst[:, r, 6:7], bias=RND).then_inc(q.hq1, 1)
            if at(3):
                kd, ii, jj, g = at(3)
                act.wait_ge(q.h_tp, g + 1)
                need(act, q.dn, g)
                src = bank_b[HT][:, 0:I]
                if kd == "expert" and jj == MID:
                    src = src.rearrange("p (k c) -> p k c", k=KI)
                    cp(h_ta[:, :, 0:HALF], src[:, :, 0:HALF])
                    cp(h_tb[:, :, HALF:], src[:, :, HALF:]).then_inc(q.h_tc, 1)
                else:
                    cp(h_t[:, :, :].rearrange("p k c -> p (k c)"), src).then_inc(q.h_tc, 1)
            if at(1):
                kd, ii, jj, g = at(1)
                r = ring_of(kd, jj)
                act.wait_ge(q.gu, g + 1)
                act.wait_ge(q.msg, g + 1)
                need(act, q.hmul, g)
                fn(g_sb[:, :], bank[GB[jj % 2]][:, :], ACT.Silu, scale=mst[:, r, 2:3]).then_inc(q.silu, 1)
                act.wait_ge(q.hmul, g + 1)
                need(act, q.mch, 7 * (g - 1))
                need(act, q.hsq, g)
                fn(m_junk[:, :], hf[:, r, :], ACT.Square, accum_out=mst[:, r, 0:1]).then_inc(q.hsq, 1)

        steps(act, "shared", mlp_step)
        steps(act, "expert", mlp_step)
        for j in range(3):
            mlp_step("expert", E // 2, j, t1=False)

        for c in range(8):
            act.wait_ge(s_in[c % 2], 16 * (c // 2 + 1))
            if c == 0:
                act.wait_ge(q.y_ok, NT + ST)
            if c == 4:
                for k in range(TE):
                    act.wait_ge(y_out[k], 16 * (E // 2))
            cp(split_dst(sw1, sw2, c // 4, c % 4, 0), raw[c % 2][:, :]).then_inc(q.s_hi, 1)

        def x4_high(p):
            for k in range(KD):
                act.wait_ge(q.xt_ps, KD * p + k + 1)
                need(act, q.hp, 3 * KF * p)
                cp(x_hi[:, k, :], bank[XT[k]][:, :]).then_inc(q.x4h, 1)

        def net_out(p, n):
            act.wait_ge(q.l2d, 3 * KF * p + KF * (n + 1))
            if n == 0:
                need(act, q.zl, p)
                need(act, q.zh, p)
            else:
                need(act, q.f_ps, 2 * p)
            cp(nets[:, n, 0, :], bank[AC[0]][:, :]).then_inc(q.ne_a, 1)

        def gate_hidden(p):
            act.wait_ge(q.g1_ps, p + 1)
            need(act, q.gt_ok, p)
            fn(gh[:, :, :].rearrange("p m b -> p (m b)"), bank[GT][:, 0:2 * KD], ACT.Relu).then_inc(q.gh_ok, 1)

        def gate_exp(p):
            act.wait_ge(q.gch, 12 * p + 3)
            fn(gl[:, 3, :, :], gl[:, 2, :, :], ACT.Exp).then_inc(q.gexp, 1)

        def z_high(p):
            act.wait_ge(q.gch, 12 * p + 12)
            cp(z_hi[:, :, :], nets[:, 0, :, :]).then_inc(q.zh, 1)

        def mix(p, prev, pre):
            for st in range(3 * KF):
                act.wait_ge(q.hp, 3 * KF * p + st + 1)
                need(act, q.l2d, 3 * KF * p + st - 2)
                fn(ring[st % 3][0][:, :], bank[HB[st % 3]][:, :], ACT.Relu).then_inc(q.h4h, 1)
                if st in (KF + 1, 2 * KF + 1):
                    net_out(p, st // KF - 1)
                if prev and st == 2:
                    gate_hidden(p - 1)
                if prev and st == 5:
                    gate_exp(p - 1)
                if prev and st == 8:
                    z_high(p - 1)
            if pre:
                x4_high(p + 1)
            net_out(p, 2)

        x4_high(0)
        mix(0, False, True)
        with act.Fori(1, NP - 1) as p:
            mix(p, True, True)
        mix(NP - 1, True, False)
        gate_hidden(NP - 1)
        gate_exp(NP - 1)
        z_high(NP - 1)

    @block.vector
    def _(v):
        ts, tt, stt, red = (nc.vector.tensor_scalar, nc.vector.tensor_tensor, nc.vector.scalar_tensor_tensor,
                            nc.vector.tensor_reduce)

        def x_low(p):
            v.wait_ge(q.xh, p + 1)
            tt(x_lo[:, :, :], x_raw[:, :, :], x_hi[:, :, :].bitcast(F32), ALU.subtract).then_inc(q.xl, 1)

        def low_low(p):
            v.wait_ge(q.lowh, p + 1)
            stt(low[R2:2 * R2, :], bank[LOW][R2:2 * R2, :], 2.0, low[R2:2 * R2, :].bitcast(F32), ALU.mult, ALU.subtract).then_inc(q.lowl, 1)

        def w_recip(n):
            v.wait_ge(q.w_m, 3 * (n + 1))
            nc.vector.reciprocal(wrec[:, :], wsum[:, 2:4]).then_inc(q.w_rec, 1)
            nc.vector.tensor_copy(flat(wscale[:, ds(n, 1), :]), wsum[:, 2:4]).then_inc(q.w_rec, 1)

        def w_clip(n):
            v.wait_ge(q.w_rnd, 2 * n + 2)
            ts(w_raw[:, :], w_raw[:, :], ROUND, -1.0, ALU.subtract, ALU.max).then_inc(q.w_clip, 1)
            v.wait_ge(q.w_clip, n + 1)
            ts(w_dst(n), w_raw[:, :], 1.0, None, ALU.min).then_inc(q.w_out, 1)

        x_low(0)
        v.wait_ge(q.w1h, 1)
        tt(w1_lo[:, :, :], w1_raw[:, :, :], w1_hi[:, :, :].bitcast(F32), ALU.subtract).then_inc(q.w1l, 1)
        low_low(0)
        v.wait_ge(q.mh, 1)
        stt(m_lo[:, :, :].rearrange("p k d -> p (k d)"), bank[2][:, :], 1.0 / D,
            m_hi[:, :, :].rearrange("p k d -> p (k d)").bitcast(F32), ALU.mult, ALU.subtract).then_inc(q.ml, 1)
        v.wait_ge(q.w2h, 1)
        tt(w2_lo[:, :, R:R2 + D], w2_raw[:, :, :], w2_hi[:, :, R:R2 + D].bitcast(F32), ALU.subtract).then_inc(q.w2l, 1)
        w_recip(0)
        w_clip(0)

        def logit_out(p, j):
            t = TP * p + j
            v.wait_ge(q.lg_ps, t + 1)
            v.wait_ge(q.cch, 8 * t + 8)
            ts(flat(logits[:, ds(t, 1), :]), bank[LG][:, 0:E], cst[:, j, 8:9], None, ALU.mult).then_inc(q.lg_sb, 1)

        def feed(p, prev, pre):
            for f in range(KF):
                v.wait_ge(q.hh, KF * p + f + 1)
                stt(h_lo[:, f, :], bank[HB[f % 3]][:, :], 0.0, h_hi[:, f, :].bitcast(F32), ALU.max, ALU.subtract).then_inc(q.hl, 1)
                if f == 3:
                    w_recip(2 * p + 1)
                if f == 6:
                    w_clip(2 * p + 1)
                if prev and f % 2:
                    logit_out(p - 1, f // 2)
            if pre:
                x_low(p + 1)

            def low_turned(j):
                v.wait_ge(q.low2h, TP * p + j + 1)
                tt(low2t[R2:2 * R2, :], bank[LT][R2:2 * R2, 0:P], low2t[R2:2 * R2, :].bitcast(F32), ALU.subtract).then_inc(q.low2l, 1)

            def c_max(j):
                t = TP * p + j
                v.wait_ge(q.c_done, t + 1)
                need(v, q.cch, 8 * (t - TP + 1))
                red(cst[:, j, 1:2], c_sb[:, j, :], X, ALU.max, apply_absolute_value=True).then_inc(q.camax, 1)

            def c_quant(j):
                t = TP * p + j
                v.wait_ge(q.cq1, t + 1)
                ts(flat(q_all[:, ds(t, 1), 0:D]), c_tmp[:, :], ROUND, None, ALU.subtract).then_inc(q.cq2, 1)

            low_turned(0)
            low_turned(1)
            c_max(0)
            low_turned(2)
            c_max(1)
            low_turned(3)
            c_max(2)
            if pre:
                low_low(p + 1)
            c_max(3)
            w_recip(2 * p + 2)
            for j in range(TP):
                c_quant(j)
            w_clip(2 * p + 2)

        feed(0, False, True)
        with v.Fori(1, NP - 1) as p:
            feed(p, True, True)
        feed(NP - 1, True, False)
        for j in range(TP):
            logit_out(NP - 1, j)

        count = [0]

        def step():
            v.wait_ge(q.route, count[0])

        def done():
            count[0] += 1
            return q.route, 1

        full = [P, NT, E]

        def over(c):
            return c[:, :].rearrange("p (t a) -> p t a", a=1).broadcast_to(full)

        def each(c):
            return c[:, :].rearrange("p (a e) -> p a e", a=1).broadcast_to(full)

        v.wait_ge(q.lg_sb, NT)
        v.wait_ge(q.built2, 9)
        red(c16[0][:, :], logits[:, :, :], X, ALU.max).then_inc(*done())
        step()
        tt(rt[0][:, :, :], logits[:, :, :], over(c16[0]), ALU.subtract).then_inc(q.r_sub, 1)
        v.wait_ge(q.r_exp, 1)
        red(c16[1][:, :], rt[1][:, :, :], X, ALU.add).then_inc(*done())
        step()
        nc.vector.reciprocal(c16[2][:, :], c16[1][:, :]).then_inc(*done())
        step()
        tt(rt[2][:, :, :], rt[1][:, :, :], over(c16[2]), ALU.mult).then_inc(*done())
        step()

        def best(probs, weight, place, eq, one):
            red(weight[:, :], probs[:, :, :], X, ALU.max).then_inc(*done())
            step()
            tt(eq[:, :, :], probs[:, :, :], over(weight), ALU.is_equal).then_inc(*done())
            step()
            tt(eq[:, :, :], eq[:, :, :], each(rev8), ALU.mult).then_inc(*done())
            step()
            red(place[:, :], eq[:, :, :], X, ALU.max).then_inc(*done())
            step()
            tt(one[:, :, :], eq[:, :, :], over(place), ALU.is_equal).then_inc(*done())
            step()

        best(rt[2], c16[3], c16[4], rt[4], rt[3])
        stt(rt[6][:, :, :], rt[3][:, :, :], -2.0, rt[2][:, :, :], ALU.mult, ALU.add).then_inc(*done())
        step()
        best(rt[6], c16[5], c16[6], rt[4], rt[5])
        ts(c16[7][:, :], c16[5][:, :], 0.0, None, ALU.is_gt).then_inc(*done())
        step()
        tt(rt[5][:, :, :], rt[5][:, :, :], over(c16[7]), ALU.mult).then_inc(*done())
        step()
        tt(sel_b[:, :, :], rt[3][:, :, :], rt[5][:, :, :], ALU.add).then_inc(q.r_ps, 1)

        v.wait_ge(q.r_inv, 1)
        totals = bank[RB][:, NT * E:2 * NT * E].rearrange("p (t e) -> p t e", e=E)
        inner = bank[RB][:, 0:NT * E].rearrange("p (t e) -> p t e", e=E)
        nc.vector.memset(cum[0][:, 0:1, :], 0.0).then_inc(*done())
        nc.vector.tensor_copy(cum[0][:, 1:NT + 1, :], totals).then_inc(*done())
        step()
        src, d = 0, 1
        while d < NT:
            tt(cum[1 - src][:, d:, :], cum[src][:, d:, :], cum[src][:, 0:NT + 1 - d, :], ALU.add).then_inc(*done())
            nc.vector.tensor_copy(cum[1 - src][:, 0:d, :], cum[src][:, 0:d, :]).then_inc(*done())
            step()
            src, d = 1 - src, 2 * d
        tt(rt[4][:, :, :], inner, cum[src][:, 0:NT, :], ALU.add).then_inc(q.cnt_rd, 1)
        v.wait_ge(q.cnt_rd, 1)
        stt(rt[6][:, :, :], rt[4][:, :, :], float(CAP), sel_b[:, :, :], ALU.is_le, ALU.mult).then_inc(*done())
        tt(rt[7][:, :, :], rt[4][:, :, :], each(e_off), ALU.add).then_inc(*done())
        step()
        tt(rt[7][:, :, :], rt[7][:, :, :], rt[6][:, :, :], ALU.mult).then_inc(*done())
        step()
        for k, (one, weight) in enumerate(((rt[3], c16[3]), (rt[5], c16[5]))):
            slot = c16[8 + k]
            tt(rt[0][:, :, :], rt[7][:, :, :], one[:, :, :], ALU.mult).then_inc(*done())
            tt(rt[1][:, :, :], rt[6][:, :, :], one[:, :, :], ALU.mult).then_inc(*done())
            step()
            red(slot[:, :], rt[0][:, :, :], X, ALU.add).then_inc(*done())
            red(c16[0][:, :], rt[1][:, :, :], X, ALU.add).then_inc(*done())
            step()
            ts(slot[:, :], slot[:, :], float(DUMP), None, ALU.add).then_inc(*done())
            tt(wts[:, k, :], c16[0][:, :], weight[:, :], ALU.mult).then_inc(*done())
            step()
            nc.vector.tensor_copy(slots[:, k, :], slot[:, :]).then_inc(*done())
            ts(c16[1 + 4 * k][:, :], slot[:, :], -(P - 1) / 2, 1.0 / P, ALU.add, ALU.mult).then_inc(*done())
            step()
            ts(c16[1 + 4 * k][:, :], c16[1 + 4 * k][:, :], ROUND, ROUND, ALU.add, ALU.subtract).then_inc(*done())
            step()
            stt(c16[2 + 4 * k][:, :], c16[1 + 4 * k][:, :], -float(P), slot[:, :], ALU.mult, ALU.add).then_inc(*done())
            step()

        def one_hots(t):
            for k in range(2):
                tile, place = c16[1 + 4 * k], c16[2 + 4 * k]
                need(v, q.oh_used, 2 * (t - 1) + k + 1)
                ts(oh_p[:, k, :], iota_p[:, :], place[:, ds(t, 1)], None, ALU.is_equal).then_inc(q.oh_ok, 1)
                ts(oh_c[:, k, :], iota_c[:, :], tile[:, ds(t, 1)], tokid[:, ds(t, 1)], ALU.is_equal, ALU.mult).then_inc(q.oh_ok, 1)

        one_hots(0)
        with v.Fori(1, NT) as t:
            one_hots(t)
        v.wait_ge(q.oh_used, 2 * NT)
        nc.vector.tensor_copy(inv[:, :], bank[RB][:, 0:ST]).then_inc(q.inv_ok, 1)

        def mlp_step(kind, i, j, t1=True):
            def at(lag):
                return tile_at(kind, i, j, lag) if t1 or j < lag else None
            if at(0):
                kd, ii, jj, g = at(0)
                v.wait_ge(q.q_tp, g + 1)
                need(v, q.gu, g - 1)
                src = bank_b[QT][:, 0:D]
                if kd == "expert" and jj == MID:
                    src = src.rearrange("p (k c) -> p k c", k=KD)
                    nc.vector.tensor_copy(q_ta[:, :, 0:HALF], src[:, :, 0:HALF])
                    nc.vector.tensor_copy(q_tb[:, :, HALF:], src[:, :, HALF:]).then_inc(q.q_tc, 1)
                else:
                    nc.vector.tensor_copy(q_t[:, turned_of(kd, jj), :, :].rearrange("p k c -> p (k c)"), src).then_inc(q.q_tc, 1)
            if at(2):
                kd, ii, jj, g = at(2)
                r = ring_of(kd, jj)
                v.wait_ge(q.hq1, g + 1)
                need(v, q.h_tp, g - 1)
                ts(hq[:, r, :], hf[:, r, :], ROUND, None, ALU.subtract).then_inc(q.hq2, 1)
            if at(1):
                kd, ii, jj, g = at(1)
                r = ring_of(kd, jj)
                v.wait_ge(q.silu, g + 1)
                need(v, q.hq2, g - 1)
                stt(hf[:, r, :], bank[YB[jj % 2]][:, :], mst[:, r, 2:3], g_sb[:, :], ALU.mult, ALU.mult).then_inc(q.hmul, 1)
                v.wait_ge(q.hmul, g + 1)
                need(v, q.mch, 7 * (g - 1))
                red(mst[:, r, 1:2], hf[:, r, :], X, ALU.max, apply_absolute_value=True).then_inc(q.hmax, 1)
            if at(3):
                kd, ii, jj, g = at(3)
                r = ring_of(kd, jj)
                v.wait_ge(q.dn, g + 1)
                v.wait_ge(q.mch, 7 * g + 7)
                if kd == "shared":
                    if isinstance(g, int) and g == 0:
                        v.wait_ge(q.xs_in, 16)
                    row = flat(xs[:, ds(g, 1), :])
                    stt(row, bank[DN][:, 0:D], mst[:, r, 8:9], row, ALU.mult, ALU.add).then_inc(q.y_ok, 1)
                else:
                    need(v, y_out[jj], 16 * ii)
                    ts(ys[:, jj, :], bank[DN][:, 0:D], mst[:, r, 8:9], None, ALU.mult).then_inc(q.y_ok, 1)

        steps(v, "shared", mlp_step)
        steps(v, "expert", mlp_step)
        for j in range(3):
            mlp_step("expert", E // 2, j, t1=False)

        for c in range(8):
            v.wait_ge(q.s_hi, c + 1)
            tt(split_dst(sw1, sw2, c // 4, c % 4, 1), raw[c % 2][:, :], split_dst(sw1, sw2, c // 4, c % 4, 0).bitcast(F32),
               ALU.subtract).then_inc(q.s_lo, 1)

        def combine(p, j):
            t = TP * p + j
            if j == 0:
                v.wait_ge(q.gath, 16 * 2 * TP * (p + 1))
            row = flat(xs[:, ds(t, 1), :])
            stt(row, gat[:, 2 * j, :], flat(wts[:, 0:1, ds(t, 1)]), row, ALU.mult, ALU.add).then_inc(q.comb, 1)
            v.wait_ge(q.comb, 2 * t + 1)
            stt(gat[:, 2 * j, :], gat[:, 2 * j + 1, :], flat(wts[:, 1:2, ds(t, 1)]), row, ALU.mult, ALU.add).then_inc(q.comb, 1)

        def x4_low(p):
            for k in range(KD):
                v.wait_ge(q.x4h, KD * p + k + 1)
                tt(x_lo[:, k, :], bank[XT[k]][:, :], x_hi[:, k, :].bitcast(F32), ALU.subtract).then_inc(q.x4l, 1)

        def net_out(p, n):
            v.wait_ge(q.l2d, 3 * KF * p + KF * (n + 1))
            if n == 0:
                need(v, q.zl, p)
                need(v, q.zh, p)
            else:
                need(v, q.f_ps, 2 * p)
            nc.vector.tensor_copy(nets[:, n, 1, :], bank[AC[1]][:, :]).then_inc(q.ne_d, 1)

        def gate_spread(p):
            v.wait_ge(q.gh_ok, p + 1)
            need(v, q.g2_ps, p)
            nc.vector.tensor_copy(gh_b[:, :, :, :].rearrange("p m b c -> p (m b) c"),
                                  gh[:, :, :].rearrange("p m (b a) -> p (m b) a", a=1).broadcast_to([P, 2 * KD, P])).then_inc(q.gt_ok, 1)

        def three(col):
            return col.broadcast_to([P, 2, 3])

        def gate_max(p):
            g0 = 12 * p
            v.wait_ge(q.g2_ps, p + 1)
            nc.vector.tensor_copy(gl[:, 0, :, :].rearrange("p b n -> p (b n)"), bank[GT][:, 8:14]).then_inc(q.gch, 1)
            v.wait_ge(q.gch, g0 + 1)
            red(gl[:, 1, :, 0], gl[:, 0, :, :], X, ALU.max).then_inc(q.gch, 1)
            v.wait_ge(q.gch, g0 + 2)
            tt(gl[:, 2, :, :], gl[:, 0, :, :], three(gl[:, 1, :, 0:1]), ALU.subtract).then_inc(q.gch, 1)

        def gate_norm(p):
            g0 = 12 * p
            v.wait_ge(q.gexp, p + 1)
            red(gl[:, 4, :, 0], gl[:, 3, :, :], X, ALU.add).then_inc(q.gch, 1)
            v.wait_ge(q.gch, g0 + 4)
            nc.vector.reciprocal(gl[:, 5, :, 0:1], gl[:, 4, :, 0:1]).then_inc(q.gch, 1)
            v.wait_ge(q.gch, g0 + 5)
            tt(gl[:, 6, :, :], gl[:, 3, :, :], three(gl[:, 5, :, 0:1]), ALU.mult).then_inc(q.gch, 1)

        def mix_nets(p, part):
            g0 = 12 * p + 6 + 2 * part
            v.wait_ge(q.ne_a, 3 * p + 3)
            v.wait_ge(q.gch, g0)
            for b in range(2):
                c = slice(b * S, (b + 1) * S)
                weight = gl[:, 6, b, (1, 0, 2)[part]:(1, 0, 2)[part] + 1]
                out = nets[:, 0, :, c]
                if part == 0:
                    ts(out, out, weight, None, ALU.mult).then_inc(q.gch, 1)
                else:
                    stt(out, nets[:, (2, 1)[part - 1], :, c], weight, out, ALU.mult, ALU.add).then_inc(q.gch, 1)

        def z_low(p):
            v.wait_ge(q.zh, p + 1)
            tt(z_lo[:, :, :], nets[:, 0, :, :], z_hi[:, :, :].bitcast(F32), ALU.subtract).then_inc(q.zl, 1)

        def fourier_out(p, h):
            v.wait_ge(q.f_ps, 2 * p + h + 1)
            v.wait_ge(q.xb, p + 1)
            rows = xs[:, ds(TP * p + 2 * h, 2), :].rearrange("p t d -> p (t d)")
            tt(rows, bank[XT[h]][:, :], rows, ALU.add).then_inc(q.f_ok, 1)

        def mix(p, prev, pre):
            for st in range(3 * KF):
                v.wait_ge(q.h4h, 3 * KF * p + st + 1)
                hi, lo = ring[st % 3]
                stt(lo[:, :], bank[HB[st % 3]][:, :], 0.0, hi[:, :].bitcast(F32), ALU.max, ALU.subtract).then_inc(q.h4l, 1)
                if st in (KF + 1, 2 * KF + 1):
                    net_out(p, st // KF - 1)
                if prev:
                    if st == 2:
                        gate_spread(p - 1)
                    if st == 4:
                        gate_max(p - 1)
                    if st == 5:
                        gate_norm(p - 1)
                        mix_nets(p - 1, 0)
                    if st in (6, 7):
                        mix_nets(p - 1, st - 5)
                    if st == 8:
                        z_low(p - 1)
                    if st in (14, 15):
                        fourier_out(p - 1, st - 14)
                if pre and 14 <= st < 14 + TP:
                    combine(p + 1, st - 14)
            if pre:
                x4_low(p + 1)
            net_out(p, 2)

        for j in range(TP):
            combine(0, j)
        x4_low(0)
        mix(0, False, True)
        with v.Fori(1, NP - 1) as p:
            mix(p, True, True)
        mix(NP - 1, True, False)
        last = NP - 1
        gate_spread(last)
        gate_max(last)
        gate_norm(last)
        for part in range(3):
            mix_nets(last, part)
        z_low(last)
        for h in range(2):
            fourier_out(last, h)

    @block.gpsimd
    def _(g):
        ts, tt, copy = nc.gpsimd.tensor_scalar, nc.gpsimd.tensor_tensor, nc.gpsimd.tensor_copy

        def hold(sem, value):
            need(g, sem, value)
            if not isinstance(value, int):
                g.sem_inc(q.pool_held, 1)

        for k, value in enumerate((-0.5, -1.0, 1.0 / 127.0, ROUND)):
            nc.gpsimd.memset(consts[:, k:k + 1], value).then_inc(q.built, 1)
        nc.gpsimd.memset(ones[:, :], 1.0).then_inc(q.built, 1)
        nc.gpsimd.memset(triu[:, :], 1.0).then_inc(q.built, 1)
        hold(q.built, 6)
        nc.gpsimd.affine_select(out=triu[:, :], in_=triu[:, :], pattern=[[1, P]], compare_op=ALU.is_ge, fill=0.0,
                                base=0, channel_multiplier=-1).then_inc(q.built, 1)
        for n, t in enumerate((id_f, id_b)):
            nc.gpsimd.memset(t[:, :], 0.0).then_inc(q.id0, 1)
            hold(q.id0, 2 * n + 1)
            nc.gpsimd.affine_select(out=t[:, :], in_=t[:, :], pattern=[[-1, P]], compare_op=ALU.not_equal, fill=1.0,
                                    base=0, channel_multiplier=1).then_inc(q.id0, 1)

        def a_split(p):
            hold(q.a_in, 32 * (p + 1))
            hold(q.low_ps, p)
            raw3 = a_raw[:, :, :, :].rearrange("p b k (a r) -> p (b k) a r", a=1).broadcast_to([P, 2 * KD, 3, R2])
            hi, lo = (t[:, :, :, :].rearrange("p b k (a r) -> p (b k) a r", a=3) for t in (a_hi, a_lo))
            copy(hi, raw3).then_inc(q.a_sp, 1)
            hold(q.a_sp, 2 * p + 1)
            tt(lo, raw3, hi.bitcast(F32), ALU.subtract).then_inc(q.a_sp, 1)

        def b_split(p, half):
            hold(q.b_in, 48 * (2 * p + half + 1))
            hold(q.h_ps, KF * p)
            copy(b_st[:, half, :], b_raw[:, :]).then_inc(q.b_sp, 1)
            hold(q.b_sp, 4 * p + 2 * half + 1)
            rows = slice(2 * R2, R3)
            tt(b_st[rows, half, :], b_raw[rows, :], b_st[rows, half, :].bitcast(F32), ALU.subtract).then_inc(q.b_sp, 1)
            hold(q.b_sp, 4 * p + 2 * half + 2)

        def second_split(p):
            hold(q.e2_in, 128 * (p + 1))
            hold(q.l2_ps, TP * p)
            for b, c in enumerate((slice(0, R), slice(R2 + D, W2C))):
                copy(w2_hi[:, :, c], e2a_raw[:, b, :, :]).then_inc(q.w2_sp, 1)
                hold(q.w2_sp, 4 * p + 2 * b + 1)
                tt(w2_lo[:, :, c], e2a_raw[:, b, :, :], w2_hi[:, :, c].bitcast(F32), ALU.subtract).then_inc(q.w2_sp, 1)
            hold(q.c_ps, TP * p)
            copy(b2_st[:, :, :], b2_raw[:, :, :]).then_inc(q.b2_sp, 1)
            hold(q.b2_sp, 2 * p + 1)
            rows = slice(2 * R2, R3)
            tt(b2_st[rows, :, :], b2_raw[rows, :, :], b2_st[rows, :, :].bitcast(F32), ALU.subtract).then_inc(q.b2_sp, 1)
            hold(q.b2_sp, 2 * p + 2)

        def w_mean(n):
            hold(q.w_abs, 2 * n + 2)
            nc.gpsimd.partition_all_reduce(wsum[:, 2:4], wsum[:, 0:2], P, RADD).then_inc(q.w_m, 1)
            hold(q.w_m, 3 * n + 1)
            for k, size in enumerate((2 * I * D, D * I)):
                ts(wsum[:, 2 + k:3 + k], wsum[:, 2 + k:3 + k], 1.0 / size, 1e-5, ALU.mult, ALU.max).then_inc(q.w_m, 1)

        hold(q.c_in, 16 * 11)
        a_split(0)
        b_split(0, 0)
        hold(q.gw_in, 32)
        for k in range(KD):
            tt(gw[:, k, :], gw[:, k, :], gnorm[:, k:k + 1].broadcast_to([P, E]), ALU.mult).then_inc(q.gwok, 1)
        b_split(0, 1)
        w_mean(0)

        def c_chain(p, j):
            t = TP * p + j
            n = 8 * t
            ssq, amax, var, r, m, rm, a_, v2, r6 = (cst[:, j, c:c + 1] for c in (0, 1, 2, 3, 4, 5, 6, 7, 8))
            hold(q.csq, t + 1)
            hold(q.camax, t + 1)
            ts(var, ssq, 1.0 / D, 1e-8, ALU.mult, ALU.add).then_inc(q.cch, 1)
            hold(q.cch, n + 1)
            tt(r, var, MHALF, ALU.pow).then_inc(q.cch, 1)
            hold(q.cch, n + 2)
            ts(m, amax, r, 1e-5, ALU.mult, ALU.max).then_inc(q.cch, 1)
            hold(q.cch, n + 3)
            tt(rm, m, MONE, ALU.pow).then_inc(q.cch, 1)
            hold(q.cch, n + 4)
            ts(a_, r, rm, 127.0, ALU.mult, ALU.mult).then_inc(q.cch, 1)
            tt(flat(q_all[:, ds(t, 1), D:D + 2]).bitcast(F32), m, I127, ALU.mult).then_inc(q.cch, 1)
            ts(v2, ssq, 1.0 / D, 1e-6, ALU.mult, ALU.add).then_inc(q.cch, 1)
            hold(q.cch, n + 7)
            hold(q.lg_sb, t - TP + 1)
            tt(r6, v2, MHALF, ALU.pow).then_inc(q.cch, 1)

        def feed(p, pre):
            second_split(p)
            w_mean(2 * p + 1)
            if pre:
                a_split(p + 1)
                for half in range(2):
                    b_split(p + 1, half)
            c_chain(p, 0)
            w_mean(2 * p + 2)
            for j in range(1, TP):
                c_chain(p, j)

        feed(0, True)
        with g.Fori(1, NP - 1) as p:
            feed(p, True)
        feed(NP - 1, False)

        hold(q.h_ps, KF * NP)
        hold(q.l2_ps, NT)
        for t in (q_ta, q_tb, h_ta, h_tb):
            nc.gpsimd.memset(t[:, :, :], 0.0).then_inc(q.built2, 1)
        for t, step, base, cm in ((iota_p[:, :], [[1, P]], 0, 0), (iota_c[:, :], [[1, ST]], 0, 0), (tokid[:, :], [[P, NT]], 0, 1),
                                  (rev8[:, :], [[-1, E]], E, 0), (e_off[:, :], [[CAP, E]], -1 - DUMP, 0)):
            nc.gpsimd.iota(t, pattern=step, base=base, channel_multiplier=cm, allow_small_or_imprecise_dtypes=True).then_inc(q.built2, 1)

        hold(q.w_rec, 2 * (E + 1))
        by_pair = wscale[:, 1:E + 1, :].rearrange("p (i h) c -> p i h c", h=2)
        tiles = tscale[:, :, :].rearrange("p (i j) c -> p i j c", j=TE)
        for rows, h, js in ((slice(0, P), 0, slice(0, MID)), (slice(0, P), 1, slice(MID + 1, TE)),
                            (slice(0, HALF), 0, slice(MID, MID + 1)), (slice(HALF, P), 1, slice(MID, MID + 1))):
            n = js.stop - js.start
            if rows.start:
                hold(q.tsc, 3)
            copy(tiles[rows, :, js, :], by_pair[rows, :, h:h + 1, :].broadcast_to([rows.stop - rows.start, E // 2, n, 2])).then_inc(q.tsc, 1)
        hold(q.tsc, 4)

        def gather(k):
            for t in range(TE * k, TE * (k + 1)):
                g.indirect_dma_start(xg[:, t, :].bitcast(U32), None, q_d, bass.IndirectOffsetOnAxis(ap=inv[:, t:t + 1], axis=0)).then_inc(g_in[k], 16)

        def here(k):
            hold(g_in[k], 16 * TE)
            g.sem_inc(q.rows_in, 1)

        def scale_of(kd, jj, g_, c):
            if kd == "shared":
                return wscale[:, 0, c:c + 1]
            return flat(tscale[:, ds(g_ - NT, 1), c:c + 1])

        def mlp_step(kind, i, j, t1=True):
            if kind == "shared" and isinstance(i, int) and i == 0:
                if j == 0:
                    hold(q.tsc, 4)
                if j in (0, 2):
                    hold(q.inv_ok, 1)
                    hold(q.rows_ok, 1)
                    gather(j // 2)
            if kind == "expert":
                if isinstance(i, int) and i == 0:
                    if j == 0:
                        here(0)
                        gather(2)
                    if j == 2:
                        here(1)
                        gather(3)
                    if j == TE - 1:
                        here(2)
                        here(3)
            if t1:
                kd, ii, jj, t = tile_at(kind, i, j, 0)
                r = ring_of(kd, jj)
                hold(q.hmul, t - 1)
                rows = q_all[:, ds(t, 1), D:D + 2] if kd == "shared" else xg[:, ds(t - NT, 1), D:D + 2]
                tt(mst[:, r, 2:3], flat(rows).bitcast(F32), scale_of(kd, jj, t, 0), ALU.mult).then_inc(q.msg, 1)
            if t1 or j < 1:
                back = tile_at(kind, i, j, 1)
                if back:
                    kd, ii, jj, t = back
                    ring_c = ring_of(kd, jj)
                    ssq, amax, var, r, m, rm, a_, dqh, od = (mst[:, ring_c, c:c + 1] for c in (0, 1, 3, 4, 5, 7, 6, 9, 8))
                    n = 7 * t
                    hold(q.hsq, t + 1)
                    hold(q.hmax, t + 1)
                    ts(var, ssq, 1.0 / I, 1e-8, ALU.mult, ALU.add).then_inc(q.mch, 1)
                    hold(q.mch, n + 1)
                    tt(r, var, MHALF, ALU.pow).then_inc(q.mch, 1)
                    hold(q.mch, n + 2)
                    ts(m, amax, r, 1e-5, ALU.mult, ALU.max).then_inc(q.mch, 1)
                    hold(q.mch, n + 3)
                    tt(rm, m, MONE, ALU.pow).then_inc(q.mch, 1)
                    hold(q.mch, n + 4)
                    hold(q.hq1, t - 1)
                    ts(a_, r, rm, 127.0, ALU.mult, ALU.mult).then_inc(q.mch, 1)
                    tt(dqh, m, I127, ALU.mult).then_inc(q.mch, 1)
                    hold(q.mch, n + 6)
                    hold(q.y_ok, t - 1)
                    tt(od, dqh, scale_of(kd, jj, t, 1), ALU.mult).then_inc(q.mch, 1)

        steps(g, "shared", mlp_step)
        steps(g, "expert", mlp_step)
        mlp_step("expert", E // 2, 0, t1=False)

        def gather_rows(p):
            hold(q.xt_ps, KD * p)
            copy(gidx[:, :].rearrange("p (j k) -> p k j", k=2), slots[:, :, ds(TP * p, TP)]).then_inc(q.gix, 1)
            hold(q.gix, p + 1)
            for n in range(2 * TP):
                g.indirect_dma_start(gat[:, n, :], None, y_d, bass.IndirectOffsetOnAxis(ap=gidx[:, n:n + 1], axis=0)).then_inc(q.gath, 16)

        def add_bias(p):
            hold(q.comb, 2 * TP * (p + 1))
            even = gat[:, :, :].rearrange("p (j k) d -> p j k d", k=2)[:, :, 0, :]
            tt(xs[:, ds(TP * p, TP), :], even, bias_b[:, :].rearrange("p (a d) -> p a d", a=1).broadcast_to([P, TP, D]),
               ALU.add).then_inc(q.xb, 1)

        def type_split(p):
            for c in range(8):
                hold(t_in[c % 2], 16 * (4 * p + c // 2 + 1))
                if c == 0:
                    hold(q.l2d, 3 * KF * p)
                hi, lo = (split_dst(tw1, tw2, c // 4, c % 4, k) for k in range(2))
                copy(hi, raw[c % 2][:, :]).then_inc(q.tsp, 1)
                hold(q.tsp, 16 * p + 2 * c + 1)
                tt(lo, raw[c % 2][:, :], hi.bitcast(F32), ALU.subtract).then_inc(q.tsp, 1)

        hold(q.y_ok, NT + ST)
        for k in range(TE):
            hold(y_out[k], 16 * (E // 2))
        gather_rows(0)
        type_split(0)
        hold(q.g1_in, 48)
        add_bias(0)
        gather_rows(1)
        with g.Fori(1, NP - 1) as p:
            type_split(p)
            add_bias(p)
            gather_rows(p + 1)
        type_split(NP - 1)
        add_bias(NP - 1)


def kernel(**inputs):
    import numpy as np
    import concourse.bacc as bacc
    from concourse.bass_utils import run_bass_kernel_spmd

    def x_of(name):
        return np.asarray(inputs[name])

    def rows(w, k):
        return np.swapaxes(w.reshape(*w.shape[:-2], k, P, w.shape[-1]), -3, -2)

    def turn(w):
        return np.swapaxes(w, -1, -2)

    x = x_of("x").reshape(N, D)
    c, t = "L0_cond_", "L0_attn_"
    n = np.arange(D)
    angle = 2.0 * np.pi * (np.outer(n, n) % D) / D
    dft = np.stack([np.cos(angle), np.sin(angle), -np.sin(angle)]).astype(np.float32)
    gates = np.concatenate([x_of(t + "shared_gate_w")[None], x_of(t + "expert_gate_w")])
    downs = np.concatenate([x_of(t + "shared_down_w")[None], x_of(t + "expert_down_w")])
    arrays = {
        "x": x, "xT": rows(x.T, KD),
        "w1T": rows(turn(x_of(c + "wi")), KD), "w2T": rows(turn(x_of(c + "wo")), KF),
        "ca1": rows(turn(x_of(c + "common_wi_a")), KD), "cb1": turn(x_of(c + "common_wi_b")),
        "ca2": rows(turn(x_of(c + "common_wo_a")), KF), "cb2": turn(x_of(c + "common_wo_b")),
        "ea1": rows(turn(x_of(c + "experts_wi_a")), KD), "eb1": turn(x_of(c + "experts_wi_b")),
        "ea2": rows(turn(x_of(c + "experts_wo_a")), KF), "eb2": turn(x_of(c + "experts_wo_b")),
        "gate_wT": rows(turn(x_of(t + "gate_w")), KD), "gnorm": x_of(t + "gate_norm_w").reshape(KD, P).T,
        "gT": rows(turn(gates), KD), "dT": rows(turn(downs), KI),
        "ids": x_of("itok_B_0_7").reshape(1, B), "types": x_of("itok_B_0_2").reshape(1, B),
        "wi": rows(x_of("L0_cond2_wi"), KD), "wo": rows(x_of("L0_cond2_wo"), KF),
        "swi": rows(x_of("L0_cond2_swi"), KD), "swo": rows(x_of("L0_cond2_swo"), KF),
        "g1": rows(x_of("L0_cond2_g1"), 3 * KD), "g2": rows(x_of("L0_cond2_g2"), KD),
        "fr": rows(x_of("L0_ffn_w_freq_real"), KD), "fi": rows(x_of("L0_ffn_w_freq_imag"), KD),
        "dft": np.swapaxes(rows(dft, KD), 0, 1), "bias": x_of("L0_ffn_bias").reshape(1, D),
    }
    nc = bacc.Bacc("TRN2", target_bir_lowering=False, num_devices=1)
    data, a = {}, {}
    for name, v in arrays.items():
        v = np.ascontiguousarray(v)
        data["in_" + name] = v
        a[name] = nc.dram_tensor("in_" + name, v.shape, mybir.dt.from_np(v.dtype), kind="ExternalInput").ap()
    a["out"] = nc.dram_tensor("out", (N, D), F32, kind="ExternalOutput").ap()
    build(nc, a)
    r = run_bass_kernel_spmd(nc, [data], core_ids=[0])
    return r.results[0]["out"].reshape(B, S, D)
```

```python
import math
from contextlib import ExitStack
from collections import namedtuple

import concourse.bass as bass
from concourse import mybir

F32 = mybir.dt.float32
F32R = mybir.dt.float32r
BF16 = mybir.dt.bfloat16
F16 = mybir.dt.float16
U32 = mybir.dt.uint32
ALU = mybir.AluOpType
ACT = mybir.ActivationFunctionType
X = mybir.AxisListType.X
RADD = bass.bass_isa.ReduceOp.add
ds = bass.ds

P = 128
B, S, D = 8, 256, 256
N = B * S
F = 1024
KD, KF = D // P, F // P
PR = 2 * S
NP = N // PR
TP = PR // P
NT = N // P
R = 16
R2 = 2 * R
R3 = 3 * R2
E = 8
I = 512
KI = I // P
CAP = int(N / E * 1.25)
NS = E * CAP
ST = NS // P
TE = 2 * CAP // P
MID = TE // 2
HALF = CAP - MID * P
QW = D + 2
GW = KD * 2 * I
DW = KI * D
WC = (GW + DW) // F
CC = 10
W2C = 3 * R + D
ROUND = 1.5 * 2.0 ** 23
DUMP = NS


def need(eng, sem, value):
    if not (isinstance(value, int) and value <= 0):
        eng.wait_ge(sem, value)


def build(nc, a):
    ctx = ExitStack()
    with ctx:
        _program(nc, a, ctx)


def _program(nc, a, ctx):
    base = -(-nc.sbuf_base // 32) * 32

    class Area:
        def __init__(self, at):
            self.at = at

        def put(self, name, shape, dt):
            size = math.prod(shape[1:]) * mybir.dt.size(dt)
            t = nc.alloc_sbuf_tensor_at(name, shape, dt, offset=self.at)
            self.at += -(-size // 32) * 32
            return t

    keep = Area(base)
    xs = keep.put("xs", [P, NT, D], F32)
    x_hi = keep.put("x_hi", [P, KD, PR], F32R)
    x_lo = keep.put("x_lo", [P, KD, PR], F32R)
    id_f = keep.put("id_f", [P, P], F32)
    id_b = keep.put("id_b", [P, P], BF16)
    wts = keep.put("wts", [P, 2, NT], F32)
    slots = keep.put("slots", [P, 2, NT], U32)
    m_hi = keep.put("m_hi", [P, KD, D], F32R)
    m_lo = keep.put("m_lo", [P, KD, D], F32R)
    consts = keep.put("consts", [P, 4], F32)
    MHALF, MONE, I127, RND = (consts[:, k:k + 1] for k in range(4))

    r1 = Area(keep.at)
    w1_hi = r1.put("w1_hi", [P, KD, F], F32R)
    w1_lo = r1.put("w1_lo", [P, KD, F], F32R)
    w2_hi = r1.put("w2_hi", [P, KF, W2C], F32R)
    w2_lo = r1.put("w2_lo", [P, KF, W2C], F32R)
    h_hi = r1.put("h_hi", [P, KF, PR], F32R)
    h_lo = r1.put("h_lo", [P, KF, PR], F32R)
    r1b = Area(keep.at)
    sw1, sw2 = [], []
    for n in range(2):
        sw1.append([r1b.put(f"sw1_{q}{n}", [P, KD, F], F32R) for q in ("hi", "lo")])
        sw2.append([r1b.put(f"sw2_{q}{n}", [P, KF, D], F32R) for q in ("hi", "lo")])

    r2 = Area(max(r1.at, r1b.at + 2 * PR * 4))
    r2_at = r2.at
    wq = r2.put("wq", [P, E, GW + DW], BF16)
    w_raw = r2.put("w_raw", [P, GW + DW], F32)
    per = (GW + DW) * 2
    s_a = Area(r2_at + 2 * per)
    w1_raw = s_a.put("w1_raw", [P, KD, F], F32)
    w2_raw = s_a.put("w2_raw", [P, KF, R + D], F32)
    assert s_a.at <= r2_at + 5 * per
    s_b = Area(r2_at + 5 * per)
    fr = s_b.put("fr", [P, KD, D], F32)
    fi = s_b.put("fi", [P, KD, D], F32)
    dft = s_b.put("dft", [P, 3, KD, D], F32)
    a_re = s_b.put("a_re", [P, KD, D], F32)
    a_im = s_b.put("a_im", [P, KD, D], F32)
    assert s_b.at <= r2_at + 8 * per
    r2b = Area(r2_at)
    tw1, tw2 = [], []
    for n in range(2):
        tw1.append([r2b.put(f"tw1_{q}{n}", [P, KD, F], F32R) for q in ("hi", "lo")])
        tw2.append([r2b.put(f"tw2_{q}{n}", [P, KF, D], F32R) for q in ("hi", "lo")])

    r3 = Area(r2.at)
    q_all = r3.put("q_all", [P, NT, QW], BF16)
    wq_s = r3.put("wq_s", [P, GW + DW], BF16)
    logits = r3.put("logits", [P, NT, E], F32)
    gw = r3.put("gw", [P, KD, E], F32)
    gnorm = r3.put("gnorm", [P, KD], F32)
    wsum = r3.put("wsum", [P, 8], F32)
    wscale = r3.put("wscale", [P, E + 1, 2], F32)
    wrec = r3.put("wrec", [P, 2], F32)
    tscale = r3.put("tscale", [P, ST, 2], F32)
    triu = r3.put("triu", [P, P], BF16)
    ones = r3.put("ones", [P, P], BF16)
    r3_at = r3.at
    x_raw = r3.put("x_raw", [P, KD, PR], F32)
    a_raw = r3.put("a_raw", [P, 2, KD, R2], F32)
    a_hi = r3.put("a_hi", [P, 2, KD, R3], F32R)
    a_lo = r3.put("a_lo", [P, 2, KD, R3], F32R)
    b_raw = r3.put("b_raw", [R3, F], F32)
    b_st = r3.put("b_st", [R3, 2, F], F32R)
    e2a_raw = r3.put("e2a_raw", [P, 2, KF, R], F32)
    b2_raw = r3.put("b2_raw", [R3, 2, D], F32)
    b2_st = r3.put("b2_st", [R3, 2, D], F32R)
    low = r3.put("low", [R3, PR], F32R)
    low2 = r3.put("low2", [P, 3, R2], F32)
    low2t = r3.put("low2t", [R3, P], F32R)
    c_sb = r3.put("c_sb", [P, TP, D], F32)
    c_tmp = r3.put("c_tmp", [P, D], F32)
    c_t = r3.put("c_t", [P, KD, P], F32)
    cst = r3.put("cst", [P, 12, TP], F32)
    c_junk = r3.put("c_junk", [P, D], BF16)
    end1 = r3.at
    rr = Area(keep.at)
    rt = [rr.put(f"rt{k}", [P, NT, E], F32) for k in range(8)]
    cum = [rr.put(f"cum{k}", [P, NT + 1, E], F32) for k in range(2)]
    sel_b = rr.put("sel_b", [P, NT, E], BF16)
    c16 = [rr.put(f"c16_{k}", [P, NT], F32) for k in range(10)]
    rev8 = rr.put("rev8", [P, E], F32)
    e_off = rr.put("e_off", [P, E], F32)
    iota_p = rr.put("iota_p", [P, P], F32)
    iota_c = rr.put("iota_c", [P, ST], F32)
    tokid = rr.put("tokid", [P, NT], F32)
    oh_p = rr.put("oh_p", [P, 2, NT, P], F16)
    oh_c = rr.put("oh_c", [P, 2, NT, ST], F16)
    inv = rr.put("inv", [P, ST], U32)
    assert rr.at <= keep.at + 3 * 16384
    rr = Area(keep.at + 3 * 16384)
    xg = rr.put("xg", [P, ST, QW], BF16)
    ys = rr.put("ys", [P, TE, D], F32)
    r3 = Area(r3_at)
    q_t = r3.put("q_t", [P, 2, KD, P], BF16)
    q_ta = r3.put("q_ta", [P, KD, P], BF16)
    q_tb = r3.put("q_tb", [P, KD, P], BF16)
    g_sb = r3.put("g_sb", [P, I], F32)
    hf = r3.put("hf", [P, 3, I], F32)
    hq = r3.put("hq", [P, 3, I], BF16)
    h_t = r3.put("h_t", [P, KI, P], BF16)
    h_ta = r3.put("h_ta", [P, KI, P], BF16)
    h_tb = r3.put("h_tb", [P, KI, P], BF16)
    mst = r3.put("mst", [P, TE, 12], F32)
    m_junk = r3.put("m_junk", [P, I], BF16)
    top = Area(nc.sbuf_usable_end // 32 * 32 - 2 * 4096)
    assert r3.at <= top.at
    raw = [top.put(f"raw{k}", [P, F], F32) for k in range(2)]
    end3 = r3.at
    r4 = Area(r2b.at)
    gat = r4.put("gat", [P, 2 * TP, D], F32)
    nets = r4.put("nets", [P, 3, KD, PR], F32)
    z_hi = Area(r4.at - 2 * KD * PR * 4).put("z_hi", [P, KD, PR], F32R)
    z_lo = Area(r4.at - KD * PR * 4).put("z_lo", [P, KD, PR], F32R)
    spare = Area(r1b.at)
    ring = [(r4.put(f"ring_hi{k}", [P, PR], F32R), r4.put(f"ring_lo{k}", [P, PR], F32R)) for k in range(2)]
    ring.append((spare.put("ring_hi2", [P, PR], F32R), spare.put("ring_lo2", [P, PR], F32R)))
    assert spare.at <= r2_at
    g1_sb = r4.put("g1_sb", [P, 3 * KD, D], F32)
    g2_sb = r4.put("g2_sb", [P, KD, 3], F32)
    bias_b = r4.put("bias_b", [P, D], F32)
    gidx = r4.put("gidx", [P, 2 * TP], U32)
    gh = r4.put("gh", [P, KD, 2], F32)
    gh_b = r4.put("gh_b", [P, KD, 2, P], F32)
    gl = r4.put("gl", [P, 8, 2, 3], F32)
    assert r4.at <= top.at

    bank = [ctx.enter_context(nc.psum_tensor(f"bank{k}", [P, 512], F32)) for k in range(8)]
    bank_b = [b[:, :].bitcast(BF16) for b in bank]

    def scratch(name, shape, dt):
        return nc.dram_tensor(name, shape, dt, kind="Internal").ap()

    q_d = scratch("q_d", (N, QW // 2), U32)
    y_d = scratch("y_d", (NS + 1, D), F32)

    def sem(name):
        return ctx.enter_context(nc.semaphore(name))

    names = """x_in a_in b_in e2_in c_in m_in w1_in w2_in gw_in xs_in ids_ok q_out zrow
        built id0 gwok xh xl w1h w1l w2h w2l m1 m1e m2 mh ml a_sp b_sp w2_sp b2_sp
        w_abs w_m w_rec w_rnd w_clip w_out low_ps lowh lowl h_ps hh hl l2_ps low2s low2t_ps low2h low2l
        c_ps c_done csq camax cch cq1 cq2 ct_ps ct_sb lg_ps lg_sb
        route r_sub r_exp cnt_rd r_ps r_inv oh_ok oh_used built2 tsc rows_ok
        q_tp q_tc gu msg silu hmul hsq hmax mch hq1 hq2 h_tp h_tc dn y_ok
        s_hi s_lo gix comb xb rows_in xt_ps x4h x4l hp gath inv_ok h4h h4l l2d ne_a ne_d thi tsp g1_ps gh_ok gt_ok g2_ps
        gch gexp pool_held sync_held zh zl f_ps f_ok o_out g1_in""".split()
    q = namedtuple("Signals", names)(*[sem(n) for n in names])
    w_in = [sem(f"w_in{k}") for k in range(WC)]
    g_in = [sem(f"g_in{k}") for k in range(E // 2)]
    y_out = [sem(f"y_out{k}") for k in range(TE)]
    s_in = [sem(f"s_in{k}") for k in range(2)]
    t_in = [sem(f"t_in{k}") for k in range(2)]



    HB = (0, 1, 2)
    OB = (3, 4, 5)
    LT, CT, LG, LOW = 6, 7, 6, 7
    QT, GB, YB, HT, DN, RB = 7, (0, 2), (1, 3), 4, 5, 6
    AC, GT, XT = (4, 5), 3, (6, 7)

    block = ctx.enter_context(nc.Block())

    def hlh(w, x):
        return ((w[0], x[0]), (w[0], x[1]), (w[1], x[0]))

    COLS = ((0, slice(2 * R, 2 * R + D), slice(0, R), slice(R, 2 * R)),
            (R, slice(R, R + D), slice(R + D, 2 * R + D), slice(0, R)))
    UP = 2 * R + D

    def ring_of(kind, j):
        return j % 2 if kind == "shared" or j < 4 else 2

    def turned_of(kind, j):
        return j % 2 if kind == "shared" or j < MID else (j - MID - 1) % 2

    SECTION = {"shared": (0, TP, NP), "expert": (NT, TE, E // 2)}

    def tile_at(kind, i, j, lag):
        first, n, _ = SECTION[kind]
        if isinstance(i, int) and n * i + j - lag < 0:
            if kind == "shared":
                return None
            return tile_at("shared", NP, j - lag, 0)
        ii, jj = (i, j - lag) if j >= lag else (i - 1, j - lag + n)
        if isinstance(ii, int) and ii >= 0 and jj < 0:
            ii, jj = ii - 1, jj + n
        if kind == "shared" and isinstance(ii, int) and (ii > NP - 1 or jj < 0):
            ii, jj = NP - 1, (j - lag) % n
            return kind, ii, jj, first + n * ii + jj
        return kind, ii, jj, n * ii + (jj + first)

    def steps(eng, kind, step):
        _, n, count = SECTION[kind]
        apart = 2 if kind == "shared" else 1
        for i in range(apart):
            for j in range(n):
                step(kind, i, j)
        with eng.Fori(apart, count) as i:
            for j in range(n):
                step(kind, i, j)

    def flat(ap):
        return ap.rearrange("p a c -> p (a c)")

    def w_dst(n):
        if isinstance(n, int) and n == 0:
            return wq_s[:, :]
        return flat(wq[:, ds(n - 1, 1), :])

    def split_dst(w1, w2, n, part, which):
        if part < 2:
            return w1[n][which][:, part, :]
        return w2[n][which][:, 4 * (part - 2):4 * (part - 2) + 4, :].rearrange("p k d -> p (k d)")

    @block.sync
    def _(sp):
        def lora_loads(p, part, half=0):
            for b in ((half,) if part == "b" else (0, 1)):
                sp.sem_inc(q.sync_held, 1)
                e = sp.value_load(a["ids"][0:1, ds(2 * p + b, 1)], min_val=0, max_val=E - 1)
                if part == "a":
                    sp.dma_start(a_raw[:, b, :, 0:R], a["ea1"][ds(e, 1)].rearrange("e p k r -> (e p) k r")).then_inc(q.a_in, 16)
                if part == "b":
                    for k in range(3):
                        sp.dma_start(b_raw[k * R2:k * R2 + R, :], a["eb1"][ds(e, 1)].rearrange("e r f -> (e r) f")).then_inc(q.b_in, 16)
                if part == "2":
                    sp.dma_start(e2a_raw[:, b, :, :], a["ea2"][ds(e, 1)].rearrange("e p k r -> (e p) k r")).then_inc(q.e2_in, 16)
                    for k in range(3):
                        sp.dma_start(b2_raw[k * R2:k * R2 + R, b, :], a["eb2"][ds(e, 1)].rearrange("e r d -> (e r) d")).then_inc(q.e2_in, 16)

        def w_load(n):
            for c in range(WC):
                need(sp, q.w_out, WC * (n - 1) + c + 1)
                src = a["gT"][ds(n, 1), :, c, :].rearrange("e p f -> (e p) f") if c < KD else a["dT"][ds(n, 1)].rearrange("e p k f -> (e p) (k f)")
                sp.dma_start(w_raw[:, c * F:(c + 1) * F], src).then_inc(w_in[c], 16)

        def x_load(p):
            sp.dma_start(x_raw[:, :, :], a["xT"][:, :, ds(p * PR, PR)]).then_inc(q.x_in, 16)

        x_load(0)
        sp.dma_start(w1_raw[:, :, :], a["w1T"]).then_inc(q.w1_in, 16)
        for t, n in ((fr, "fr"), (fi, "fi"), (dft, "dft")):
            sp.dma_start(t[:, :], a[n]).then_inc(q.m_in, 16)
        for b in range(2):
            sp.dma_start(a_raw[:, b, :, R:R2], a["ca1"]).then_inc(q.c_in, 16)
        for k in range(3):
            sp.dma_start(b_raw[k * R2 + R:(k + 1) * R2, :], a["cb1"]).then_inc(q.c_in, 16)
            for b in range(2):
                sp.dma_start(b2_raw[k * R2 + R:(k + 1) * R2, b, :], a["cb2"]).then_inc(q.c_in, 16)
        lora_loads(0, "a")
        lora_loads(0, "b", 0)
        sp.dma_start(w2_raw[:, :, 0:R], a["ca2"]).then_inc(q.w2_in, 16)
        sp.dma_start(w2_raw[:, :, R:], a["w2T"]).then_inc(q.w2_in, 16)
        lora_loads(0, "2")
        w_load(0)
        sp.dma_start(gw[:, :, :], a["gate_wT"]).then_inc(q.gw_in, 16)
        sp.dma_start(gnorm[:, :], a["gnorm"]).then_inc(q.gw_in, 16)
        sp.wait_ge(q.b_sp, 2)
        lora_loads(0, "b", 1)

        def q_store(p):
            sp.wait_ge(q.cq2, TP * p + TP)
            sp.sem_inc(q.sync_held, 1)
            sp.wait_ge(q.cch, CC * p + 8)
            sp.dma_start(q_d[ds(p * PR, PR), :].rearrange("(t p) c -> p t c", p=P), q_all[:, ds(p * TP, TP), :].bitcast(U32)).then_inc(q.q_out, 16)

        def feed(p, prev, pre):
            w_load(2 * p + 1)
            if pre:
                sp.wait_ge(q.xl, p + 1)
                x_load(p + 1)
                sp.wait_ge(q.a_sp, 2 * p + 2)
                lora_loads(p + 1, "a")
                sp.wait_ge(q.b_sp, 4 * p + 4)
                lora_loads(p + 1, "b", 0)
                sp.wait_ge(q.w2_sp, 4 * p + 4)
                sp.wait_ge(q.b2_sp, 2 * p + 2)
                lora_loads(p + 1, "2")
            w_load(2 * p + 2)
            if pre:
                sp.wait_ge(q.b_sp, 4 * p + 6)
                lora_loads(p + 1, "b", 1)
            if prev:
                q_store(p - 1)

        feed(0, False, True)
        sp.dma_start(xs[:, :, :], a["x"].rearrange("(t p) d -> p t d", p=P)).then_inc(q.xs_in, 16)
        with sp.Fori(1, NP - 1) as p:
            feed(p, True, True)
        feed(NP - 1, True, False)
        q_store(NP - 1)
        sp.wait_ge(q.q_out, 16 * NP)

        sp.wait_ge(q.built2, 2)
        sp.dma_start(y_d[DUMP:DUMP + 1, :].rearrange("a (b c) -> (a b) c", b=2), q_ta[0:2, :, :].rearrange("p k c -> p (k c)").bitcast(F32)).then_inc(q.zrow, 16)
        sp.wait_ge(q.zrow, 16)
        sp.sem_inc(q.rows_ok, 1)

        def s_load(c):
            n, part, k = c // 4, c // 2 % 2, c % 2
            need(sp, q.s_lo, c - 1)
            src = a["swi"][n, :, k, :] if part == 0 else a["swo"][n, :, 4 * k:4 * k + 4, :].rearrange("p k d -> p (k d)")
            sp.dma_start(raw[c % 2][:, :], src).then_inc(s_in[c % 2], 16)

        def y_store(kind, i, j):
            t = tile_at(kind, i, j, 0)
            sp.wait_ge(q.y_ok, t[3] + 1)
            sp.dma_start(y_d[ds(P * (t[3] - NT), P), :], ys[:, j, :]).then_inc(y_out[j], 16)

        sp.wait_ge(q.lg_sb, NT)
        s_load(0)
        s_load(1)
        with sp.Fori(0, E // 2) as i:
            for j in range(TE):
                y_store("expert", i, j)
        for c in range(2, 8):
            s_load(c)
        sp.dma_start(g1_sb[:, :, :], a["g1"]).then_inc(q.g1_in, 16)
        sp.dma_start(g2_sb[:, :, :], a["g2"]).then_inc(q.g1_in, 16)
        sp.dma_start(bias_b[:, :], a["bias"].partition_broadcast(P)).then_inc(q.g1_in, 16)

        def types(p):
            for b in range(2):
                sp.sem_inc(q.sync_held, 1)
                v = sp.value_load(a["types"][0:1, ds(2 * p + b, 1)], min_val=0, max_val=4)
                for m in range(4):
                    c = 4 * b + m
                    if c >= 2:
                        need(sp, q.tsp, 8 * p + c - 1)
                    elif isinstance(p, int) and p == 0:
                        sp.wait_ge(q.s_lo, 7 + c)
                    else:
                        need(sp, q.tsp, 8 * p + c - 1)
                    if m < 2:
                        src = a["wi"][ds(v, 1), :, m, :].rearrange("e p f -> (e p) f")
                    else:
                        src = a["wo"][ds(v, 1), :, 4 * (m - 2):4 * (m - 2) + 4, :].rearrange("e p k d -> (e p) (k d)")
                    sp.dma_start(raw[c % 2][:, :], src).then_inc(t_in[c % 2], 16)

        def store(p):
            for h in range(2):
                sp.wait_ge(q.f_ok, 2 * p + h + 1)
                sp.dma_start(a["out"][ds(p * PR + h * S, S), :].rearrange("(t p) d -> p t d", p=P), xs[:, ds(p * TP + 2 * h, 2), :]).then_inc(q.o_out, 16)

        types(0)
        with sp.Fori(1, NP) as p:
            types(p)
            store(p - 1)
        store(NP - 1)
        sp.wait_ge(q.o_out, 2 * 16 * NP)

    @block.tensor
    def _(pe):
        mm = nc.tensor.matmul

        pe.wait_ge(q.m_in, 48)
        for o in range(KD):
            for out_bank, terms in ((0, ((fr, 0), (fi, 1))), (1, ((fi, 0), (fr, 2)))):
                seq = [(w, t, k) for w, t in terms for k in range(KD)]
                for n, (w, t, k) in enumerate(seq):
                    last = mm(bank[out_bank][:, o * D:(o + 1) * D], w[:, k, o * P:(o + 1) * P], dft[:, t, k, :],
                              start=n == 0, stop=n == len(seq) - 1)
        last.then_inc(q.m1, 1)
        pe.wait_ge(q.m1e, 2)
        for m in range(KD):
            seq = [(w, t, k) for w, t in ((a_re, 0), (a_im, 2)) for k in range(KD)]
            for n, (w, t, k) in enumerate(seq):
                last = mm(bank[2][:, m * D:(m + 1) * D], w[:, k, m * P:(m + 1) * P], dft[:, t, k, :],
                          start=n == 0, stop=n == len(seq) - 1)
        last.then_inc(q.m2, 1)

        def low_rank(p):
            pe.wait_ge(q.xl, p + 1)
            pe.wait_ge(q.a_sp, 2 * p + 2)
            for b in range(2):
                seq = [(w, x, k) for k in range(KD) for w, x in hlh((a_hi, a_lo), (x_hi, x_lo))]
                for n, (w, x, k) in enumerate(seq):
                    last = mm(bank[LOW][0:R3, b * S:(b + 1) * S], w[:, b, k, :], x[:, k, b * S:(b + 1) * S],
                              start=n == 0, stop=n == len(seq) - 1)
            last.then_inc(q.low_ps, 1)

        def turn_c(p, j):
            t = TP * p + j
            pe.wait_ge(q.c_done, t + 1)
            if j == 0:
                need(pe, q.lowl, p + 1)
            if j:
                pe.wait_ge(q.ct_sb, t)
            for k in range(KD):
                last = nc.tensor.transpose(bank[CT][:, k * P:(k + 1) * P], c_sb[:, j, k * P:(k + 1) * P], id_f[:, :])
            last.then_inc(q.ct_ps, 1)

        def router(p, j):
            t = TP * p + j
            pe.wait_ge(q.ct_sb, t + 1)
            if j:
                pe.wait_ge(q.lg_sb, t)
            pe.wait_ge(q.low2l, TP * p + TP)
            for k in range(KD):
                last = mm(bank[LG][:, 0:E], c_t[:, k, :], gw[:, k, :], start=k == 0, stop=k == KD - 1)
            last.then_inc(q.lg_ps, 1)

        def turn_low(p, j):
            pe.wait_ge(q.low2s, 2 * (TP * p + j + 1))
            need(pe, q.low2l, TP * p + j)
            if j == 0:
                need(pe, q.lg_sb, TP * p)
            nc.tensor.transpose(bank[LT][0:R3, 0:P], low2[:, :, :].rearrange("p a b -> p (a b)"), id_f[:, :]).then_inc(q.low2t_ps, 1)

        def finish(p, j):
            pe.wait_ge(q.low2l, TP * p + j + 1)
            mm(bank[OB[j % 3]][:, COLS[j // 2][1]], low2t[:, :], b2_st[:, j // 2, :],
               start=False, stop=True, skip_group_check=True).then_inc(q.c_ps, 1)

        def feed(p, prev, pre):
            for f in range(KF):
                if f == 0:
                    pe.wait_ge(q.lowl, p + 1)
                    pe.wait_ge(q.b_sp, 4 * p + 4)
                need(pe, q.hl, KF * p + f - 2)
                fs = slice(f * P, (f + 1) * P)
                seq = [(w, x, k) for k in range(KD) for w, x in hlh((w1_hi, w1_lo), (x_hi, x_lo))]
                for n, (w, x, k) in enumerate(seq):
                    mm(bank[HB[f % 3]][:, :], w[:, k, fs], x[:, k, :], start=n == 0, stop=False, skip_group_check=True)
                for b in range(2):
                    last = mm(bank[HB[f % 3]][:, b * S:(b + 1) * S], b_st[:, b, fs], low[:, b * S:(b + 1) * S],
                              start=False, stop=b == 1, skip_group_check=True)
                last.then_inc(q.h_ps, 1)
                if prev:
                    if f == 0:
                        finish(p - 1, 2)
                        turn_low(p - 1, 3)
                    if f == 1:
                        finish(p - 1, 3)
                    if 2 <= f < 2 + TP:
                        turn_c(p - 1, f - 2)
                    if 3 <= f < 3 + TP:
                        router(p - 1, f - 3)

            def down(j):
                c0 = COLS[j // 2][0]
                need(pe, q.c_done, TP * p if j < 3 else TP * p + 1)
                for f in range(KF):
                    for n, (h, w) in enumerate(((h_hi, w2_hi), (h_hi, w2_lo), (h_lo, w2_hi))):
                        last = mm(bank[OB[j % 3]][:, 0:UP], h[:, f, j * P:(j + 1) * P], w[:, f, c0:c0 + UP],
                                  start=f == 0 and n == 0, stop=False, skip_group_check=True)
                last.then_inc(q.l2_ps, 1)

            pe.wait_ge(q.hl, KF * p + KF)
            pe.wait_ge(q.w2_sp, 4 * p + 4)
            pe.wait_ge(q.b2_sp, 2 * p + 2)
            if isinstance(p, int) and p == 0:
                pe.wait_ge(q.w2l, 1)
            down(0)
            down(1)
            turn_low(p, 0)
            need(pe, q.ct_sb, TP * p)
            if pre:
                low_rank(p + 1)
            down(2)
            finish(p, 0)
            turn_low(p, 1)
            down(3)
            finish(p, 1)
            turn_low(p, 2)

        pe.wait_ge(q.w1l, 1)
        low_rank(0)
        pe.wait_ge(q.ml, 1)
        pe.wait_ge(q.id0, 4)
        feed(0, False, True)
        pe.wait_ge(q.gwok, 2)
        with pe.Fori(1, NP - 1) as p:
            feed(p, True, True)
        feed(NP - 1, True, False)
        finish(NP - 1, 2)
        turn_low(NP - 1, 3)
        finish(NP - 1, 3)
        for j in range(TP):
            turn_c(NP - 1, j)
            router(NP - 1, j)

        pe.wait_ge(q.r_ps, 1)
        sel = sel_b[:, :, :].rearrange("p t e -> p (t e)")
        mm(bank[RB][:, 0:NT * E], triu[:, :], sel, start=True, stop=True)
        mm(bank[RB][:, NT * E:2 * NT * E], ones[:, :], sel, start=True, stop=True).then_inc(q.r_inv, 1)

        pe.wait_ge(q.cnt_rd, 1)
        for k in range(2):
            pe.wait_ge(q.oh_ok, 3 * (k + 1))
            for t in range(NT):
                last = mm(bank[RB][:, 0:ST], oh_p[:, k, t, :], oh_c[:, k, t, :], start=k == 0 and t == 0, stop=k == 1 and t == NT - 1)
        last.then_inc(q.oh_used, 1)

        def rows_of(kind, i, j, c):
            if kind == "shared":
                return q_all[:, ds(TP * i + j, 1), c].rearrange("p a c -> p (a c)")
            return xg[:, ds(TE * i + j, 1), c].rearrange("p a c -> p (a c)")

        def weights(kind, i, j):
            if kind == "shared":
                return [(None, wq_s[:, :])]
            if j == MID:
                return [(0, wq[:, ds(2 * i, 1), :].rearrange("p e c -> p (e c)")),
                        (1, wq[:, ds(2 * i + 1, 1), :].rearrange("p e c -> p (e c)"))]
            return [(None, wq[:, ds(2 * i + (1 if j > MID else 0), 1), :].rearrange("p e c -> p (e c)"))]

        def mlp_step(kind, i, j, t1=True):
            if t1:
                _, ii, jj, g = tile_at(kind, i, j, 0)
                need(pe, q.q_tc, g)
                if kind == "expert" and j == 0:
                    pe.wait_ge(q.rows_in, i + 1)
                for k in range(KD):
                    last = nc.tensor.transpose(bank_b[QT][:, k * P:(k + 1) * P], rows_of(kind, i, j, slice(k * P, (k + 1) * P)), id_b[:, :])
                last.then_inc(q.q_tp, 1)
            back1 = tile_at(kind, i, j, 1) if t1 or j == 0 else None
            if back1:
                kd, ii, jj, g = back1
                pe.wait_ge(q.q_tc, g + 1)
                r = jj % 2
                same = kd == "expert" and jj == 0 and not (isinstance(ii, int) and ii == 0)
                need(pe, q.hmul, g if same else g - 1)
                for out_bank, c0 in ((GB[r], 0), (YB[r], I)):
                    seq = [(m, w, k) for m, w in weights(kd, ii, jj) for k in range(KD)]
                    for n, (m, w, k) in enumerate(seq):
                        lhs = q_t[:, turned_of(kd, jj), k, :] if m is None else (q_ta, q_tb)[m][:, k, :]
                        last = mm(bank[out_bank][:, :], lhs, w[:, k * 2 * I + c0:k * 2 * I + c0 + I],
                                  start=n == 0, stop=n == len(seq) - 1)
                last.then_inc(q.gu, 1)
            back4 = tile_at(kind, i, j, 4)
            if back4:
                kd, ii, jj, g = back4
                pe.wait_ge(q.h_tc, g + 1)
                need(pe, q.y_ok, g)
                seq = [(m, w, k) for m, w in weights(kd, ii, jj) for k in range(KI)]
                for n, (m, w, k) in enumerate(seq):
                    lhs = h_t[:, k, :] if m is None else (h_ta, h_tb)[m][:, k, :]
                    last = mm(bank[DN][:, 0:D], lhs, w[:, GW + k * D:GW + (k + 1) * D], start=n == 0, stop=n == len(seq) - 1)
                last.then_inc(q.dn, 1)
            back3 = tile_at(kind, i, j, 3) if t1 or j < 3 else None
            if back3:
                kd, ii, jj, g = back3
                pe.wait_ge(q.hq2, g + 1)
                need(pe, q.h_tc, g)
                for k in range(KI):
                    last = nc.tensor.transpose(bank_b[HT][:, k * P:(k + 1) * P], hq[:, ring_of(kd, jj), k * P:(k + 1) * P], id_b[:, :])
                last.then_inc(q.h_tp, 1)

        pe.wait_ge(q.w_out, WC * (E + 1))
        pe.wait_ge(q.built2, 4)
        steps(pe, "shared", mlp_step)
        steps(pe, "expert", mlp_step)
        for j in range(4):
            mlp_step("expert", E // 2, j, t1=False)

        def turn_x(p):
            need(pe, q.f_ok, 2 * (p - 1))
            for k in range(KD):
                for j in range(TP):
                    pe.wait_ge(q.comb, 2 * (TP * p + j + 1))
                    last = nc.tensor.transpose(bank[XT[k]][:, j * P:(j + 1) * P], gat[:, 2 * j, k * P:(k + 1) * P], id_f[:, :])
                last.then_inc(q.xt_ps, 1)

        def up(p, st):
            n, f = st // KF, st % KF
            fs = slice(f * P, (f + 1) * P)
            out = bank[HB[st % 3]]
            need(pe, q.h4l, 3 * KF * p + st - 2)
            if st == 0:
                pe.wait_ge(q.x4l, KD * p + KD)
            if n < 2:
                if f == 0 and isinstance(p, int) and p == 0:
                    pe.wait_ge(q.s_lo, 4 * n + 2)
                seq = [(w, x, k) for k in range(KD) for w, x in hlh(sw1[n], (x_hi, x_lo))]
                for m, (w, x, k) in enumerate(seq):
                    last = mm(out[:, :], w[:, k, fs], x[:, k, :], start=m == 0, stop=m == len(seq) - 1)
            else:
                if f == 0:
                    pe.wait_ge(q.tsp, 8 * p + 8)
                for b in range(2):
                    seq = [(w, x, k) for k in range(KD) for w, x in hlh(tw1[b], (x_hi, x_lo))]
                    for m, (w, x, k) in enumerate(seq):
                        last = mm(out[:, b * S:(b + 1) * S], w[:, k, fs], x[:, k, b * S:(b + 1) * S],
                                  start=b == 0 and m == 0, stop=m == len(seq) - 1, skip_group_check=True)
            last.then_inc(q.hp, 1)

        def down4(p, st):
            n, f = st // KF, st % KF
            pe.wait_ge(q.h4l, 3 * KF * p + st + 1)
            if f == 0:
                need(pe, q.ne_a, 3 * p + n)
                need(pe, q.ne_d, 3 * p + n)
                if n < 2 and isinstance(p, int) and p == 0:
                    pe.wait_ge(q.s_lo, 4 * n + 4)
            h = ring[st % 3]
            for m in range(KD):
                ms = slice(m * P, (m + 1) * P)
                for b in ((None,) if n < 2 else (0, 1)):
                    cs = slice(0, PR) if b is None else slice(b * S, (b + 1) * S)
                    w2 = sw2[n] if b is None else tw2[b]
                    for t, (w, x) in enumerate(hlh(w2, h)):
                        last = mm(bank[AC[m]][:, cs], w[:, f, ms], x[:, cs], start=f == 0 and t == 0 and b != 1,
                                  stop=f == KF - 1 and t == 2, skip_group_check=True)
            last.then_inc(q.l2d, 1)

        def gate1(p):
            pe.wait_ge(q.ne_d, 3 * p + 3)
            pe.wait_ge(q.ne_a, 3 * p + 3)
            for m in range(KD):
                for n, net in enumerate((2, 0, 1)):
                    for k in range(KD):
                        last = mm(bank[GT][:, 2 * m:2 * m + 2], g1_sb[:, n * KD + k, m * P:(m + 1) * P], nets[:, net, k, 0:PR:S],
                                  start=n == 0 and k == 0, stop=n == 2 and k == KD - 1)
            last.then_inc(q.g1_ps, 1)

        def gate2(p):
            pe.wait_ge(q.gt_ok, p + 1)
            for b in range(2):
                for m in range(KD):
                    last = mm(bank[GT][:, 8 + 3 * b:11 + 3 * b], gh_b[:, m, b, :], g2_sb[:, m, :], start=m == 0, stop=m == KD - 1)
            last.then_inc(q.g2_ps, 1)

        def fourier(p, last_pair=False):
            pe.wait_ge(q.zl, p + 1)
            pe.wait_ge(q.x4l, KD * p + KD if last_pair else KD * p + 2 * KD)
            for j in range(TP):
                seq = [(z, w, k) for k in range(KD) for z, w in ((z_hi, m_hi), (z_hi, m_lo), (z_lo, m_hi))]
                for n, (z, w, k) in enumerate(seq):
                    last = mm(bank[XT[j // 2]][:, (j % 2) * D:(j % 2 + 1) * D], z[:, k, j * P:(j + 1) * P], w[:, k, :],
                              start=n == 0, stop=n == len(seq) - 1)
                if j % 2:
                    last.then_inc(q.f_ps, 1)

        def mix(p, prev, pre):
            for st in range(3 * KF):
                up(p, st)
                if st >= 2:
                    down4(p, st - 2)
                if prev:
                    if st == 2:
                        gate1(p - 1)
                    if st == 4:
                        gate2(p - 1)
                    if st == 13:
                        fourier(p - 1)
                if pre and st == 20:
                    turn_x(p + 1)
            down4(p, 3 * KF - 2)
            down4(p, 3 * KF - 1)

        pe.wait_ge(q.g1_in, 48)
        turn_x(0)
        mix(0, False, True)
        with pe.Fori(1, NP - 1) as p:
            mix(p, True, True)
        mix(NP - 1, True, False)
        gate1(NP - 1)
        gate2(NP - 1)
        fourier(NP - 1, True)

    @block.scalar
    def _(act):
        fn = nc.scalar.activation
        cp = nc.scalar.copy

        def x_high(p):
            act.wait_ge(q.x_in, 16 * (p + 1))
            need(act, q.h_ps, KF * p)
            cp(x_hi[:, :, :], x_raw[:, :, :]).then_inc(q.xh, 1)

        def low_high(p):
            act.wait_ge(q.low_ps, p + 1)
            need(act, q.h_ps, KF * p)
            fn(low[:, :], bank[LOW][0:R3, :], ACT.Copy, scale=2.0).then_inc(q.lowh, 1)

        def w_abs(n, c):
            act.wait_ge(w_in[c], 16 * (n + 1))
            fn(w_dst(n)[:, c * F:(c + 1) * F], w_raw[:, c * F:(c + 1) * F], ACT.Abs, accum_out=wsum[:, c:c + 1]).then_inc(q.w_abs, 1)

        def w_round(n, c):
            if c == 0:
                act.wait_ge(q.w_rec, 2 * n + 1)
            k = c // KD
            cs = slice(c * F, (c + 1) * F)
            fn(w_raw[:, cs], w_raw[:, cs], ACT.Identity, scale=wrec[:, k:k + 1], bias=RND).then_inc(q.w_rnd, 1)

        act.wait_ge(q.built, 7)
        x_high(0)
        act.wait_ge(q.w1_in, 16)
        cp(w1_hi[:, :, :], w1_raw[:, :, :]).then_inc(q.w1h, 1)
        act.wait_ge(q.m1, 1)
        cp(a_re[:, :, :].rearrange("p k d -> p (k d)"), bank[0][:, :]).then_inc(q.m1e, 1)
        cp(a_im[:, :, :].rearrange("p k d -> p (k d)"), bank[1][:, :]).then_inc(q.m1e, 1)
        low_high(0)
        act.wait_ge(q.m2, 1)
        fn(m_hi[:, :, :].rearrange("p k d -> p (k d)"), bank[2][:, :], ACT.Copy, scale=1.0 / D).then_inc(q.mh, 1)
        act.wait_ge(q.w2_in, 32)
        cp(w2_hi[:, :, R:R2 + D], w2_raw[:, :, :]).then_inc(q.w2h, 1)
        for c in range(WC):
            w_abs(0, c)
        for c in range(WC):
            w_round(0, c)

        def feed(p, prev, pre):
            for f in range(KF):
                act.wait_ge(q.h_ps, KF * p + f + 1)
                if f == 0:
                    need(act, q.l2_ps, TP * p)
                fn(h_hi[:, f, :], bank[HB[f % 3]][:, :], ACT.Relu).then_inc(q.hh, 1)
                if prev and f == 0:
                    c_out(p - 1, 2)
                    low_turned(p - 1, 3)
                if prev and f == 1:
                    c_out(p - 1, 3)
                if prev and 2 <= f < 2 + TP:
                    turned(p - 1, f - 2)
                if 1 <= f < 1 + WC:
                    w_abs(2 * p + 1, f - 1)
                if prev and 4 <= f < 4 + TP:
                    c_round(p - 1, f - 4)
                if KF - WC <= f:
                    w_round(2 * p + 1, f - KF + WC)
            if pre:
                x_high(p + 1)
            n = 2 * p + 2
            w_abs(n, 0)
            low_out(p, 0)
            w_abs(n, 1)
            low_out(p, 1)
            w_abs(n, 2)
            low_turned(p, 0)
            if pre:
                low_high(p + 1)
            low_out(p, 2)
            c_out(p, 0)
            low_turned(p, 1)
            w_round(n, 0)
            low_out(p, 3)
            c_out(p, 1)
            w_round(n, 1)
            low_turned(p, 2)
            w_round(n, 2)

        def low_out(p, j):
            t = TP * p + j
            act.wait_ge(q.l2_ps, t + 1)
            need(act, q.low2t_ps, t)
            for c, dst in ((COLS[j // 2][2], slice(0, R)), (COLS[j // 2][3], slice(R, R2))):
                src = bank[OB[j % 3]][:, c].rearrange("p (a r) -> p a r", a=1).broadcast_to([P, 3, R])
                fn(low2[:, :, dst], src, ACT.Copy, scale=2.0).then_inc(q.low2s, 1)

        def low_turned(p, j):
            t = TP * p + j
            act.wait_ge(q.low2t_ps, t + 1)
            need(act, q.c_ps, t)
            cp(low2t[:, :], bank[LT][0:R3, 0:P]).then_inc(q.low2h, 1)

        def c_out(p, j):
            t = TP * p + j
            act.wait_ge(q.c_ps, t + 1)
            if j == 0:
                need(act, q.cch, CC * p)
                need(act, q.ct_ps, TP * p)
                need(act, q.cq1, TP * p)
                need(act, q.lg_ps, TP * p)
                need(act, q.cq2, TP * p)
            need(act, q.csq, t)
            src = bank[OB[j % 3]][:, COLS[j // 2][1]]
            fn(c_junk[:, :], src, ACT.Square, accum_out=cst[:, 0, j:j + 1]).then_inc(q.csq, 1)
            cp(c_sb[:, j, :], src).then_inc(q.c_done, 1)

        def c_round(p, j):
            t = TP * p + j
            act.wait_ge(q.cch, CC * p + 7)
            if j:
                act.wait_ge(q.cq2, t)
            fn(c_tmp[:, :], c_sb[:, j, :], ACT.Identity, scale=cst[:, 6, j:j + 1], bias=RND).then_inc(q.cq1, 1)

        def turned(p, j):
            t = TP * p + j
            act.wait_ge(q.ct_ps, t + 1)
            if j:
                act.wait_ge(q.lg_ps, t)
            cp(c_t[:, :, :].rearrange("p k d -> p (k d)"), bank[CT][:, 0:D]).then_inc(q.ct_sb, 1)

        feed(0, False, True)
        with act.Fori(1, NP - 1) as p:
            feed(p, True, True)
        feed(NP - 1, True, False)
        c_out(NP - 1, 2)
        low_turned(NP - 1, 3)
        c_out(NP - 1, 3)
        for j in range(TP):
            turned(NP - 1, j)
        for j in range(TP):
            c_round(NP - 1, j)

        act.wait_ge(q.r_sub, 1)
        fn(rt[1][:, :, :], rt[0][:, :, :], ACT.Exp).then_inc(q.r_exp, 1)

        def mlp_step(kind, i, j, t1=True):
            def at(lag):
                return tile_at(kind, i, j, lag) if t1 or j < lag else None
            if at(4):
                kd, ii, jj, g = at(4)
                act.wait_ge(q.h_tp, g + 1)
                need(act, q.dn, g)
                src = bank_b[HT][:, 0:I]
                if kd == "expert" and jj == MID:
                    src = src.rearrange("p (k c) -> p k c", k=KI)
                    cp(h_ta[:, :, 0:HALF], src[:, :, 0:HALF])
                    cp(h_tb[:, :, HALF:], src[:, :, HALF:]).then_inc(q.h_tc, 1)
                else:
                    cp(h_t[:, :, :].rearrange("p k c -> p (k c)"), src).then_inc(q.h_tc, 1)
            if at(1):
                kd, ii, jj, g = at(1)
                r = ring_of(kd, jj)
                act.wait_ge(q.gu, g + 1)
                act.wait_ge(q.msg, g + 1)
                need(act, q.hmul, g)
                fn(g_sb[:, :], bank[GB[jj % 2]][:, :], ACT.Silu, scale=mst[:, jj, 2:3]).then_inc(q.silu, 1)
            if at(1):
                kd, ii, jj, g = at(1)
                r = ring_of(kd, jj)
                act.wait_ge(q.hmul, g + 1)
                need(act, q.mch, 6 * (g - 3))
                need(act, q.hsq, g)
                fn(m_junk[:, :], hf[:, r, :], ACT.Square, accum_out=mst[:, jj, 0:1]).then_inc(q.hsq, 1)
            if at(2):
                kd, ii, jj, g = at(2)
                r = ring_of(kd, jj)
                act.wait_ge(q.mch, 6 * g + 5)
                fn(hf[:, r, :], hf[:, r, :], ACT.Identity, scale=mst[:, jj, 6:7], bias=RND).then_inc(q.hq1, 1)

        steps(act, "shared", mlp_step)
        steps(act, "expert", mlp_step)
        for j in range(4):
            mlp_step("expert", E // 2, j, t1=False)

        for c in range(8):
            act.wait_ge(s_in[c % 2], 16 * (c // 2 + 1))
            if c == 0:
                act.wait_ge(q.y_ok, NT + ST)
            if c == 4:
                for k in range(TE):
                    act.wait_ge(y_out[k], 16 * (E // 2))
            cp(split_dst(sw1, sw2, c // 4, c % 4, 0), raw[c % 2][:, :]).then_inc(q.s_hi, 1)

        def x4_high(p):
            for k in range(KD):
                act.wait_ge(q.xt_ps, KD * p + k + 1)
                need(act, q.hp, 3 * KF * p)
                cp(x_hi[:, k, :], bank[XT[k]][:, :]).then_inc(q.x4h, 1)

        def net_out(p, n):
            act.wait_ge(q.l2d, 3 * KF * p + KF * (n + 1))
            if n == 0:
                need(act, q.zl, p)
                need(act, q.zh, p)
            else:
                need(act, q.f_ps, 2 * p)
            cp(nets[:, n, 0, :], bank[AC[0]][:, :]).then_inc(q.ne_a, 1)

        def gate_hidden(p):
            act.wait_ge(q.g1_ps, p + 1)
            fn(gh[:, :, :].rearrange("p m b -> p (m b)"), bank[GT][:, 0:2 * KD], ACT.Relu).then_inc(q.gh_ok, 1)

        def gate_exp(p):
            act.wait_ge(q.gch, 12 * p + 3)
            fn(gl[:, 3, :, :], gl[:, 2, :, :], ACT.Exp).then_inc(q.gexp, 1)

        def z_high(p):
            act.wait_ge(q.gch, 12 * p + 12)
            cp(z_hi[:, :, :], nets[:, 0, :, :]).then_inc(q.zh, 1)

        def type_high(p, c):
            act.wait_ge(t_in[c % 2], 16 * (4 * p + c // 2 + 1))
            if c == 0:
                need(act, q.l2d, 3 * KF * p)
            cp(split_dst(tw1, tw2, c // 4, c % 4, 0), raw[c % 2][:, :]).then_inc(q.thi, 1)

        def mix(p, prev, pre):
            for st in range(3 * KF):
                act.wait_ge(q.hp, 3 * KF * p + st + 1)
                need(act, q.l2d, 3 * KF * p + st - 2)
                fn(ring[st % 3][0][:, :], bank[HB[st % 3]][:, :], ACT.Relu).then_inc(q.h4h, 1)
                if st in (KF + 1, 2 * KF + 1):
                    net_out(p, st // KF - 1)
                if st < 8 and (prev or st >= 2):
                    type_high(p, st)
                if prev and st == 2:
                    gate_hidden(p - 1)
                if prev and st == 5:
                    gate_exp(p - 1)
                if prev and st == 8:
                    z_high(p - 1)
            if pre:
                x4_high(p + 1)
            net_out(p, 2)

        x4_high(0)
        type_high(0, 0)
        type_high(0, 1)
        mix(0, False, True)
        with act.Fori(1, NP - 1) as p:
            mix(p, True, True)
        mix(NP - 1, True, False)
        gate_hidden(NP - 1)
        gate_exp(NP - 1)
        z_high(NP - 1)

    @block.vector
    def _(v):
        ts, tt, stt, red = (nc.vector.tensor_scalar, nc.vector.tensor_tensor, nc.vector.scalar_tensor_tensor,
                            nc.vector.tensor_reduce)

        def x_low(p):
            v.wait_ge(q.xh, p + 1)
            tt(x_lo[:, :, :], x_raw[:, :, :], x_hi[:, :, :].bitcast(F32), ALU.subtract).then_inc(q.xl, 1)

        def low_low(p):
            v.wait_ge(q.lowh, p + 1)
            stt(low[R2:2 * R2, :], bank[LOW][R2:2 * R2, :], 2.0, low[R2:2 * R2, :].bitcast(F32), ALU.mult, ALU.subtract).then_inc(q.lowl, 1)

        def w_recip(n):
            v.wait_ge(q.w_m, 4 * (n + 1))
            nc.vector.reciprocal(wrec[:, :], wsum[:, 4:6]).then_inc(q.w_rec, 1)
            nc.vector.tensor_copy(flat(wscale[:, ds(n, 1), :]), wsum[:, 4:6]).then_inc(q.w_rec, 1)

        def w_clip(n, c):
            cs = slice(c * F, (c + 1) * F)
            v.wait_ge(q.w_rnd, WC * n + c + 1)
            ts(w_raw[:, cs], w_raw[:, cs], ROUND, -1.0, ALU.subtract, ALU.max).then_inc(q.w_clip, 1)
            v.wait_ge(q.w_clip, WC * n + c + 1)
            ts(w_dst(n)[:, cs], w_raw[:, cs], 1.0, None, ALU.min).then_inc(q.w_out, 1)

        def b_split(p, half):
            v.wait_ge(q.b_in, 48 * (2 * p + half + 1))
            need(v, q.h_ps, KF * p)
            nc.vector.tensor_copy(b_st[:, half, :], b_raw[:, :]).then_inc(q.b_sp, 1)
            v.wait_ge(q.b_sp, 4 * p + 2 * half + 1)
            rows = slice(2 * R2, R3)
            tt(b_st[rows, half, :], b_raw[rows, :], b_st[rows, half, :].bitcast(F32), ALU.subtract).then_inc(q.b_sp, 1)

        x_low(0)
        v.wait_ge(q.w1h, 1)
        tt(w1_lo[:, :, :], w1_raw[:, :, :], w1_hi[:, :, :].bitcast(F32), ALU.subtract).then_inc(q.w1l, 1)
        v.wait_ge(q.c_in, 16 * 11)
        b_split(0, 0)
        low_low(0)
        b_split(0, 1)
        v.wait_ge(q.mh, 1)
        stt(m_lo[:, :, :].rearrange("p k d -> p (k d)"), bank[2][:, :], 1.0 / D,
            m_hi[:, :, :].rearrange("p k d -> p (k d)").bitcast(F32), ALU.mult, ALU.subtract).then_inc(q.ml, 1)
        v.wait_ge(q.w2h, 1)
        tt(w2_lo[:, :, R:R2 + D], w2_raw[:, :, :], w2_hi[:, :, R:R2 + D].bitcast(F32), ALU.subtract).then_inc(q.w2l, 1)
        w_recip(0)
        for c in range(WC):
            w_clip(0, c)

        def logit_out(p, j):
            t = TP * p + j
            v.wait_ge(q.lg_ps, t + 1)
            v.wait_ge(q.cch, CC * p + CC)
            ts(flat(logits[:, ds(t, 1), :]), bank[LG][:, 0:E], cst[:, 8, j:j + 1], None, ALU.mult).then_inc(q.lg_sb, 1)

        def low_turned(p, j):
            v.wait_ge(q.low2h, TP * p + j + 1)
            tt(low2t[R2:2 * R2, :], bank[LT][R2:2 * R2, 0:P], low2t[R2:2 * R2, :].bitcast(F32), ALU.subtract).then_inc(q.low2l, 1)

        def c_max(p, j):
            t = TP * p + j
            v.wait_ge(q.c_done, t + 1)
            if j == 0:
                need(v, q.cch, CC * p)
            red(cst[:, 1, j:j + 1], c_sb[:, j, :], X, ALU.max, apply_absolute_value=True).then_inc(q.camax, 1)

        def c_quant(p, j):
            t = TP * p + j
            v.wait_ge(q.cq1, t + 1)
            ts(flat(q_all[:, ds(t, 1), 0:D]), c_tmp[:, :], ROUND, None, ALU.subtract).then_inc(q.cq2, 1)

        def feed(p, prev, pre):
            for f in range(KF):
                v.wait_ge(q.hh, KF * p + f + 1)
                stt(h_lo[:, f, :], bank[HB[f % 3]][:, :], 0.0, h_hi[:, f, :].bitcast(F32), ALU.max, ALU.subtract).then_inc(q.hl, 1)
                if prev and f == 0:
                    c_max(p - 1, 2)
                    low_turned(p - 1, 3)
                if prev and f == 1:
                    c_max(p - 1, 3)
                if f == 4:
                    w_recip(2 * p + 1)
                if prev and 4 <= f < 4 + TP:
                    logit_out(p - 1, f - 4)
                if prev and 5 <= f < 4 + TP:
                    c_quant(p - 1, f - 5)
                if f > KF - WC:
                    w_clip(2 * p + 1, f - 1 - KF + WC)
            if prev:
                c_quant(p - 1, TP - 1)
            w_clip(2 * p + 1, WC - 1)
            if pre:
                x_low(p + 1)
                b_split(p + 1, 0)
            low_turned(p, 0)
            if pre:
                low_low(p + 1)
            n = 2 * p + 2
            w_recip(n)
            c_max(p, 0)
            low_turned(p, 1)
            w_clip(n, 0)
            if pre:
                b_split(p + 1, 1)
            c_max(p, 1)
            w_clip(n, 1)
            low_turned(p, 2)
            w_clip(n, 2)

        feed(0, False, True)
        with v.Fori(1, NP - 1) as p:
            feed(p, True, True)
        feed(NP - 1, True, False)
        c_max(NP - 1, 2)
        low_turned(NP - 1, 3)
        c_max(NP - 1, 3)
        for j in range(TP):
            logit_out(NP - 1, j)
        for j in range(TP):
            c_quant(NP - 1, j)

        count = [0]

        def step():
            v.wait_ge(q.route, count[0])

        def done():
            count[0] += 1
            return q.route, 1

        full = [P, NT, E]

        def over(c):
            return c[:, :].rearrange("p (t a) -> p t a", a=1).broadcast_to(full)

        def each(c):
            return c[:, :].rearrange("p (a e) -> p a e", a=1).broadcast_to(full)

        v.wait_ge(q.lg_sb, NT)
        v.wait_ge(q.built2, 9)
        red(c16[0][:, :], logits[:, :, :], X, ALU.max).then_inc(*done())
        step()
        tt(rt[0][:, :, :], logits[:, :, :], over(c16[0]), ALU.subtract).then_inc(q.r_sub, 1)
        v.wait_ge(q.r_exp, 1)
        red(c16[1][:, :], rt[1][:, :, :], X, ALU.add).then_inc(*done())
        step()
        nc.vector.reciprocal(c16[2][:, :], c16[1][:, :]).then_inc(*done())
        step()
        tt(rt[2][:, :, :], rt[1][:, :, :], over(c16[2]), ALU.mult).then_inc(*done())
        step()

        def best(probs, weight, place, eq, one):
            red(weight[:, :], probs[:, :, :], X, ALU.max).then_inc(*done())
            step()
            tt(eq[:, :, :], probs[:, :, :], over(weight), ALU.is_equal).then_inc(*done())
            step()
            tt(eq[:, :, :], eq[:, :, :], each(rev8), ALU.mult).then_inc(*done())
            step()
            red(place[:, :], eq[:, :, :], X, ALU.max).then_inc(*done())
            step()
            tt(one[:, :, :], eq[:, :, :], over(place), ALU.is_equal).then_inc(*done())
            step()

        best(rt[2], c16[3], c16[4], rt[4], rt[3])
        stt(rt[6][:, :, :], rt[3][:, :, :], -2.0, rt[2][:, :, :], ALU.mult, ALU.add).then_inc(*done())
        step()
        best(rt[6], c16[5], c16[6], rt[4], rt[5])
        ts(c16[7][:, :], c16[5][:, :], 0.0, None, ALU.is_gt).then_inc(*done())
        step()
        tt(rt[5][:, :, :], rt[5][:, :, :], over(c16[7]), ALU.mult).then_inc(*done())
        step()
        tt(sel_b[:, :, :], rt[3][:, :, :], rt[5][:, :, :], ALU.add).then_inc(q.r_ps, 1)

        v.wait_ge(q.r_inv, 1)
        totals = bank[RB][:, NT * E:2 * NT * E].rearrange("p (t e) -> p t e", e=E)
        inner = bank[RB][:, 0:NT * E].rearrange("p (t e) -> p t e", e=E)
        nc.vector.memset(cum[0][:, 0:1, :], 0.0).then_inc(*done())
        nc.vector.tensor_copy(cum[0][:, 1:NT + 1, :], totals).then_inc(*done())
        step()
        src, d = 0, 1
        while d < NT:
            tt(cum[1 - src][:, d:, :], cum[src][:, d:, :], cum[src][:, 0:NT + 1 - d, :], ALU.add).then_inc(*done())
            nc.vector.tensor_copy(cum[1 - src][:, 0:d, :], cum[src][:, 0:d, :]).then_inc(*done())
            step()
            src, d = 1 - src, 2 * d
        tt(rt[4][:, :, :], inner, cum[src][:, 0:NT, :], ALU.add).then_inc(q.cnt_rd, 1)
        v.wait_ge(q.cnt_rd, 1)
        stt(rt[6][:, :, :], rt[4][:, :, :], float(CAP), sel_b[:, :, :], ALU.is_le, ALU.mult).then_inc(*done())
        tt(rt[7][:, :, :], rt[4][:, :, :], each(e_off), ALU.add).then_inc(*done())
        step()
        tt(rt[7][:, :, :], rt[7][:, :, :], rt[6][:, :, :], ALU.mult).then_inc(*done())
        step()
        for k, (one, weight) in enumerate(((rt[3], c16[3]), (rt[5], c16[5]))):
            slot = c16[8 + k]
            tt(rt[0][:, :, :], rt[7][:, :, :], one[:, :, :], ALU.mult).then_inc(*done())
            tt(rt[1][:, :, :], rt[6][:, :, :], one[:, :, :], ALU.mult).then_inc(*done())
            step()
            red(slot[:, :], rt[0][:, :, :], X, ALU.add).then_inc(*done())
            red(c16[0][:, :], rt[1][:, :, :], X, ALU.add).then_inc(*done())
            step()
            ts(slot[:, :], slot[:, :], float(DUMP), None, ALU.add).then_inc(*done())
            tt(wts[:, k, :], c16[0][:, :], weight[:, :], ALU.mult).then_inc(*done())
            step()
            nc.vector.tensor_copy(slots[:, k, :], slot[:, :]).then_inc(*done())
            ts(c16[1 + 4 * k][:, :], slot[:, :], -(P - 1) / 2, 1.0 / P, ALU.add, ALU.mult).then_inc(*done())
            step()
            ts(c16[1 + 4 * k][:, :], c16[1 + 4 * k][:, :], ROUND, ROUND, ALU.add, ALU.subtract).then_inc(*done())
            step()
            stt(c16[2 + 4 * k][:, :], c16[1 + 4 * k][:, :], -float(P), slot[:, :], ALU.mult, ALU.add).then_inc(*done())
            step()

        for k in range(2):
            tile, place = c16[1 + 4 * k], c16[2 + 4 * k]

            def wide(c, n):
                return c[:, :].rearrange("p (t a) -> p t a", a=1).broadcast_to([P, NT, n])

            def row(c, n):
                return c[:, :].rearrange("p (a e) -> p a e", a=1).broadcast_to([P, NT, n])

            tt(oh_c[:, k, :, :], row(iota_c, ST), wide(tile, ST), ALU.is_equal).then_inc(q.oh_ok, 1)
            v.wait_ge(q.oh_ok, 3 * k + 1)
            tt(oh_c[:, k, :, :], oh_c[:, k, :, :], wide(tokid, ST), ALU.mult).then_inc(q.oh_ok, 1)
            tt(oh_p[:, k, :, :], row(iota_p, P), wide(place, P), ALU.is_equal).then_inc(q.oh_ok, 1)
        v.wait_ge(q.oh_used, 1)
        nc.vector.tensor_copy(inv[:, :], bank[RB][:, 0:ST]).then_inc(q.inv_ok, 1)

        def mlp_step(kind, i, j, t1=True):
            def at(lag):
                return tile_at(kind, i, j, lag) if t1 or j < lag else None
            if at(0):
                kd, ii, jj, g = at(0)
                v.wait_ge(q.q_tp, g + 1)
                need(v, q.gu, g - 1)
                src = bank_b[QT][:, 0:D]
                if kd == "expert" and jj == MID:
                    src = src.rearrange("p (k c) -> p k c", k=KD)
                    nc.vector.tensor_copy(q_ta[:, :, 0:HALF], src[:, :, 0:HALF])
                    nc.vector.tensor_copy(q_tb[:, :, HALF:], src[:, :, HALF:]).then_inc(q.q_tc, 1)
                else:
                    nc.vector.tensor_copy(q_t[:, turned_of(kd, jj), :, :].rearrange("p k c -> p (k c)"), src).then_inc(q.q_tc, 1)
            if at(1):
                kd, ii, jj, g = at(1)
                r = ring_of(kd, jj)
                v.wait_ge(q.silu, g + 1)
                need(v, q.hq2, g - 1)
                stt(hf[:, r, :], bank[YB[jj % 2]][:, :], mst[:, jj, 2:3], g_sb[:, :], ALU.mult, ALU.mult).then_inc(q.hmul, 1)
                v.wait_ge(q.hmul, g + 1)
                need(v, q.mch, 6 * (g - 3))
                red(mst[:, jj, 1:2], hf[:, r, :], X, ALU.max, apply_absolute_value=True).then_inc(q.hmax, 1)
            if at(2):
                kd, ii, jj, g = at(2)
                r = ring_of(kd, jj)
                v.wait_ge(q.hq1, g + 1)
                need(v, q.h_tp, g - 1)
                ts(hq[:, r, :], hf[:, r, :], ROUND, None, ALU.subtract).then_inc(q.hq2, 1)
            if at(4):
                kd, ii, jj, g = at(4)
                v.wait_ge(q.dn, g + 1)
                v.wait_ge(q.mch, 6 * g + 6)
                if kd == "shared":
                    if isinstance(g, int) and g == 0:
                        v.wait_ge(q.xs_in, 16)
                    row = flat(xs[:, ds(g, 1), :])
                    stt(row, bank[DN][:, 0:D], mst[:, jj, 8:9], row, ALU.mult, ALU.add).then_inc(q.y_ok, 1)
                else:
                    need(v, y_out[jj], 16 * ii)
                    ts(ys[:, jj, :], bank[DN][:, 0:D], mst[:, jj, 8:9], None, ALU.mult).then_inc(q.y_ok, 1)

        steps(v, "shared", mlp_step)
        steps(v, "expert", mlp_step)
        for j in range(4):
            mlp_step("expert", E // 2, j, t1=False)

        for c in range(8):
            v.wait_ge(q.s_hi, c + 1)
            tt(split_dst(sw1, sw2, c // 4, c % 4, 1), raw[c % 2][:, :], split_dst(sw1, sw2, c // 4, c % 4, 0).bitcast(F32),
               ALU.subtract).then_inc(q.s_lo, 1)

        def combine(p, j):
            t = TP * p + j
            if j == 0:
                v.wait_ge(q.gath, 16 * 2 * TP * (p + 1))
            row = flat(xs[:, ds(t, 1), :])
            stt(row, gat[:, 2 * j, :], flat(wts[:, 0:1, ds(t, 1)]), row, ALU.mult, ALU.add).then_inc(q.comb, 1)
            v.wait_ge(q.comb, 2 * t + 1)
            stt(gat[:, 2 * j, :], gat[:, 2 * j + 1, :], flat(wts[:, 1:2, ds(t, 1)]), row, ALU.mult, ALU.add).then_inc(q.comb, 1)

        def x4_low(p):
            for k in range(KD):
                v.wait_ge(q.x4h, KD * p + k + 1)
                tt(x_lo[:, k, :], bank[XT[k]][:, :], x_hi[:, k, :].bitcast(F32), ALU.subtract).then_inc(q.x4l, 1)

        def net_out(p, n):
            v.wait_ge(q.l2d, 3 * KF * p + KF * (n + 1))
            if n == 0:
                need(v, q.zl, p)
                need(v, q.zh, p)
            else:
                need(v, q.f_ps, 2 * p)
            nc.vector.tensor_copy(nets[:, n, 1, :], bank[AC[1]][:, :]).then_inc(q.ne_d, 1)

        def gate_spread(p):
            v.wait_ge(q.gh_ok, p + 1)
            nc.vector.tensor_copy(gh_b[:, :, :, :].rearrange("p m b c -> p (m b) c"),
                                  gh[:, :, :].rearrange("p m (b a) -> p (m b) a", a=1).broadcast_to([P, 2 * KD, P])).then_inc(q.gt_ok, 1)

        def three(col):
            return col.broadcast_to([P, 2, 3])

        def gate_max(p):
            g0 = 12 * p
            v.wait_ge(q.g2_ps, p + 1)
            nc.vector.tensor_copy(gl[:, 0, :, :].rearrange("p b n -> p (b n)"), bank[GT][:, 8:14]).then_inc(q.gch, 1)
            v.wait_ge(q.gch, g0 + 1)
            red(gl[:, 1, :, 0], gl[:, 0, :, :], X, ALU.max).then_inc(q.gch, 1)
            v.wait_ge(q.gch, g0 + 2)
            tt(gl[:, 2, :, :], gl[:, 0, :, :], three(gl[:, 1, :, 0:1]), ALU.subtract).then_inc(q.gch, 1)

        def gate_norm(p):
            g0 = 12 * p
            v.wait_ge(q.gexp, p + 1)
            red(gl[:, 4, :, 0], gl[:, 3, :, :], X, ALU.add).then_inc(q.gch, 1)
            v.wait_ge(q.gch, g0 + 4)
            nc.vector.reciprocal(gl[:, 5, :, 0:1], gl[:, 4, :, 0:1]).then_inc(q.gch, 1)
            v.wait_ge(q.gch, g0 + 5)
            tt(gl[:, 6, :, :], gl[:, 3, :, :], three(gl[:, 5, :, 0:1]), ALU.mult).then_inc(q.gch, 1)

        def mix_nets(p, part):
            g0 = 12 * p + 6 + 2 * part
            v.wait_ge(q.ne_a, 3 * p + 3)
            v.wait_ge(q.gch, g0)
            for b in range(2):
                c = slice(b * S, (b + 1) * S)
                weight = gl[:, 6, b, (1, 0, 2)[part]:(1, 0, 2)[part] + 1]
                out = nets[:, 0, :, c]
                if part == 0:
                    ts(out, out, weight, None, ALU.mult).then_inc(q.gch, 1)
                else:
                    stt(out, nets[:, (2, 1)[part - 1], :, c], weight, out, ALU.mult, ALU.add).then_inc(q.gch, 1)

        def z_low(p):
            v.wait_ge(q.zh, p + 1)
            tt(z_lo[:, :, :], nets[:, 0, :, :], z_hi[:, :, :].bitcast(F32), ALU.subtract).then_inc(q.zl, 1)

        def fourier_out(p, h):
            v.wait_ge(q.f_ps, 2 * p + h + 1)
            v.wait_ge(q.xb, p + 1)
            rows = xs[:, ds(TP * p + 2 * h, 2), :].rearrange("p t d -> p (t d)")
            tt(rows, bank[XT[h]][:, :], rows, ALU.add).then_inc(q.f_ok, 1)

        def mix(p, prev, pre):
            for st in range(3 * KF):
                v.wait_ge(q.h4h, 3 * KF * p + st + 1)
                hi, lo = ring[st % 3]
                stt(lo[:, :], bank[HB[st % 3]][:, :], 0.0, hi[:, :].bitcast(F32), ALU.max, ALU.subtract).then_inc(q.h4l, 1)
                if st in (KF + 1, 2 * KF + 1):
                    net_out(p, st // KF - 1)
                if prev:
                    if st == 2:
                        gate_spread(p - 1)
                    if st == 4:
                        gate_max(p - 1)
                    if st == 5:
                        gate_norm(p - 1)
                        mix_nets(p - 1, 0)
                    if st in (6, 7):
                        mix_nets(p - 1, st - 5)
                    if st == 8:
                        z_low(p - 1)
                    if st in (14, 15):
                        fourier_out(p - 1, st - 14)
                if pre and 14 <= st < 14 + TP:
                    combine(p + 1, st - 14)
            if pre:
                x4_low(p + 1)
            net_out(p, 2)

        for j in range(TP):
            combine(0, j)
        x4_low(0)
        mix(0, False, True)
        with v.Fori(1, NP - 1) as p:
            mix(p, True, True)
        mix(NP - 1, True, False)
        last = NP - 1
        gate_spread(last)
        gate_max(last)
        gate_norm(last)
        for part in range(3):
            mix_nets(last, part)
        z_low(last)
        for h in range(2):
            fourier_out(last, h)

    @block.gpsimd
    def _(g):
        ts, tt, copy = nc.gpsimd.tensor_scalar, nc.gpsimd.tensor_tensor, nc.gpsimd.tensor_copy

        def hold(sem, value):
            need(g, sem, value)
            if not isinstance(value, int):
                g.sem_inc(q.pool_held, 1)

        for k, value in enumerate((-0.5, -1.0, 1.0 / 127.0, ROUND)):
            nc.gpsimd.memset(consts[:, k:k + 1], value).then_inc(q.built, 1)
        nc.gpsimd.memset(ones[:, :], 1.0).then_inc(q.built, 1)
        nc.gpsimd.memset(triu[:, :], 1.0).then_inc(q.built, 1)
        hold(q.built, 6)
        nc.gpsimd.affine_select(out=triu[:, :], in_=triu[:, :], pattern=[[1, P]], compare_op=ALU.is_ge, fill=0.0,
                                base=0, channel_multiplier=-1).then_inc(q.built, 1)
        for n, t in enumerate((id_f, id_b)):
            nc.gpsimd.memset(t[:, :], 0.0).then_inc(q.id0, 1)
            hold(q.id0, 2 * n + 1)
            nc.gpsimd.affine_select(out=t[:, :], in_=t[:, :], pattern=[[-1, P]], compare_op=ALU.not_equal, fill=1.0,
                                    base=0, channel_multiplier=1).then_inc(q.id0, 1)

        def a_split(p):
            hold(q.a_in, 32 * (p + 1))
            hold(q.low_ps, p)
            raw3 = a_raw[:, :, :, :].rearrange("p b k (a r) -> p (b k) a r", a=1).broadcast_to([P, 2 * KD, 3, R2])
            hi, lo = (t[:, :, :, :].rearrange("p b k (a r) -> p (b k) a r", a=3) for t in (a_hi, a_lo))
            copy(hi, raw3).then_inc(q.a_sp, 1)
            hold(q.a_sp, 2 * p + 1)
            tt(lo, raw3, hi.bitcast(F32), ALU.subtract).then_inc(q.a_sp, 1)

        def second_split(p):
            hold(q.e2_in, 128 * (p + 1))
            hold(q.l2_ps, TP * p)
            for b, c in enumerate((slice(0, R), slice(R2 + D, W2C))):
                copy(w2_hi[:, :, c], e2a_raw[:, b, :, :]).then_inc(q.w2_sp, 1)
                hold(q.w2_sp, 4 * p + 2 * b + 1)
                tt(w2_lo[:, :, c], e2a_raw[:, b, :, :], w2_hi[:, :, c].bitcast(F32), ALU.subtract).then_inc(q.w2_sp, 1)
            hold(q.c_ps, TP * p)
            copy(b2_st[:, :, :], b2_raw[:, :, :]).then_inc(q.b2_sp, 1)
            hold(q.b2_sp, 2 * p + 1)
            rows = slice(2 * R2, R3)
            tt(b2_st[rows, :, :], b2_raw[rows, :, :], b2_st[rows, :, :].bitcast(F32), ALU.subtract).then_inc(q.b2_sp, 1)
            hold(q.b2_sp, 2 * p + 2)

        def w_mean(n):
            hold(q.w_abs, WC * (n + 1))
            nc.gpsimd.partition_all_reduce(wsum[:, 3:6], wsum[:, 0:3], P, RADD).then_inc(q.w_m, 1)
            hold(q.w_m, 4 * n + 1)
            tt(wsum[:, 4:5], wsum[:, 3:4], wsum[:, 4:5], ALU.add).then_inc(q.w_m, 1)
            ts(wsum[:, 5:6], wsum[:, 5:6], 1.0 / (D * I), 1e-5, ALU.mult, ALU.max).then_inc(q.w_m, 1)
            hold(q.w_m, 4 * n + 2)
            ts(wsum[:, 4:5], wsum[:, 4:5], 1.0 / (2 * I * D), 1e-5, ALU.mult, ALU.max).then_inc(q.w_m, 1)

        hold(q.c_in, 16 * 11)
        a_split(0)
        hold(q.gw_in, 32)
        for k in range(KD):
            tt(gw[:, k, :], gw[:, k, :], gnorm[:, k:k + 1].broadcast_to([P, E]), ALU.mult).then_inc(q.gwok, 1)
        w_mean(0)

        def c_chain(p):
            n = CC * p
            ssq, amax, var, r, m, rm, a_, v2, r6, am, ra = (cst[:, c, :] for c in (0, 1, 2, 3, 4, 5, 6, 7, 8, 9, 10))

            def four(c):
                return c.broadcast_to([P, TP])

            hold(q.csq, TP * (p + 1))
            hold(q.camax, TP * (p + 1))
            ts(var, ssq, 1.0 / D, 1e-8, ALU.mult, ALU.add).then_inc(q.cch, 1)
            hold(q.cch, n + 1)
            tt(r, var, four(MHALF), ALU.pow).then_inc(q.cch, 1)
            hold(q.cch, n + 2)
            tt(am, amax, r, ALU.mult).then_inc(q.cch, 1)
            hold(q.cch, n + 3)
            ts(m, am, 1e-5, None, ALU.max).then_inc(q.cch, 1)
            hold(q.cch, n + 4)
            tt(rm, m, four(MONE), ALU.pow).then_inc(q.cch, 1)
            hold(q.cch, n + 5)
            tt(ra, r, rm, ALU.mult).then_inc(q.cch, 1)
            hold(q.cch, n + 6)
            ts(a_, ra, 127.0, None, ALU.mult).then_inc(q.cch, 1)
            tt(q_all[:, ds(TP * p, TP), D:D + 2].bitcast(F32), m.rearrange("p (t a) -> p t a", a=1),
               I127.rearrange("p (t a) -> p t a", a=1).broadcast_to([P, TP, 1]), ALU.mult).then_inc(q.cch, 1)
            ts(v2, ssq, 1.0 / D, 1e-6, ALU.mult, ALU.add).then_inc(q.cch, 1)
            hold(q.cch, n + 9)
            tt(r6, v2, four(MHALF), ALU.pow).then_inc(q.cch, 1)

        def feed(p, prev, pre):
            second_split(p)
            if prev:
                c_chain(p - 1)
            if pre:
                a_split(p + 1)
            w_mean(2 * p + 1)
            hold(q.cq1, TP * p)
            hold(q.lg_sb, TP * p)
            w_mean(2 * p + 2)

        feed(0, False, True)
        with g.Fori(1, NP - 1) as p:
            feed(p, True, True)
        feed(NP - 1, True, False)
        c_chain(NP - 1)

        hold(q.h_ps, KF * NP)
        hold(q.l2_ps, NT)
        for t in (q_ta, q_tb, h_ta, h_tb):
            nc.gpsimd.memset(t[:, :, :], 0.0).then_inc(q.built2, 1)
        for t, step, base, cm in ((iota_p[:, :], [[1, P]], 0, 0), (iota_c[:, :], [[1, ST]], 0, 0), (tokid[:, :], [[P, NT]], 0, 1),
                                  (rev8[:, :], [[-1, E]], E, 0), (e_off[:, :], [[CAP, E]], -1 - DUMP, 0)):
            nc.gpsimd.iota(t, pattern=step, base=base, channel_multiplier=cm, allow_small_or_imprecise_dtypes=True).then_inc(q.built2, 1)

        hold(q.w_rec, 2 * (E + 1))
        tt(wscale[:, :, 1], wscale[:, :, 1], I127.broadcast_to([P, E + 1]), ALU.mult).then_inc(q.tsc, 1)
        hold(q.tsc, 1)
        by_pair = wscale[:, 1:E + 1, :].rearrange("p (i h) c -> p i h c", h=2)
        tiles = tscale[:, :, :].rearrange("p (i j) c -> p i j c", j=TE)
        for rows, h, js in ((slice(0, P), 0, slice(0, MID)), (slice(0, P), 1, slice(MID + 1, TE)),
                            (slice(0, HALF), 0, slice(MID, MID + 1)), (slice(HALF, P), 1, slice(MID, MID + 1))):
            n = js.stop - js.start
            if rows.start:
                hold(q.tsc, 4)
            copy(tiles[rows, :, js, :], by_pair[rows, :, h:h + 1, :].broadcast_to([rows.stop - rows.start, E // 2, n, 2])).then_inc(q.tsc, 1)
        hold(q.tsc, 5)

        def gather(k):
            for t in range(TE * k, TE * (k + 1)):
                g.indirect_dma_start(xg[:, t, :].bitcast(U32), None, q_d, bass.IndirectOffsetOnAxis(ap=inv[:, t:t + 1], axis=0)).then_inc(g_in[k], 16)

        def here(k):
            hold(g_in[k], 16 * TE)
            g.sem_inc(q.rows_in, 1)

        def scale_of(kd, jj, g_, c):
            if kd == "shared":
                return wscale[:, 0, c:c + 1]
            return flat(tscale[:, ds(g_ - NT, 1), c:c + 1])

        def mlp_step(kind, i, j, t1=True):
            if kind == "shared" and isinstance(i, int) and i == 0:
                if j == 0:
                    hold(q.tsc, 5)
                if j in (0, 2):
                    hold(q.inv_ok, 1)
                    hold(q.rows_ok, 1)
                    gather(j // 2)
            if kind == "expert":
                if isinstance(i, int) and i == 0:
                    if j == 0:
                        here(0)
                        gather(2)
                    if j == 2:
                        here(1)
                        gather(3)
                    if j == TE - 1:
                        here(2)
                        here(3)
            if t1:
                kd, ii, jj, t = tile_at(kind, i, j, 0)
                hold(q.hmul, t - 3)
                rows = q_all[:, ds(t, 1), D:D + 2] if kd == "shared" else xg[:, ds(t - NT, 1), D:D + 2]
                tt(mst[:, jj, 2:3], flat(rows).bitcast(F32), scale_of(kd, jj, t, 0), ALU.mult).then_inc(q.msg, 1)
            if t1 or j < 1:
                back = tile_at(kind, i, j, 1)
                if back:
                    kd, ii, jj, t = back
                    ssq, amax, var, r, m, rm, a_, od = (mst[:, jj, c:c + 1] for c in (0, 1, 3, 4, 5, 7, 6, 8))
                    n = 6 * t
                    hold(q.hsq, t + 1)
                    hold(q.hmax, t + 1)
                    ts(var, ssq, 1.0 / I, 1e-8, ALU.mult, ALU.add).then_inc(q.mch, 1)
                    hold(q.mch, n + 1)
                    tt(r, var, MHALF, ALU.pow).then_inc(q.mch, 1)
                    hold(q.mch, n + 2)
                    ts(m, amax, r, 1e-5, ALU.mult, ALU.max).then_inc(q.mch, 1)
                    hold(q.mch, n + 3)
                    tt(rm, m, MONE, ALU.pow).then_inc(q.mch, 1)
                    hold(q.mch, n + 4)
                    hold(q.hq1, t - 3)
                    ts(a_, r, rm, 127.0, ALU.mult, ALU.mult).then_inc(q.mch, 1)
                    hold(q.y_ok, t - 3)
                    tt(od, m, scale_of(kd, jj, t, 1), ALU.mult).then_inc(q.mch, 1)

        steps(g, "shared", mlp_step)
        steps(g, "expert", mlp_step)
        mlp_step("expert", E // 2, 0, t1=False)

        def gather_rows(p):
            hold(q.xt_ps, KD * p)
            copy(gidx[:, :].rearrange("p (j k) -> p k j", k=2), slots[:, :, ds(TP * p, TP)]).then_inc(q.gix, 1)
            hold(q.gix, p + 1)
            for n in range(2 * TP):
                g.indirect_dma_start(gat[:, n, :], None, y_d, bass.IndirectOffsetOnAxis(ap=gidx[:, n:n + 1], axis=0)).then_inc(q.gath, 16)

        def add_bias(p):
            hold(q.comb, 2 * TP * (p + 1))
            even = gat[:, :, :].rearrange("p (j k) d -> p j k d", k=2)[:, :, 0, :]
            tt(xs[:, ds(TP * p, TP), :], even, bias_b[:, :].rearrange("p (a d) -> p a d", a=1).broadcast_to([P, TP, D]),
               ALU.add).then_inc(q.xb, 1)

        def type_split(p):
            for c in range(8):
                hi, lo = (split_dst(tw1, tw2, c // 4, c % 4, k) for k in range(2))
                hold(q.thi, 8 * p + c + 1)
                tt(lo, raw[c % 2][:, :], hi.bitcast(F32), ALU.subtract).then_inc(q.tsp, 1)

        hold(q.y_ok, NT + ST)
        for k in range(TE):
            hold(y_out[k], 16 * (E // 2))
        gather_rows(0)
        type_split(0)
        hold(q.g1_in, 48)
        add_bias(0)
        gather_rows(1)
        with g.Fori(1, NP - 1) as p:
            type_split(p)
            add_bias(p)
            gather_rows(p + 1)
        type_split(NP - 1)
        add_bias(NP - 1)


def kernel(**inputs):
    import numpy as np
    import concourse.bacc as bacc
    from concourse.bass_utils import run_bass_kernel_spmd

    def x_of(name):
        return np.asarray(inputs[name])

    def rows(w, k):
        return np.swapaxes(w.reshape(*w.shape[:-2], k, P, w.shape[-1]), -3, -2)

    def turn(w):
        return np.swapaxes(w, -1, -2)

    x = x_of("x").reshape(N, D)
    c, t = "L0_cond_", "L0_attn_"
    n = np.arange(D)
    angle = 2.0 * np.pi * (np.outer(n, n) % D) / D
    dft = np.stack([np.cos(angle), np.sin(angle), -np.sin(angle)]).astype(np.float32)
    gates = np.concatenate([x_of(t + "shared_gate_w")[None], x_of(t + "expert_gate_w")])
    downs = np.concatenate([x_of(t + "shared_down_w")[None], x_of(t + "expert_down_w")])
    arrays = {
        "x": x, "xT": rows(x.T, KD),
        "w1T": rows(turn(x_of(c + "wi")), KD), "w2T": rows(turn(x_of(c + "wo")), KF),
        "ca1": rows(turn(x_of(c + "common_wi_a")), KD), "cb1": turn(x_of(c + "common_wi_b")),
        "ca2": rows(turn(x_of(c + "common_wo_a")), KF), "cb2": turn(x_of(c + "common_wo_b")),
        "ea1": rows(turn(x_of(c + "experts_wi_a")), KD), "eb1": turn(x_of(c + "experts_wi_b")),
        "ea2": rows(turn(x_of(c + "experts_wo_a")), KF), "eb2": turn(x_of(c + "experts_wo_b")),
        "gate_wT": rows(turn(x_of(t + "gate_w")), KD), "gnorm": x_of(t + "gate_norm_w").reshape(KD, P).T,
        "gT": rows(turn(gates), KD), "dT": rows(turn(downs), KI),
        "ids": x_of("itok_B_0_7").reshape(1, B), "types": x_of("itok_B_0_2").reshape(1, B),
        "wi": rows(x_of("L0_cond2_wi"), KD), "wo": rows(x_of("L0_cond2_wo"), KF),
        "swi": rows(x_of("L0_cond2_swi"), KD), "swo": rows(x_of("L0_cond2_swo"), KF),
        "g1": rows(x_of("L0_cond2_g1"), 3 * KD), "g2": rows(x_of("L0_cond2_g2"), KD),
        "fr": rows(x_of("L0_ffn_w_freq_real"), KD), "fi": rows(x_of("L0_ffn_w_freq_imag"), KD),
        "dft": np.swapaxes(rows(dft, KD), 0, 1), "bias": x_of("L0_ffn_bias").reshape(1, D),
    }
    nc = bacc.Bacc("TRN2", target_bir_lowering=False, num_devices=1)
    data, a = {}, {}
    for name, v in arrays.items():
        v = np.ascontiguousarray(v)
        data["in_" + name] = v
        a[name] = nc.dram_tensor("in_" + name, v.shape, mybir.dt.from_np(v.dtype), kind="ExternalInput").ap()
    a["out"] = nc.dram_tensor("out", (N, D), F32, kind="ExternalOutput").ap()
    build(nc, a)
    r = run_bass_kernel_spmd(nc, [data], core_ids=[0])
    return r.results[0]["out"].reshape(B, S, D)
```

```python
import math
from contextlib import ExitStack
from collections import namedtuple

import concourse.bass as bass
from concourse import mybir

F32 = mybir.dt.float32
F32R = mybir.dt.float32r
BF16 = mybir.dt.bfloat16
F16 = mybir.dt.float16
U32 = mybir.dt.uint32
ALU = mybir.AluOpType
ACT = mybir.ActivationFunctionType
X = mybir.AxisListType.X
RADD = bass.bass_isa.ReduceOp.add
ds = bass.ds

P = 128
B, S, D = 8, 256, 256
N = B * S
F = 1024
KD, KF = D // P, F // P
PR = 2 * S
NP = N // PR
TP = PR // P
NT = N // P
R = 16
R2 = 2 * R
R3 = 3 * R2
E = 8
I = 512
KI = I // P
CAP = int(N / E * 1.25)
NS = E * CAP
ST = NS // P
TE = 2 * CAP // P
MID = TE // 2
HALF = CAP - MID * P
QW = D + 2
GW = KD * 2 * I
DW = KI * D
WC = (GW + DW) // F
CC = 10
W2C = 3 * R + D
ROUND = 1.5 * 2.0 ** 23
DUMP = NS


def need(eng, sem, value):
    if not (isinstance(value, int) and value <= 0):
        eng.wait_ge(sem, value)


def build(nc, a):
    ctx = ExitStack()
    with ctx:
        _program(nc, a, ctx)


def _program(nc, a, ctx):
    base = -(-nc.sbuf_base // 32) * 32

    class Area:
        def __init__(self, at):
            self.at = at

        def put(self, name, shape, dt):
            size = math.prod(shape[1:]) * mybir.dt.size(dt)
            t = nc.alloc_sbuf_tensor_at(name, shape, dt, offset=self.at)
            self.at += -(-size // 32) * 32
            return t

    keep = Area(base)
    xs = keep.put("xs", [P, NT, D], F32)
    x_hi = keep.put("x_hi", [P, KD, PR], F32R)
    x_lo = keep.put("x_lo", [P, KD, PR], F32R)
    id_f = keep.put("id_f", [P, P], F32)
    id_b = keep.put("id_b", [P, P], BF16)
    wts = keep.put("wts", [P, 2, NT], F32)
    slots = keep.put("slots", [P, 2, NT], U32)
    m_hi = keep.put("m_hi", [P, KD, D], F32R)
    m_lo = keep.put("m_lo", [P, KD, D], F32R)
    consts = keep.put("consts", [P, 4], F32)
    MHALF, MONE, I127, RND = (consts[:, k:k + 1] for k in range(4))

    r1 = Area(keep.at)
    w1_hi = r1.put("w1_hi", [P, KD, F], F32R)
    w1_lo = r1.put("w1_lo", [P, KD, F], F32R)
    w2_hi = r1.put("w2_hi", [P, KF, W2C], F32R)
    w2_lo = r1.put("w2_lo", [P, KF, W2C], F32R)
    h_hi = r1.put("h_hi", [P, KF, PR], F32R)
    h_lo = r1.put("h_lo", [P, KF, PR], F32R)
    r1b = Area(keep.at)
    sw = r1b.put("sw", [P, 4, 2, 2, F], F32R)
    sw1 = [[sw[:, 2 * n, q, :, :] for q in range(2)] for n in range(2)]
    sw2 = [[sw[:, 2 * n + 1, q, :, :].rearrange("p h (k d) -> p (h k) d", d=D) for q in range(2)] for n in range(2)]

    r2 = Area(max(r1.at, r1b.at + 2 * PR * 4))
    r2_at = r2.at
    wq = r2.put("wq", [P, E, GW + DW], BF16)
    w_raw = r2.put("w_raw", [P, GW + DW], F32)
    per = (GW + DW) * 2
    s_a = Area(r2_at + 2 * per)
    w1_raw = s_a.put("w1_raw", [P, KD, F], F32)
    w2_raw = s_a.put("w2_raw", [P, KF, R + D], F32)
    assert s_a.at <= r2_at + 5 * per
    r2b = Area(r2_at)
    tw1, tw2 = [], []
    for n in range(2):
        tw1.append([r2b.put(f"tw1_{q}{n}", [P, KD, F], F32R) for q in ("hi", "lo")])
        tw2.append([r2b.put(f"tw2_{q}{n}", [P, KF, D], F32R) for q in ("hi", "lo")])

    r3 = Area(r2.at)
    q_all = r3.put("q_all", [P, NT, QW], BF16)
    wq_s = r3.put("wq_s", [P, GW + DW], BF16)
    logits = r3.put("logits", [P, NT, E], F32)
    gw = r3.put("gw", [P, KD, E], F32)
    gnorm = r3.put("gnorm", [P, KD], F32)
    wsum = r3.put("wsum", [P, 8], F32)
    wscale = r3.put("wscale", [P, E + 1, 2], F32)
    wrec = r3.put("wrec", [P, 2], F32)
    tscale = r3.put("tscale", [P, ST, 2], F32)
    triu = r3.put("triu", [P, P], BF16)
    ones = r3.put("ones", [P, P], BF16)
    rinv = r3.put("rinv", [P, NT], F32)
    r3_at = r3.at
    x_raw = r3.put("x_raw", [P, KD, PR], F32)
    a_raw = r3.put("a_raw", [P, 2, KD, R2], F32)
    a_hi = r3.put("a_hi", [P, 2, KD, R3], F32R)
    a_lo = r3.put("a_lo", [P, 2, KD, R3], F32R)
    b_raw = r3.put("b_raw", [R3, F], F32)
    b_st = r3.put("b_st", [R3, 2, F], F32R)
    e2a_raw = r3.put("e2a_raw", [P, 2, KF, R], F32)
    b2_raw = r3.put("b2_raw", [R3, 2, D], F32)
    b2_st = r3.put("b2_st", [R3, 2, D], F32R)
    low = r3.put("low", [R3, PR], F32R)
    low2 = r3.put("low2", [P, 3, R2], F32)
    low2t = r3.put("low2t", [R3, P], F32R)
    c_sb = r3.put("c_sb", [P, TP, D], F32)
    c_tmp = r3.put("c_tmp", [P, D], F32)
    c_t = r3.put("c_t", [P, KD, P], F32)
    cst = r3.put("cst", [P, 12, TP], F32)
    c_junk = r3.put("c_junk", [P, D], BF16)
    end1 = r3.at
    rr = Area(keep.at)
    rt = [rr.put(f"rt{k}", [P, NT, E], F32) for k in range(8)]
    cum = [rr.put(f"cum{k}", [P, NT + 1, E], F32) for k in range(2)]
    sel_b = rr.put("sel_b", [P, NT, E], BF16)
    c16 = [rr.put(f"c16_{k}", [P, NT], F32) for k in range(10)]
    rev8 = rr.put("rev8", [P, E], F32)
    e_off = rr.put("e_off", [P, E], F32)
    iota_p = rr.put("iota_p", [P, P], F32)
    iota_c = rr.put("iota_c", [P, ST], F32)
    tokid = rr.put("tokid", [P, NT], F32)
    oh_p = rr.put("oh_p", [P, 2, NT, P], F16)
    oh_c = rr.put("oh_c", [P, 2, NT, ST], F16)
    inv = rr.put("inv", [P, ST], U32)
    fr = rr.put("fr", [P, KD, D], F32)
    fi = rr.put("fi", [P, KD, D], F32)
    dft = rr.put("dft", [P, 3, KD, D], F32)
    a_re = rr.put("a_re", [P, KD, D], F32)
    a_im = rr.put("a_im", [P, KD, D], F32)
    assert rr.at <= keep.at + 3 * 16384
    rr = Area(keep.at + 3 * 16384)
    xg = rr.put("xg", [P, ST, QW], BF16)
    ys = rr.put("ys", [P, TE, D], F32)
    r3 = Area(r3_at)
    q_t = r3.put("q_t", [P, 2, KD, P], BF16)
    q_ta = r3.put("q_ta", [P, KD, P], BF16)
    q_tb = r3.put("q_tb", [P, KD, P], BF16)
    g_sb = r3.put("g_sb", [P, I], F32)
    hf = r3.put("hf", [P, TE, I], F32)
    hq = r3.put("hq", [P, TE, I], BF16)
    h_t = r3.put("h_t", [P, KI, P], BF16)
    h_ta = r3.put("h_ta", [P, KI, P], BF16)
    h_tb = r3.put("h_tb", [P, KI, P], BF16)
    mst = r3.put("mst", [P, TE, 12], F32)
    m_junk = r3.put("m_junk", [P, I], BF16)
    top = Area(nc.sbuf_usable_end // 32 * 32 - 2 * 4096)
    assert r3.at <= top.at
    raw = [top.put(f"raw{k}", [P, F], F32) for k in range(2)]
    end3 = r3.at
    r4 = Area(r2b.at)
    gat = r4.put("gat", [P, 2 * TP, D], F32)
    nets = r4.put("nets", [P, 3, KD, PR], F32)
    z_hi = Area(r4.at - 2 * KD * PR * 4).put("z_hi", [P, KD, PR], F32R)
    z_lo = Area(r4.at - KD * PR * 4).put("z_lo", [P, KD, PR], F32R)
    spare = Area(r1b.at)
    ring = [(r4.put(f"ring_hi{k}", [P, PR], F32R), r4.put(f"ring_lo{k}", [P, PR], F32R)) for k in range(2)]
    ring.append((spare.put("ring_hi2", [P, PR], F32R), spare.put("ring_lo2", [P, PR], F32R)))
    assert spare.at <= r2_at
    g1_sb = r4.put("g1_sb", [P, 3 * KD, D], F32)
    g2_sb = r4.put("g2_sb", [P, KD, 3], F32)
    bias_b = r4.put("bias_b", [P, D], F32)
    gidx = r4.put("gidx", [P, 2 * TP], U32)
    gh = r4.put("gh", [P, KD, 2], F32)
    gh_b = r4.put("gh_b", [P, KD, 2, P], F32)
    gl = r4.put("gl", [P, 8, 2, 3], F32)
    assert r4.at <= top.at

    bank = [ctx.enter_context(nc.psum_tensor(f"bank{k}", [P, 512], F32)) for k in range(8)]
    bank_b = [b[:, :].bitcast(BF16) for b in bank]

    def scratch(name, shape, dt):
        return nc.dram_tensor(name, shape, dt, kind="Internal").ap()

    q_d = scratch("q_d", (N, QW // 2), U32)
    y_d = scratch("y_d", (NS + 1, D), F32)

    def sem(name):
        return ctx.enter_context(nc.semaphore(name))

    names = """x_in a_in b_in e2_in c_in ca_in cb_in m_in w1_in w2_in gw_in xs_in q_out zrow built id0 gwok xh xl w1h
        w1l w2h w2l m1 m1e m2 mh ml a_sp b_sp w2_sp b2_sp w_abs w_m w_rec w_rnd w_clip w_out low_ps lowh lowl
        h_ps hh hl l2_ps low2s low2t_ps low2h low2l c_ps c_done csq camax cch cq1 cq2 ct_ps ct_sb lg_ps lg_sb
        route r_sub r_exp cnt_rd r_ps r_inv oh_ok oh_used built2 tsc rows_ok q_tp q_tc gu msg silu hmul hsq hmax
        mch hq1 hq2 h_tp h_tc dn y_ok s_hi s_lo gix comb xb rows_in xt_ps x4h x4l hp inv_ok h4h h4l l2d ne_a
        ne_d thi tsp g1_ps gh_ok gt_ok g2_ps gch gexp pool_held sync_held zh zl f_ps f_ok o_out g1_in""".split()
    q = namedtuple("Signals", names)(*[sem(n) for n in names])
    w_in = [sem(f"w_in{k}") for k in range(WC)]
    g_in = [sem(f"g_in{k}") for k in range(E // 2)]
    y_out = [sem(f"y_out{k}") for k in range(TE)]
    gath = [sem(f"gath{k}") for k in range(TP)]
    s_in = [sem(f"s_in{k}") for k in range(2)]
    t_in = [sem(f"t_in{k}") for k in range(2)]



    HB = (0, 1, 2)
    OB = (3, 4, 5, 2)
    LT, CT, LG, LOW = 6, 7, 6, 7
    QT, GB, YB, HT, DN, RB = 7, (0, 2), (1, 3), 4, 5, 6
    AC, GT, XT = (4, 5), 3, (6, 7)

    block = ctx.enter_context(nc.Block())

    def hlh(w, x):
        return ((w[0], x[0]), (w[0], x[1]), (w[1], x[0]))

    COLS = ((0, slice(2 * R, 2 * R + D), slice(0, R), slice(R, 2 * R)),
            (R, slice(R, R + D), slice(R + D, 2 * R + D), slice(0, R)))
    UP = 2 * R + D

    def turned_of(kind, j):
        return j % 2 if kind == "shared" or j < MID else (j - MID - 1) % 2

    SECTION = {"shared": (0, TP, NP), "expert": (NT, TE, E // 2)}

    def tile_at(kind, i, j, lag):
        first, n, _ = SECTION[kind]
        back, jj = divmod(j - lag, n)
        if isinstance(i, int) and i + back < 0:
            if kind == "shared":
                return None
            return tile_at("shared", NP, j - lag + n * i, 0)
        return kind, i + back, jj, n * (i + back) + (jj + first)

    def steps(eng, kind, step):
        _, n, count = SECTION[kind]
        apart = 2 if kind == "shared" else 1
        for i in range(apart):
            for j in range(n):
                step(kind, i, j)
        with eng.Fori(apart, count) as i:
            for j in range(n):
                step(kind, i, j)

    def flat(ap):
        return ap.rearrange("p a c -> p (a c)")

    def w_dst(n):
        if isinstance(n, int) and n == 0:
            return wq_s[:, :]
        return flat(wq[:, ds(n - 1, 1), :])

    def split_dst(w1, w2, n, part, which):
        if part < 2:
            return w1[n][which][:, part, :]
        return w2[n][which][:, 4 * (part - 2):4 * (part - 2) + 4, :].rearrange("p k d -> p (k d)")

    @block.sync
    def _(sp):
        def lora_loads(p, part, half=0):
            for b in ((half,) if part == "b" else (0, 1)):
                sp.sem_inc(q.sync_held, 1)
                e = sp.value_load(a["ids"][0:1, ds(2 * p + b, 1)], min_val=0, max_val=E - 1)
                if part == "a":
                    sp.dma_start(a_raw[:, b, :, 0:R], a["ea1"][ds(e, 1)].rearrange("e p k r -> (e p) k r")).then_inc(q.a_in, 16)
                if part == "b":
                    for k in range(3):
                        sp.dma_start(b_raw[k * R2:k * R2 + R, :], a["eb1"][ds(e, 1)].rearrange("e r f -> (e r) f")).then_inc(q.b_in, 16)
                if part == "2":
                    sp.dma_start(e2a_raw[:, b, :, :], a["ea2"][ds(e, 1)].rearrange("e p k r -> (e p) k r")).then_inc(q.e2_in, 16)
                    for k in range(3):
                        sp.dma_start(b2_raw[k * R2:k * R2 + R, b, :], a["eb2"][ds(e, 1)].rearrange("e r d -> (e r) d")).then_inc(q.e2_in, 16)

        def w_load(n):
            for c in range(WC):
                need(sp, q.w_out, WC * (n - 1) + c + 1)
                src = a["gT"][ds(n, 1), :, c, :].rearrange("e p f -> (e p) f") if c < KD else a["dT"][ds(n, 1)].rearrange("e p k f -> (e p) (k f)")
                sp.dma_start(w_raw[:, c * F:(c + 1) * F], src).then_inc(w_in[c], 16)

        def x_load(p):
            sp.dma_start(x_raw[:, :, :], a["xT"][:, :, ds(p * PR, PR)]).then_inc(q.x_in, 16)

        x_load(0)
        for b in range(2):
            sp.dma_start(a_raw[:, b, :, R:R2], a["ca1"]).then_inc(q.ca_in, 16)
        lora_loads(0, "a")
        for k in range(3):
            sp.dma_start(b_raw[k * R2 + R:(k + 1) * R2, :], a["cb1"]).then_inc(q.c_in, 16)
        lora_loads(0, "b", 0)
        sp.wait_ge(q.b_sp, 2)
        lora_loads(0, "b", 1)
        for k in range(3):
            for b in range(2):
                sp.dma_start(b2_raw[k * R2 + R:(k + 1) * R2, b, :], a["cb2"]).then_inc(q.cb_in, 16)
        lora_loads(0, "2")
        w_load(0)
        sp.dma_start(gw[:, :, :], a["gate_wT"]).then_inc(q.gw_in, 16)
        sp.dma_start(gnorm[:, :], a["gnorm"]).then_inc(q.gw_in, 16)

        def q_store(p):
            sp.wait_ge(q.cq2, TP * p + TP)
            sp.sem_inc(q.sync_held, 1)
            sp.wait_ge(q.cch, CC * p + 8)
            sp.dma_start(q_d[ds(p * PR, PR), :].rearrange("(t p) c -> p t c", p=P), q_all[:, ds(p * TP, TP), :].bitcast(U32)).then_inc(q.q_out, 16)

        def feed(p, prev, pre):
            if prev:
                w_load(2 * p)
            if pre:
                sp.wait_ge(q.xl, p + 1)
                x_load(p + 1)
                sp.wait_ge(q.a_sp, 2 * p + 2)
                lora_loads(p + 1, "a")
                sp.wait_ge(q.b_sp, 4 * p + 4)
                lora_loads(p + 1, "b", 0)
                sp.wait_ge(q.w2_sp, 4 * p + 4)
                sp.wait_ge(q.b2_sp, 2 * p + 2)
                lora_loads(p + 1, "2")
            w_load(2 * p + 1)
            if pre:
                sp.wait_ge(q.b_sp, 4 * p + 6)
                lora_loads(p + 1, "b", 1)
            if prev:
                q_store(p - 1)

        feed(0, False, True)
        sp.dma_start(xs[:, :, :], a["x"].rearrange("(t p) d -> p t d", p=P)).then_inc(q.xs_in, 16)
        with sp.Fori(1, NP - 1) as p:
            feed(p, True, True)
        feed(NP - 1, True, False)
        sp.wait_ge(q.l2_ps, NT)
        for t, n in ((fr, "fr"), (fi, "fi"), (dft, "dft")):
            sp.dma_start(t[:, :], a[n]).then_inc(q.m_in, 16)
        w_load(E)
        q_store(NP - 1)
        sp.wait_ge(q.q_out, 16 * NP)

        sp.wait_ge(q.built2, 2)
        sp.dma_start(y_d[DUMP:DUMP + 1, :].rearrange("a (b c) -> (a b) c", b=2), q_ta[0:2, :, :].rearrange("p k c -> p (k c)").bitcast(F32)).then_inc(q.zrow, 16)
        sp.wait_ge(q.zrow, 16)
        sp.sem_inc(q.rows_ok, 1)

        def s_load(m, k):
            need(sp, q.s_lo, 2 * (m - 1) + k + 1)
            sp.dma_start(raw[k][:, :], a["sw"][ds(m, 1), k].rearrange("a p f -> (a p) f")).then_inc(s_in[k], 16)

        def y_store(kind, i, j):
            t = tile_at(kind, i, j, 0)
            sp.wait_ge(q.y_ok, t[3] + 1)
            sp.dma_start(y_d[ds(P * (t[3] - NT), P), :], ys[:, j, :]).then_inc(y_out[j], 16)

        sp.wait_ge(q.lg_sb, NT)
        s_load(0, 0)
        s_load(0, 1)
        for j in range(TE):
            sp.sem_inc(y_out[j], 1)
        for j in range(TE):
            y_store("expert", 0, j)
        with sp.Fori(1, E // 2) as i:
            for j in range(TE):
                y_store("expert", i, j)
                if j == 0:
                    s_load(i, 0)
                    s_load(i, 1)
        sp.dma_start(g1_sb[:, :, :], a["g1"]).then_inc(q.g1_in, 16)
        sp.dma_start(g2_sb[:, :, :], a["g2"]).then_inc(q.g1_in, 16)
        sp.dma_start(bias_b[:, :], a["bias"].partition_broadcast(P)).then_inc(q.g1_in, 16)

        def types(p):
            for b in range(2):
                sp.sem_inc(q.sync_held, 1)
                v = sp.value_load(a["types"][0:1, ds(2 * p + b, 1)], min_val=0, max_val=4)
                for m in range(4):
                    c = 4 * b + m
                    if c >= 2:
                        need(sp, q.tsp, 8 * p + c - 1)
                    elif isinstance(p, int) and p == 0:
                        sp.wait_ge(q.s_lo, 7 + c)
                    else:
                        sp.wait_ge(q.tsp, 8 * p + c - 1)
                    if m < 2:
                        src = a["wi"][ds(v, 1), :, m, :].rearrange("e p f -> (e p) f")
                    else:
                        src = a["wo"][ds(v, 1), :, 4 * (m - 2):4 * (m - 2) + 4, :].rearrange("e p k d -> (e p) (k d)")
                    sp.dma_start(raw[c % 2][:, :], src).then_inc(t_in[c % 2], 16)

        def store(p):
            for h in range(2):
                sp.wait_ge(q.f_ok, 2 * p + h + 1)
                sp.dma_start(a["out"][ds(p * PR + h * S, S), :].rearrange("(t p) d -> p t d", p=P), xs[:, ds(p * TP + 2 * h, 2), :]).then_inc(q.o_out, 16)

        types(0)
        with sp.Fori(1, NP) as p:
            types(p)
            store(p - 1)
        store(NP - 1)
        sp.wait_ge(q.o_out, 2 * 16 * NP)

    @block.tensor
    def _(pe):
        mm = nc.tensor.matmul

        def low_rank(p):
            pe.wait_ge(q.xl, p + 1)
            pe.wait_ge(q.a_sp, 2 * p + 2)
            for b in range(2):
                seq = [(w, x, k) for k in range(KD) for w, x in hlh((a_hi, a_lo), (x_hi, x_lo))]
                for n, (w, x, k) in enumerate(seq):
                    last = mm(bank[LOW][0:R3, b * S:(b + 1) * S], w[:, b, k, :], x[:, k, b * S:(b + 1) * S],
                              start=n == 0, stop=n == len(seq) - 1)
            last.then_inc(q.low_ps, 1)

        def turn_c(p, j):
            t = TP * p + j
            pe.wait_ge(q.c_done, t + 1)
            if j == 0:
                need(pe, q.lowl, p + 1)
            if j:
                pe.wait_ge(q.ct_sb, t)
            for k in range(KD):
                last = nc.tensor.transpose(bank[CT][:, k * P:(k + 1) * P], c_sb[:, j, k * P:(k + 1) * P], id_f[:, :])
            last.then_inc(q.ct_ps, 1)

        def router(p, j):
            t = TP * p + j
            pe.wait_ge(q.ct_sb, t + 1)
            if j:
                pe.wait_ge(q.lg_sb, t)
            pe.wait_ge(q.low2l, TP * p + TP)
            for k in range(KD):
                last = mm(bank[LG][:, 0:E], c_t[:, k, :], gw[:, k, :], start=k == 0, stop=k == KD - 1)
            last.then_inc(q.lg_ps, 1)

        def turn_low(p, j):
            pe.wait_ge(q.low2s, 2 * (TP * p + j + 1))
            need(pe, q.low2l, TP * p + j)
            if j == 0:
                need(pe, q.lg_sb, TP * p)
            nc.tensor.transpose(bank[LT][0:R3, 0:P], low2[:, :, :].rearrange("p a b -> p (a b)"), id_f[:, :]).then_inc(q.low2t_ps, 1)

        def finish(p, j):
            pe.wait_ge(q.low2l, TP * p + j + 1)
            mm(bank[OB[j]][:, COLS[j // 2][1]], low2t[:, :], b2_st[:, j // 2, :],
               start=False, stop=True, skip_group_check=True).then_inc(q.c_ps, 1)

        def feed(p, prev, pre):
            for f in range(KF):
                if f == 0:
                    pe.wait_ge(q.lowl, p + 1)
                    pe.wait_ge(q.b_sp, 4 * p + 4)
                need(pe, q.hl, KF * p + f - 2)
                if prev and f == 2:
                    pe.wait_ge(q.c_done, TP * p)
                fs = slice(f * P, (f + 1) * P)
                seq = [(w, x, k) for k in range(KD) for w, x in hlh((w1_hi, w1_lo), (x_hi, x_lo))]
                for n, (w, x, k) in enumerate(seq):
                    mm(bank[HB[f % 3]][:, :], w[:, k, fs], x[:, k, :], start=n == 0, stop=False, skip_group_check=True)
                for b in range(2):
                    last = mm(bank[HB[f % 3]][:, b * S:(b + 1) * S], b_st[:, b, fs], low[:, b * S:(b + 1) * S],
                              start=False, stop=b == 1, skip_group_check=True)
                last.then_inc(q.h_ps, 1)
                if prev:
                    if f == 0:
                        finish(p - 1, 2)
                        turn_low(p - 1, 3)
                    if f == 1:
                        finish(p - 1, 3)
                    if 2 <= f < 2 + TP:
                        turn_c(p - 1, f - 2)
                    if 3 <= f < 3 + TP:
                        router(p - 1, f - 3)

            def down(j):
                c0 = COLS[j // 2][0]
                need(pe, q.c_done, TP * p)
                for f in range(KF):
                    if j == 0:
                        pe.wait_ge(q.hl, KF * p + f + 1)
                    for n, (h, w) in enumerate(((h_hi, w2_hi), (h_hi, w2_lo), (h_lo, w2_hi))):
                        last = mm(bank[OB[j]][:, 0:UP], h[:, f, j * P:(j + 1) * P], w[:, f, c0:c0 + UP],
                                  start=f == 0 and n == 0, stop=False, skip_group_check=True)
                last.then_inc(q.l2_ps, 1)

            pe.wait_ge(q.w2_sp, 4 * p + 4)
            pe.wait_ge(q.b2_sp, 2 * p + 2)
            if isinstance(p, int) and p == 0:
                pe.wait_ge(q.w2l, 1)
            down(0)
            down(1)
            turn_low(p, 0)
            need(pe, q.ct_sb, TP * p)
            if pre:
                low_rank(p + 1)
            down(2)
            finish(p, 0)
            turn_low(p, 1)
            down(3)
            finish(p, 1)
            turn_low(p, 2)

        low_rank(0)
        pe.wait_ge(q.w1l, 1)
        pe.wait_ge(q.id0, 4)
        feed(0, False, True)
        pe.wait_ge(q.gwok, 2)
        with pe.Fori(1, NP - 1) as p:
            feed(p, True, True)
        feed(NP - 1, True, False)
        finish(NP - 1, 2)
        turn_low(NP - 1, 3)
        finish(NP - 1, 3)
        for j in range(TP + 1):
            if j < TP:
                turn_c(NP - 1, j)
            if j:
                router(NP - 1, j - 1)

        pe.wait_ge(q.m_in, 48)
        for o in range(KD):
            for out_bank, terms in ((0, ((fr, 0), (fi, 1))), (1, ((fi, 0), (fr, 2)))):
                seq = [(w, t, k) for w, t in terms for k in range(KD)]
                for n, (w, t, k) in enumerate(seq):
                    last = mm(bank[out_bank][:, o * D:(o + 1) * D], w[:, k, o * P:(o + 1) * P], dft[:, t, k, :],
                              start=n == 0, stop=n == len(seq) - 1)
        last.then_inc(q.m1, 1)

        pe.wait_ge(q.r_ps, 1)
        sel = sel_b[:, :, :].rearrange("p t e -> p (t e)")
        mm(bank[RB][:, 0:NT * E], triu[:, :], sel, start=True, stop=True)
        mm(bank[RB][:, NT * E:2 * NT * E], ones[:, :], sel, start=True, stop=True).then_inc(q.r_inv, 1)
        pe.wait_ge(q.m1e, 2)
        for m in range(KD):
            seq = [(w, t, k) for w, t in ((a_re, 0), (a_im, 2)) for k in range(KD)]
            for n, (w, t, k) in enumerate(seq):
                last = mm(bank[2][:, m * D:(m + 1) * D], w[:, k, m * P:(m + 1) * P], dft[:, t, k, :],
                          start=n == 0, stop=n == len(seq) - 1)
        last.then_inc(q.m2, 1)

        pe.wait_ge(q.cnt_rd, 1)
        for k in range(2):
            pe.wait_ge(q.oh_ok, 3 * (k + 1))
            for t in range(NT):
                last = mm(bank[RB][:, 0:ST], oh_p[:, k, t, :], oh_c[:, k, t, :], start=k == 0 and t == 0, stop=k == 1 and t == NT - 1)
        last.then_inc(q.oh_used, 1)

        def rows_of(kind, i, j, c):
            if kind == "shared":
                return q_all[:, ds(TP * i + j, 1), c].rearrange("p a c -> p (a c)")
            return xg[:, ds(TE * i + j, 1), c].rearrange("p a c -> p (a c)")

        def weights(kind, i, j):
            if kind == "shared":
                return [(None, wq_s[:, :])]
            if j == MID:
                return [(0, wq[:, ds(2 * i, 1), :].rearrange("p e c -> p (e c)")),
                        (1, wq[:, ds(2 * i + 1, 1), :].rearrange("p e c -> p (e c)"))]
            return [(None, wq[:, ds(2 * i + (1 if j > MID else 0), 1), :].rearrange("p e c -> p (e c)"))]

        def mlp_step(kind, i, j, t1=True):
            if t1:
                _, ii, jj, g = tile_at(kind, i, j, 0)
                need(pe, q.q_tc, g)
                if kind == "expert" and isinstance(i, int) and j == 0:
                    pe.wait_ge(q.w_out, WC * (E + 1))
                if kind == "expert" and j == 0:
                    pe.wait_ge(q.rows_in, i + 1)
                for k in range(KD):
                    last = nc.tensor.transpose(bank_b[QT][:, k * P:(k + 1) * P], rows_of(kind, i, j, slice(k * P, (k + 1) * P)), id_b[:, :])
                last.then_inc(q.q_tp, 1)
            back1 = tile_at(kind, i, j, 1) if t1 or j == 0 else None
            if back1:
                kd, ii, jj, g = back1
                pe.wait_ge(q.q_tc, g + 1)
                r = jj % 2
                same = kd == "expert" and jj == 0 and not (isinstance(ii, int) and ii == 0)
                need(pe, q.hmul, g if same else g - 1)
                for out_bank, c0 in ((GB[r], 0), (YB[r], I)):
                    seq = [(m, w, k) for m, w in weights(kd, ii, jj) for k in range(KD)]
                    for n, (m, w, k) in enumerate(seq):
                        lhs = q_t[:, turned_of(kd, jj), k, :] if m is None else (q_ta, q_tb)[m][:, k, :]
                        last = mm(bank[out_bank][:, :], lhs, w[:, k * 2 * I + c0:k * 2 * I + c0 + I],
                                  start=n == 0, stop=n == len(seq) - 1)
                last.then_inc(q.gu, 1)
            back5 = tile_at(kind, i, j, 5)
            if back5:
                kd, ii, jj, g = back5
                pe.wait_ge(q.h_tc, g + 1)
                need(pe, q.y_ok, g)
                seq = [(m, w, k) for m, w in weights(kd, ii, jj) for k in range(KI)]
                for n, (m, w, k) in enumerate(seq):
                    lhs = h_t[:, k, :] if m is None else (h_ta, h_tb)[m][:, k, :]
                    last = mm(bank[DN][:, 0:D], lhs, w[:, GW + k * D:GW + (k + 1) * D], start=n == 0, stop=n == len(seq) - 1)
                last.then_inc(q.dn, 1)
            back4 = tile_at(kind, i, j, 4) if t1 or j < 4 else None
            if back4:
                kd, ii, jj, g = back4
                pe.wait_ge(q.hq2, g + 1)
                need(pe, q.h_tc, g)
                for k in range(KI):
                    last = nc.tensor.transpose(bank_b[HT][:, k * P:(k + 1) * P], hq[:, jj, k * P:(k + 1) * P], id_b[:, :])
                last.then_inc(q.h_tp, 1)

        pe.wait_ge(q.ml, 1)
        pe.wait_ge(q.w_out, WC * E)
        pe.wait_ge(q.built2, 4)
        steps(pe, "shared", mlp_step)
        steps(pe, "expert", mlp_step)
        for j in range(5):
            mlp_step("expert", E // 2, j, t1=False)

        def turn_x(p):
            need(pe, q.f_ok, 2 * (p - 1))
            for k in range(KD):
                for j in range(TP):
                    pe.wait_ge(q.comb, 2 * (TP * p + j + 1))
                    last = nc.tensor.transpose(bank[XT[k]][:, j * P:(j + 1) * P], gat[:, 2 * j, k * P:(k + 1) * P], id_f[:, :])
                last.then_inc(q.xt_ps, 1)

        def up(p, st):
            n, f = st // KF, st % KF
            fs = slice(f * P, (f + 1) * P)
            out = bank[HB[st % 3]]
            need(pe, q.h4l, 3 * KF * p + st - 2)
            if st == 0:
                pe.wait_ge(q.x4l, KD * p + KD)
            if n < 2:
                if f == 0 and isinstance(p, int) and p == 0:
                    pe.wait_ge(q.s_lo, 4 * n + 2)
                seq = [(w, x, k) for k in range(KD) for w, x in hlh(sw1[n], (x_hi, x_lo))]
                for m, (w, x, k) in enumerate(seq):
                    last = mm(out[:, :], w[:, k, fs], x[:, k, :], start=m == 0, stop=m == len(seq) - 1)
            else:
                if f == 0:
                    pe.wait_ge(q.tsp, 8 * p + 8)
                for b in range(2):
                    seq = [(w, x, k) for k in range(KD) for w, x in hlh(tw1[b], (x_hi, x_lo))]
                    for m, (w, x, k) in enumerate(seq):
                        last = mm(out[:, b * S:(b + 1) * S], w[:, k, fs], x[:, k, b * S:(b + 1) * S],
                                  start=b == 0 and m == 0, stop=m == len(seq) - 1, skip_group_check=True)
            last.then_inc(q.hp, 1)

        def down4(p, st):
            n, f = st // KF, st % KF
            pe.wait_ge(q.h4l, 3 * KF * p + st + 1)
            if f == 0:
                need(pe, q.ne_a, 3 * p + n)
                need(pe, q.ne_d, 3 * p + n)
                if n < 2 and isinstance(p, int) and p == 0:
                    pe.wait_ge(q.s_lo, 4 * n + 4)
            h = ring[st % 3]
            for m in range(KD):
                ms = slice(m * P, (m + 1) * P)
                for b in ((None,) if n < 2 else (0, 1)):
                    cs = slice(0, PR) if b is None else slice(b * S, (b + 1) * S)
                    w2 = sw2[n] if b is None else tw2[b]
                    for t, (w, x) in enumerate(hlh(w2, h)):
                        last = mm(bank[AC[m]][:, cs], w[:, f, ms], x[:, cs], start=f == 0 and t == 0 and b != 1,
                                  stop=f == KF - 1 and t == 2, skip_group_check=True)
            last.then_inc(q.l2d, 1)

        def gate1(p):
            pe.wait_ge(q.ne_d, 3 * p + 3)
            pe.wait_ge(q.ne_a, 3 * p + 3)
            for m in range(KD):
                for n, net in enumerate((2, 0, 1)):
                    for k in range(KD):
                        last = mm(bank[GT][:, 2 * m:2 * m + 2], g1_sb[:, n * KD + k, m * P:(m + 1) * P], nets[:, net, k, 0:PR:S],
                                  start=n == 0 and k == 0, stop=n == 2 and k == KD - 1)
            last.then_inc(q.g1_ps, 1)

        def gate2(p):
            pe.wait_ge(q.gt_ok, p + 1)
            for b in range(2):
                for m in range(KD):
                    last = mm(bank[GT][:, 8 + 3 * b:11 + 3 * b], gh_b[:, m, b, :], g2_sb[:, m, :], start=m == 0, stop=m == KD - 1)
            last.then_inc(q.g2_ps, 1)

        def fourier(p, last_pair=False):
            pe.wait_ge(q.zl, p + 1)
            pe.wait_ge(q.x4l, KD * p + KD if last_pair else KD * p + 2 * KD)
            for j in range(TP):
                seq = [(z, w, k) for k in range(KD) for z, w in ((z_hi, m_hi), (z_hi, m_lo), (z_lo, m_hi))]
                for n, (z, w, k) in enumerate(seq):
                    last = mm(bank[XT[j // 2]][:, (j % 2) * D:(j % 2 + 1) * D], z[:, k, j * P:(j + 1) * P], w[:, k, :],
                              start=n == 0, stop=n == len(seq) - 1)
                if j % 2:
                    last.then_inc(q.f_ps, 1)

        def mix(p, prev, pre):
            for st in range(3 * KF):
                up(p, st)
                if st >= 2:
                    down4(p, st - 2)
                if prev:
                    if st == 2:
                        gate1(p - 1)
                    if st == 4:
                        gate2(p - 1)
                    if st == 13:
                        fourier(p - 1)
                if pre and st == 20:
                    turn_x(p + 1)
            down4(p, 3 * KF - 2)
            down4(p, 3 * KF - 1)

        pe.wait_ge(q.g1_in, 48)
        turn_x(0)
        mix(0, False, True)
        with pe.Fori(1, NP - 1) as p:
            mix(p, True, True)
        mix(NP - 1, True, False)
        gate1(NP - 1)
        gate2(NP - 1)
        fourier(NP - 1, True)

    @block.scalar
    def _(act):
        fn = nc.scalar.activation
        cp = nc.scalar.copy

        def x_high(p):
            act.wait_ge(q.x_in, 16 * (p + 1))
            need(act, q.h_ps, KF * p)
            cp(x_hi[:, :, :], x_raw[:, :, :]).then_inc(q.xh, 1)

        def low_high(p):
            act.wait_ge(q.low_ps, p + 1)
            need(act, q.h_ps, KF * p)
            fn(low[:, :], bank[LOW][0:R3, :], ACT.Copy, scale=2.0).then_inc(q.lowh, 1)

        def w_abs(n, c):
            act.wait_ge(w_in[c], 16 * (n + 1))
            fn(w_dst(n)[:, c * F:(c + 1) * F], w_raw[:, c * F:(c + 1) * F], ACT.Abs, accum_out=wsum[:, c:c + 1]).then_inc(q.w_abs, 1)

        def w_round(n, c):
            if c == 0:
                act.wait_ge(q.w_rec, 2 * n + 1)
            k = c // KD
            cs = slice(c * F, (c + 1) * F)
            fn(w_raw[:, cs], w_raw[:, cs], ACT.Identity, scale=wrec[:, k:k + 1], bias=RND).then_inc(q.w_rnd, 1)

        act.dma_start(w1_raw[:, :, :], a["w1T"]).then_inc(q.w1_in, 16)
        act.dma_start(w2_raw[:, :, 0:R], a["ca2"]).then_inc(q.w2_in, 16)
        act.dma_start(w2_raw[:, :, R:], a["w2T"]).then_inc(q.w2_in, 16)
        act.wait_ge(q.built, 7)
        x_high(0)
        act.wait_ge(q.w1_in, 16)
        cp(w1_hi[:, :, :], w1_raw[:, :, :]).then_inc(q.w1h, 1)
        low_high(0)
        act.wait_ge(q.w2_in, 32)
        cp(w2_hi[:, :, R:R2 + D], w2_raw[:, :, :]).then_inc(q.w2h, 1)
        def feed(p, prev, pre):
            for f in range(KF):
                act.wait_ge(q.h_ps, KF * p + f + 1)
                if f == 0:
                    need(act, q.l2_ps, TP * p)
                fn(h_hi[:, f, :], bank[HB[f % 3]][:, :], ACT.Relu).then_inc(q.hh, 1)
                if prev and f == 0:
                    c_out(p - 1, 2)
                    low_turned(p - 1, 3)
                    w_round(2 * p - 1, 1)
                if prev and f == 1:
                    c_out(p - 1, 3)
                    w_round(2 * p - 1, 2)
                if prev and 2 <= f < 2 + TP:
                    turned(p - 1, f - 2)
                if 2 <= f < 2 + WC:
                    w_abs(2 * p, f - 2)
                if prev and 4 <= f < 4 + TP:
                    c_round(p - 1, f - 4)
                if KF - 2 <= f:
                    w_round(2 * p, f - KF + 2)
            if pre:
                x_high(p + 1)
            w_round(2 * p, 2)
            n = 2 * p + 1
            low_out(p, 0)
            low_turned(p, 0)
            if pre:
                low_high(p + 1)
            w_abs(n, 0)
            low_out(p, 1)
            w_abs(n, 1)
            c_out(p, 0)
            low_turned(p, 1)
            low_out(p, 2)
            w_abs(n, 2)
            c_out(p, 1)
            low_turned(p, 2)
            low_out(p, 3)
            w_round(n, 0)

        def low_out(p, j):
            t = TP * p + j
            act.wait_ge(q.l2_ps, t + 1)
            need(act, q.low2t_ps, t)
            for c, dst in ((COLS[j // 2][2], slice(0, R)), (COLS[j // 2][3], slice(R, R2))):
                src = bank[OB[j]][:, c].rearrange("p (a r) -> p a r", a=1).broadcast_to([P, 3, R])
                fn(low2[:, :, dst], src, ACT.Copy, scale=2.0).then_inc(q.low2s, 1)

        def low_turned(p, j):
            t = TP * p + j
            act.wait_ge(q.low2t_ps, t + 1)
            need(act, q.c_ps, t)
            cp(low2t[:, :], bank[LT][0:R3, 0:P]).then_inc(q.low2h, 1)

        def c_out(p, j):
            t = TP * p + j
            act.wait_ge(q.c_ps, t + 1)
            if j == 0:
                need(act, q.cch, CC * p)
                need(act, q.ct_ps, TP * p)
                need(act, q.cq1, TP * p)
                need(act, q.lg_ps, TP * p)
                need(act, q.cq2, TP * p)
            need(act, q.csq, t)
            src = bank[OB[j]][:, COLS[j // 2][1]]
            fn(c_junk[:, :], src, ACT.Square, accum_out=cst[:, 0, j:j + 1]).then_inc(q.csq, 1)
            cp(c_sb[:, j, :], src).then_inc(q.c_done, 1)

        def c_round(p, j):
            t = TP * p + j
            act.wait_ge(q.cch, CC * p + 7)
            if j:
                act.wait_ge(q.cq2, t)
            fn(c_tmp[:, :], c_sb[:, j, :], ACT.Identity, scale=cst[:, 6, j:j + 1], bias=RND).then_inc(q.cq1, 1)

        def turned(p, j):
            t = TP * p + j
            act.wait_ge(q.ct_ps, t + 1)
            if j:
                act.wait_ge(q.lg_ps, t)
            cp(c_t[:, :, :].rearrange("p k d -> p (k d)"), bank[CT][:, 0:D]).then_inc(q.ct_sb, 1)

        feed(0, False, True)
        with act.Fori(1, NP - 1) as p:
            feed(p, True, True)
        feed(NP - 1, True, False)
        c_out(NP - 1, 2)
        low_turned(NP - 1, 3)
        c_out(NP - 1, 3)
        w_round(E - 1, 1)
        w_round(E - 1, 2)
        for j in range(TP):
            turned(NP - 1, j)
        for j in range(TP):
            c_round(NP - 1, j)
        for c in range(WC):
            w_abs(E, c)

        act.wait_ge(q.r_sub, 1)
        fn(rt[1][:, :, :], rt[0][:, :, :], ACT.Exp).then_inc(q.r_exp, 1)

        act.wait_ge(q.m1, 1)
        cp(a_re[:, :, :].rearrange("p k d -> p (k d)"), bank[0][:, :]).then_inc(q.m1e, 1)
        cp(a_im[:, :, :].rearrange("p k d -> p (k d)"), bank[1][:, :]).then_inc(q.m1e, 1)
        act.wait_ge(q.m2, 1)
        fn(m_hi[:, :, :].rearrange("p k d -> p (k d)"), bank[2][:, :], ACT.Copy, scale=1.0 / D).then_inc(q.mh, 1)

        def s_high(i, k):
            act.wait_ge(s_in[k], 16 * i)
            cp(sw[:, ds(i - 1, 1), 0, k, :].rearrange("p a f -> p (a f)"), raw[k][:, :]).then_inc(q.s_hi, 1)

        def mlp_step(kind, i, j, t1=True):
            def at(lag):
                return tile_at(kind, i, j, lag) if t1 or j < lag else None
            if kind == "expert" and t1 and not isinstance(i, int) and j >= TE - 2:
                if j == TE - 2:
                    act.wait_ge(q.rows_in, E // 2)
                s_high(i, j - TE + 2)
            if at(5):
                kd, ii, jj, g = at(5)
                act.wait_ge(q.h_tp, g + 1)
                need(act, q.dn, g)
                src = bank_b[HT][:, 0:I]
                if kd == "expert" and jj == MID:
                    src = src.rearrange("p (k c) -> p k c", k=KI)
                    cp(h_ta[:, :, 0:HALF], src[:, :, 0:HALF])
                    cp(h_tb[:, :, HALF:], src[:, :, HALF:]).then_inc(q.h_tc, 1)
                else:
                    cp(h_t[:, :, :].rearrange("p k c -> p (k c)"), src).then_inc(q.h_tc, 1)
            if at(1):
                kd, ii, jj, g = at(1)
                act.wait_ge(q.gu, g + 1)
                act.wait_ge(q.msg, g + 1)
                need(act, q.hmul, g)
                fn(g_sb[:, :], bank[GB[jj % 2]][:, :], ACT.Silu, scale=mst[:, jj, 2:3]).then_inc(q.silu, 1)
            if at(3):
                kd, ii, jj, g = at(3)
                act.wait_ge(q.mch, 6 * g + 5)
                fn(hf[:, jj, :], hf[:, jj, :], ACT.Identity, scale=mst[:, jj, 6:7], bias=RND).then_inc(q.hq1, 1)
            if at(1):
                kd, ii, jj, g = at(1)
                act.wait_ge(q.hmul, g + 1)
                need(act, q.mch, 6 * (g - 3))
                need(act, q.hsq, g)
                fn(m_junk[:, :], hf[:, jj, :], ACT.Square, accum_out=mst[:, jj, 0:1]).then_inc(q.hsq, 1)
            if kind == "shared" and isinstance(i, int) and i == 0 and j < WC:
                w_round(E, j)

        steps(act, "shared", mlp_step)
        steps(act, "expert", mlp_step)
        for j in range(5):
            mlp_step("expert", E // 2, j, t1=False)

        act.wait_ge(q.y_ok, NT + ST)
        for k in range(TE):
            act.wait_ge(y_out[k], 16 * (E // 2) + 1)
        for k in range(2):
            s_high(E // 2, k)

        def x4_high(p):
            for k in range(KD):
                act.wait_ge(q.xt_ps, KD * p + k + 1)
                need(act, q.hp, 3 * KF * p)
                cp(x_hi[:, k, :], bank[XT[k]][:, :]).then_inc(q.x4h, 1)

        def net_out(p, n):
            act.wait_ge(q.l2d, 3 * KF * p + KF * (n + 1))
            if n == 0:
                need(act, q.zl, p)
                need(act, q.zh, p)
            else:
                need(act, q.f_ps, 2 * p)
            cp(nets[:, n, 0, :], bank[AC[0]][:, :]).then_inc(q.ne_a, 1)

        def gate_hidden(p):
            act.wait_ge(q.g1_ps, p + 1)
            fn(gh[:, :, :].rearrange("p m b -> p (m b)"), bank[GT][:, 0:2 * KD], ACT.Relu).then_inc(q.gh_ok, 1)

        def gate_exp(p):
            act.wait_ge(q.gch, 12 * p + 3)
            fn(gl[:, 3, :, :], gl[:, 2, :, :], ACT.Exp).then_inc(q.gexp, 1)

        def z_high(p):
            act.wait_ge(q.gch, 12 * p + 12)
            cp(z_hi[:, :, :], nets[:, 0, :, :]).then_inc(q.zh, 1)

        def type_high(p, c):
            act.wait_ge(t_in[c % 2], 16 * (4 * p + c // 2 + 1))
            if c == 0:
                need(act, q.l2d, 3 * KF * p)
            cp(split_dst(tw1, tw2, c // 4, c % 4, 0), raw[c % 2][:, :]).then_inc(q.thi, 1)

        def mix(p, prev, pre):
            for st in range(3 * KF):
                act.wait_ge(q.hp, 3 * KF * p + st + 1)
                need(act, q.l2d, 3 * KF * p + st - 2)
                fn(ring[st % 3][0][:, :], bank[HB[st % 3]][:, :], ACT.Relu).then_inc(q.h4h, 1)
                if st in (KF + 1, 2 * KF + 1):
                    net_out(p, st // KF - 1)
                if st < 8 and (prev or st >= 2):
                    type_high(p, st)
                if prev and st == 2:
                    gate_hidden(p - 1)
                if prev and st == 5:
                    gate_exp(p - 1)
                if prev and st == 8:
                    z_high(p - 1)
            if pre:
                x4_high(p + 1)
            net_out(p, 2)

        x4_high(0)
        type_high(0, 0)
        type_high(0, 1)
        mix(0, False, True)
        with act.Fori(1, NP - 1) as p:
            mix(p, True, True)
        mix(NP - 1, True, False)
        gate_hidden(NP - 1)
        gate_exp(NP - 1)
        z_high(NP - 1)

    @block.vector
    def _(v):
        ts, tt, stt, red = (nc.vector.tensor_scalar, nc.vector.tensor_tensor, nc.vector.scalar_tensor_tensor,
                            nc.vector.tensor_reduce)

        def x_low(p):
            v.wait_ge(q.xh, p + 1)
            tt(x_lo[:, :, :], x_raw[:, :, :], x_hi[:, :, :].bitcast(F32), ALU.subtract).then_inc(q.xl, 1)

        def low_low(p):
            v.wait_ge(q.lowh, p + 1)
            stt(low[R2:2 * R2, :], bank[LOW][R2:2 * R2, :], 2.0, low[R2:2 * R2, :].bitcast(F32), ALU.mult, ALU.subtract).then_inc(q.lowl, 1)

        def w_recip(n):
            v.wait_ge(q.w_m, 4 * (n + 1))
            nc.vector.reciprocal(wrec[:, :], wsum[:, 4:6]).then_inc(q.w_rec, 1)
            nc.vector.tensor_copy(flat(wscale[:, ds(n, 1), :]), wsum[:, 4:6]).then_inc(q.w_rec, 1)

        def w_clip(n, c):
            cs = slice(c * F, (c + 1) * F)
            v.wait_ge(q.w_rnd, WC * n + c + 1)
            ts(w_raw[:, cs], w_raw[:, cs], ROUND, -1.0, ALU.subtract, ALU.max).then_inc(q.w_clip, 1)
            v.wait_ge(q.w_clip, WC * n + c + 1)
            ts(w_dst(n)[:, cs], w_raw[:, cs], 1.0, None, ALU.min).then_inc(q.w_out, 1)

        def b_split(p, half):
            v.wait_ge(q.b_in, 48 * (2 * p + half + 1))
            need(v, q.h_ps, KF * p)
            nc.vector.tensor_copy(b_st[:, half, :], b_raw[:, :]).then_inc(q.b_sp, 1)
            v.wait_ge(q.b_sp, 4 * p + 2 * half + 1)
            rows = slice(2 * R2, R3)
            tt(b_st[rows, half, :], b_raw[rows, :], b_st[rows, half, :].bitcast(F32), ALU.subtract).then_inc(q.b_sp, 1)

        x_low(0)
        v.wait_ge(q.c_in, 16 * 3)
        b_split(0, 0)
        v.wait_ge(q.w1h, 1)
        tt(w1_lo[:, :, :], w1_raw[:, :, :], w1_hi[:, :, :].bitcast(F32), ALU.subtract).then_inc(q.w1l, 1)
        low_low(0)
        b_split(0, 1)
        v.wait_ge(q.w2h, 1)
        tt(w2_lo[:, :, R:R2 + D], w2_raw[:, :, :], w2_hi[:, :, R:R2 + D].bitcast(F32), ALU.subtract).then_inc(q.w2l, 1)

        def logit_out(p, j):
            t = TP * p + j
            v.wait_ge(q.lg_ps, t + 1)
            nc.vector.tensor_copy(flat(logits[:, ds(t, 1), :]), bank[LG][:, 0:E]).then_inc(q.lg_sb, 1)

        def low_turned(p, j):
            v.wait_ge(q.low2h, TP * p + j + 1)
            tt(low2t[R2:2 * R2, :], bank[LT][R2:2 * R2, 0:P], low2t[R2:2 * R2, :].bitcast(F32), ALU.subtract).then_inc(q.low2l, 1)

        def c_max(p, j):
            t = TP * p + j
            v.wait_ge(q.c_done, t + 1)
            if j == 0:
                need(v, q.cch, CC * p)
            red(cst[:, 1, j:j + 1], c_sb[:, j, :], X, ALU.max, apply_absolute_value=True).then_inc(q.camax, 1)

        def c_quant(p, j):
            t = TP * p + j
            v.wait_ge(q.cq1, t + 1)
            ts(flat(q_all[:, ds(t, 1), 0:D]), c_tmp[:, :], ROUND, None, ALU.subtract).then_inc(q.cq2, 1)

        def feed(p, prev, pre):
            for f in range(KF):
                v.wait_ge(q.hh, KF * p + f + 1)
                stt(h_lo[:, f, :], bank[HB[f % 3]][:, :], 0.0, h_hi[:, f, :].bitcast(F32), ALU.max, ALU.subtract).then_inc(q.hl, 1)
                if prev and f == 0:
                    c_max(p - 1, 2)
                    low_turned(p - 1, 3)
                    w_clip(2 * p - 1, 1)
                if prev and f == 1:
                    c_max(p - 1, 3)
                    w_clip(2 * p - 1, 2)
                if f == 5:
                    w_recip(2 * p)
                if prev and 3 <= f < 3 + TP:
                    logit_out(p - 1, f - 3)
                if prev and 5 <= f < 4 + TP:
                    c_quant(p - 1, f - 5)
                if f == KF - 1:
                    w_clip(2 * p, 0)
            if prev:
                c_quant(p - 1, TP - 1)
            if pre:
                x_low(p + 1)
            w_clip(2 * p, 1)
            w_clip(2 * p, 2)
            if pre:
                b_split(p + 1, 0)
            low_turned(p, 0)
            if pre:
                low_low(p + 1)
            n = 2 * p + 1
            low_turned(p, 1)
            if pre:
                b_split(p + 1, 1)
            c_max(p, 0)
            c_max(p, 1)
            low_turned(p, 2)
            w_recip(n)
            w_clip(n, 0)

        feed(0, False, True)
        with v.Fori(1, NP - 1) as p:
            feed(p, True, True)
        feed(NP - 1, True, False)
        c_max(NP - 1, 2)
        low_turned(NP - 1, 3)
        c_max(NP - 1, 3)
        w_clip(E - 1, 1)
        for j in range(TP):
            logit_out(NP - 1, j)
        w_clip(E - 1, 2)
        for j in range(TP):
            c_quant(NP - 1, j)

        count = [0]

        def step():
            v.wait_ge(q.route, count[0])

        def done():
            count[0] += 1
            return q.route, 1

        full = [P, NT, E]

        def over(c):
            return c[:, :].rearrange("p (t a) -> p t a", a=1).broadcast_to(full)

        def each(c):
            return c[:, :].rearrange("p (a e) -> p a e", a=1).broadcast_to(full)

        v.wait_ge(q.lg_sb, NT)
        v.wait_ge(q.built2, 9)
        v.wait_ge(q.cch, CC * NP)
        tt(logits[:, :, :], logits[:, :, :], over(rinv), ALU.mult).then_inc(*done())
        step()
        red(c16[0][:, :], logits[:, :, :], X, ALU.max).then_inc(*done())
        step()
        tt(rt[0][:, :, :], logits[:, :, :], over(c16[0]), ALU.subtract).then_inc(q.r_sub, 1)
        v.wait_ge(q.r_exp, 1)
        red(c16[1][:, :], rt[1][:, :, :], X, ALU.add).then_inc(*done())
        step()
        nc.vector.reciprocal(c16[2][:, :], c16[1][:, :]).then_inc(*done())
        step()
        tt(rt[2][:, :, :], rt[1][:, :, :], over(c16[2]), ALU.mult).then_inc(*done())
        step()

        def best(probs, weight, place, eq, one):
            red(weight[:, :], probs[:, :, :], X, ALU.max).then_inc(*done())
            step()
            tt(eq[:, :, :], probs[:, :, :], over(weight), ALU.is_equal).then_inc(*done())
            step()
            tt(eq[:, :, :], eq[:, :, :], each(rev8), ALU.mult).then_inc(*done())
            step()
            red(place[:, :], eq[:, :, :], X, ALU.max).then_inc(*done())
            step()
            tt(one[:, :, :], eq[:, :, :], over(place), ALU.is_equal).then_inc(*done())
            step()

        best(rt[2], c16[3], c16[4], rt[4], rt[3])
        stt(rt[6][:, :, :], rt[3][:, :, :], -2.0, rt[2][:, :, :], ALU.mult, ALU.add).then_inc(*done())
        step()
        best(rt[6], c16[5], c16[6], rt[4], rt[5])
        ts(c16[7][:, :], c16[5][:, :], 0.0, None, ALU.is_gt).then_inc(*done())
        step()
        tt(rt[5][:, :, :], rt[5][:, :, :], over(c16[7]), ALU.mult).then_inc(*done())
        step()
        tt(sel_b[:, :, :], rt[3][:, :, :], rt[5][:, :, :], ALU.add).then_inc(q.r_ps, 1)

        v.wait_ge(q.r_inv, 1)
        totals = bank[RB][:, NT * E:2 * NT * E].rearrange("p (t e) -> p t e", e=E)
        inner = bank[RB][:, 0:NT * E].rearrange("p (t e) -> p t e", e=E)
        nc.vector.memset(cum[0][:, 0:1, :], 0.0).then_inc(*done())
        nc.vector.tensor_copy(cum[0][:, 1:NT + 1, :], totals).then_inc(*done())
        step()
        src, d = 0, 1
        while d < NT:
            tt(cum[1 - src][:, d:, :], cum[src][:, d:, :], cum[src][:, 0:NT + 1 - d, :], ALU.add).then_inc(*done())
            nc.vector.tensor_copy(cum[1 - src][:, 0:d, :], cum[src][:, 0:d, :]).then_inc(*done())
            step()
            src, d = 1 - src, 2 * d
        tt(rt[4][:, :, :], inner, cum[src][:, 0:NT, :], ALU.add).then_inc(q.cnt_rd, 1)
        v.wait_ge(q.cnt_rd, 1)
        stt(rt[6][:, :, :], rt[4][:, :, :], float(CAP), sel_b[:, :, :], ALU.is_le, ALU.mult).then_inc(*done())
        tt(rt[7][:, :, :], rt[4][:, :, :], each(e_off), ALU.add).then_inc(*done())
        step()
        tt(rt[7][:, :, :], rt[7][:, :, :], rt[6][:, :, :], ALU.mult).then_inc(*done())
        step()
        for k, (one, weight) in enumerate(((rt[3], c16[3]), (rt[5], c16[5]))):
            slot = c16[8 + k]
            tt(rt[0][:, :, :], rt[7][:, :, :], one[:, :, :], ALU.mult).then_inc(*done())
            tt(rt[1][:, :, :], rt[6][:, :, :], one[:, :, :], ALU.mult).then_inc(*done())
            step()
            red(slot[:, :], rt[0][:, :, :], X, ALU.add).then_inc(*done())
            red(c16[0][:, :], rt[1][:, :, :], X, ALU.add).then_inc(*done())
            step()
            ts(slot[:, :], slot[:, :], float(DUMP), None, ALU.add).then_inc(*done())
            tt(wts[:, k, :], c16[0][:, :], weight[:, :], ALU.mult).then_inc(*done())
            step()
            nc.vector.tensor_copy(slots[:, k, :], slot[:, :]).then_inc(*done())
            ts(c16[1 + 4 * k][:, :], slot[:, :], -(P - 1) / 2, 1.0 / P, ALU.add, ALU.mult).then_inc(*done())
            step()
            ts(c16[1 + 4 * k][:, :], c16[1 + 4 * k][:, :], ROUND, ROUND, ALU.add, ALU.subtract).then_inc(*done())
            step()
            stt(c16[2 + 4 * k][:, :], c16[1 + 4 * k][:, :], -float(P), slot[:, :], ALU.mult, ALU.add).then_inc(*done())
            step()

        for k in range(2):
            tile, place = c16[1 + 4 * k], c16[2 + 4 * k]

            def wide(c, n):
                return c[:, :].rearrange("p (t a) -> p t a", a=1).broadcast_to([P, NT, n])

            def row(c, n):
                return c[:, :].rearrange("p (a e) -> p a e", a=1).broadcast_to([P, NT, n])

            tt(oh_c[:, k, :, :], row(iota_c, ST), wide(tile, ST), ALU.is_equal).then_inc(q.oh_ok, 1)
            v.wait_ge(q.oh_ok, 3 * k + 1)
            tt(oh_c[:, k, :, :], oh_c[:, k, :, :], wide(tokid, ST), ALU.mult).then_inc(q.oh_ok, 1)
            tt(oh_p[:, k, :, :], row(iota_p, P), wide(place, P), ALU.is_equal).then_inc(q.oh_ok, 1)
        w_recip(E)
        v.wait_ge(q.mh, 1)
        stt(m_lo[:, :, :].rearrange("p k d -> p (k d)"), bank[2][:, :], 1.0 / D,
            m_hi[:, :, :].rearrange("p k d -> p (k d)").bitcast(F32), ALU.mult, ALU.subtract).then_inc(q.ml, 1)
        v.wait_ge(q.oh_used, 1)
        nc.vector.tensor_copy(inv[:, :], bank[RB][:, 0:ST]).then_inc(q.inv_ok, 1)

        def s_low(i, k):
            v.wait_ge(q.s_hi, 2 * (i - 1) + k + 1)
            hi, lo = (sw[:, ds(i - 1, 1), c, k, :].rearrange("p a f -> p (a f)") for c in range(2))
            tt(lo, raw[k][:, :], hi.bitcast(F32), ALU.subtract).then_inc(q.s_lo, 1)

        def mlp_step(kind, i, j, t1=True):
            def at(lag):
                return tile_at(kind, i, j, lag) if t1 or j < lag else None
            if kind == "shared" and isinstance(i, int) and i == 1 and j < WC:
                w_clip(E, j)
            if at(0):
                kd, ii, jj, g = at(0)
                v.wait_ge(q.q_tp, g + 1)
                need(v, q.gu, g - 1)
                src = bank_b[QT][:, 0:D]
                if kd == "expert" and jj == MID:
                    src = src.rearrange("p (k c) -> p k c", k=KD)
                    nc.vector.tensor_copy(q_ta[:, :, 0:HALF], src[:, :, 0:HALF])
                    nc.vector.tensor_copy(q_tb[:, :, HALF:], src[:, :, HALF:]).then_inc(q.q_tc, 1)
                else:
                    nc.vector.tensor_copy(q_t[:, turned_of(kd, jj), :, :].rearrange("p k c -> p (k c)"), src).then_inc(q.q_tc, 1)
            if at(1):
                kd, ii, jj, g = at(1)
                v.wait_ge(q.silu, g + 1)
                need(v, q.hq2, g - 3)
                stt(hf[:, jj, :], bank[YB[jj % 2]][:, :], mst[:, jj, 2:3], g_sb[:, :], ALU.mult, ALU.mult).then_inc(q.hmul, 1)
                v.wait_ge(q.hmul, g + 1)
                need(v, q.mch, 6 * (g - 3))
                red(mst[:, jj, 1:2], hf[:, jj, :], X, ALU.max, apply_absolute_value=True).then_inc(q.hmax, 1)
            if kind == "expert" and t1 and not isinstance(i, int) and j >= TE - 2:
                s_low(i, j - TE + 2)
            if at(3):
                kd, ii, jj, g = at(3)
                v.wait_ge(q.hq1, g + 1)
                need(v, q.h_tp, g - 3)
                ts(hq[:, jj, :], hf[:, jj, :], ROUND, None, ALU.subtract).then_inc(q.hq2, 1)
            if at(5):
                kd, ii, jj, g = at(5)
                v.wait_ge(q.dn, g + 1)
                v.wait_ge(q.mch, 6 * g + 6)
                if kd == "shared":
                    if isinstance(g, int) and g == 0:
                        v.wait_ge(q.xs_in, 16)
                    row = flat(xs[:, ds(g, 1), :])
                    stt(row, bank[DN][:, 0:D], mst[:, jj, 8:9], row, ALU.mult, ALU.add).then_inc(q.y_ok, 1)
                else:
                    v.wait_ge(y_out[jj], 16 * ii + 1)
                    ts(ys[:, jj, :], bank[DN][:, 0:D], mst[:, jj, 8:9], None, ALU.mult).then_inc(q.y_ok, 1)

        steps(v, "shared", mlp_step)
        steps(v, "expert", mlp_step)
        for j in range(5):
            mlp_step("expert", E // 2, j, t1=False)

        for k in range(2):
            s_low(E // 2, k)

        def combine(p, j):
            t = TP * p + j
            v.wait_ge(gath[j], 32 * (p + 1))
            row = flat(xs[:, ds(t, 1), :])
            stt(row, gat[:, 2 * j, :], flat(wts[:, 0:1, ds(t, 1)]), row, ALU.mult, ALU.add).then_inc(q.comb, 1)
            v.wait_ge(q.comb, 2 * t + 1)
            stt(gat[:, 2 * j, :], gat[:, 2 * j + 1, :], flat(wts[:, 1:2, ds(t, 1)]), row, ALU.mult, ALU.add).then_inc(q.comb, 1)

        def x4_low(p):
            for k in range(KD):
                v.wait_ge(q.x4h, KD * p + k + 1)
                tt(x_lo[:, k, :], bank[XT[k]][:, :], x_hi[:, k, :].bitcast(F32), ALU.subtract).then_inc(q.x4l, 1)

        def net_out(p, n):
            v.wait_ge(q.l2d, 3 * KF * p + KF * (n + 1))
            if n == 0:
                need(v, q.zl, p)
                need(v, q.zh, p)
            else:
                need(v, q.f_ps, 2 * p)
            nc.vector.tensor_copy(nets[:, n, 1, :], bank[AC[1]][:, :]).then_inc(q.ne_d, 1)

        def gate_spread(p):
            v.wait_ge(q.gh_ok, p + 1)
            nc.vector.tensor_copy(gh_b[:, :, :, :].rearrange("p m b c -> p (m b) c"),
                                  gh[:, :, :].rearrange("p m (b a) -> p (m b) a", a=1).broadcast_to([P, 2 * KD, P])).then_inc(q.gt_ok, 1)

        def three(col):
            return col.broadcast_to([P, 2, 3])

        def gate_max(p):
            g0 = 12 * p
            v.wait_ge(q.g2_ps, p + 1)
            nc.vector.tensor_copy(gl[:, 0, :, :].rearrange("p b n -> p (b n)"), bank[GT][:, 8:14]).then_inc(q.gch, 1)
            v.wait_ge(q.gch, g0 + 1)
            red(gl[:, 1, :, 0], gl[:, 0, :, :], X, ALU.max).then_inc(q.gch, 1)
            v.wait_ge(q.gch, g0 + 2)
            tt(gl[:, 2, :, :], gl[:, 0, :, :], three(gl[:, 1, :, 0:1]), ALU.subtract).then_inc(q.gch, 1)

        def gate_norm(p):
            g0 = 12 * p
            v.wait_ge(q.gexp, p + 1)
            red(gl[:, 4, :, 0], gl[:, 3, :, :], X, ALU.add).then_inc(q.gch, 1)
            v.wait_ge(q.gch, g0 + 4)
            nc.vector.reciprocal(gl[:, 5, :, 0:1], gl[:, 4, :, 0:1]).then_inc(q.gch, 1)
            v.wait_ge(q.gch, g0 + 5)
            tt(gl[:, 6, :, :], gl[:, 3, :, :], three(gl[:, 5, :, 0:1]), ALU.mult).then_inc(q.gch, 1)

        def mix_nets(p, part):
            g0 = 12 * p + 6 + 2 * part
            v.wait_ge(q.ne_a, 3 * p + 3)
            v.wait_ge(q.gch, g0)
            for b in range(2):
                c = slice(b * S, (b + 1) * S)
                weight = gl[:, 6, b, (1, 0, 2)[part]:(1, 0, 2)[part] + 1]
                out = nets[:, 0, :, c]
                if part == 0:
                    ts(out, out, weight, None, ALU.mult).then_inc(q.gch, 1)
                else:
                    stt(out, nets[:, (2, 1)[part - 1], :, c], weight, out, ALU.mult, ALU.add).then_inc(q.gch, 1)

        def z_low(p):
            v.wait_ge(q.zh, p + 1)
            tt(z_lo[:, :, :], nets[:, 0, :, :], z_hi[:, :, :].bitcast(F32), ALU.subtract).then_inc(q.zl, 1)

        def fourier_out(p, h):
            v.wait_ge(q.f_ps, 2 * p + h + 1)
            v.wait_ge(q.xb, p + 1)
            rows = xs[:, ds(TP * p + 2 * h, 2), :].rearrange("p t d -> p (t d)")
            tt(rows, bank[XT[h]][:, :], rows, ALU.add).then_inc(q.f_ok, 1)

        def mix(p, prev, pre):
            for st in range(3 * KF):
                v.wait_ge(q.h4h, 3 * KF * p + st + 1)
                hi, lo = ring[st % 3]
                stt(lo[:, :], bank[HB[st % 3]][:, :], 0.0, hi[:, :].bitcast(F32), ALU.max, ALU.subtract).then_inc(q.h4l, 1)
                if st in (KF + 1, 2 * KF + 1):
                    net_out(p, st // KF - 1)
                if prev:
                    if st == 2:
                        gate_spread(p - 1)
                    if st == 4:
                        gate_max(p - 1)
                    if st == 5:
                        gate_norm(p - 1)
                        mix_nets(p - 1, 0)
                    if st in (6, 7):
                        mix_nets(p - 1, st - 5)
                    if st == 8:
                        z_low(p - 1)
                    if st in (14, 15):
                        fourier_out(p - 1, st - 14)
                if pre and 14 <= st < 14 + TP:
                    combine(p + 1, st - 14)
            if pre:
                x4_low(p + 1)
            net_out(p, 2)

        for j in range(TP):
            combine(0, j)
        x4_low(0)
        mix(0, False, True)
        with v.Fori(1, NP - 1) as p:
            mix(p, True, True)
        mix(NP - 1, True, False)
        last = NP - 1
        gate_spread(last)
        gate_max(last)
        gate_norm(last)
        for part in range(3):
            mix_nets(last, part)
        z_low(last)
        for h in range(2):
            fourier_out(last, h)

    @block.gpsimd
    def _(g):
        ts, tt, copy = nc.gpsimd.tensor_scalar, nc.gpsimd.tensor_tensor, nc.gpsimd.tensor_copy

        def hold(sem, value):
            need(g, sem, value)
            if not isinstance(value, int):
                g.sem_inc(q.pool_held, 1)

        for k, value in enumerate((-0.5, -1.0, 1.0 / 127.0, ROUND)):
            nc.gpsimd.memset(consts[:, k:k + 1], value).then_inc(q.built, 1)
        nc.gpsimd.memset(ones[:, :], 1.0).then_inc(q.built, 1)
        nc.gpsimd.memset(triu[:, :], 1.0).then_inc(q.built, 1)
        hold(q.built, 6)
        nc.gpsimd.affine_select(out=triu[:, :], in_=triu[:, :], pattern=[[1, P]], compare_op=ALU.is_ge, fill=0.0,
                                base=0, channel_multiplier=-1).then_inc(q.built, 1)
        for n, t in enumerate((id_f, id_b)):
            nc.gpsimd.memset(t[:, :], 0.0).then_inc(q.id0, 1)
            hold(q.id0, 2 * n + 1)
            nc.gpsimd.affine_select(out=t[:, :], in_=t[:, :], pattern=[[-1, P]], compare_op=ALU.not_equal, fill=1.0,
                                    base=0, channel_multiplier=1).then_inc(q.id0, 1)

        def a_split(p):
            hold(q.a_in, 32 * (p + 1))
            hold(q.low_ps, p)
            raw3 = a_raw[:, :, :, :].rearrange("p b k (a r) -> p (b k) a r", a=1).broadcast_to([P, 2 * KD, 3, R2])
            hi, lo = (t[:, :, :, :].rearrange("p b k (a r) -> p (b k) a r", a=3) for t in (a_hi, a_lo))
            copy(hi, raw3).then_inc(q.a_sp, 1)
            hold(q.a_sp, 2 * p + 1)
            tt(lo, raw3, hi.bitcast(F32), ALU.subtract).then_inc(q.a_sp, 1)

        def second_split(p):
            hold(q.e2_in, 128 * (p + 1))
            hold(q.l2_ps, TP * p)
            for b, c in enumerate((slice(0, R), slice(R2 + D, W2C))):
                copy(w2_hi[:, :, c], e2a_raw[:, b, :, :]).then_inc(q.w2_sp, 1)
                hold(q.w2_sp, 4 * p + 2 * b + 1)
                tt(w2_lo[:, :, c], e2a_raw[:, b, :, :], w2_hi[:, :, c].bitcast(F32), ALU.subtract).then_inc(q.w2_sp, 1)

        def way_split(p):
            hold(q.c_ps, TP * p)
            copy(b2_st[:, :, :], b2_raw[:, :, :]).then_inc(q.b2_sp, 1)
            hold(q.b2_sp, 2 * p + 1)
            rows = slice(2 * R2, R3)
            tt(b2_st[rows, :, :], b2_raw[rows, :, :], b2_st[rows, :, :].bitcast(F32), ALU.subtract).then_inc(q.b2_sp, 1)
            hold(q.b2_sp, 2 * p + 2)

        def w_mean(n):
            hold(q.w_abs, WC * (n + 1))
            nc.gpsimd.partition_all_reduce(wsum[:, 3:6], wsum[:, 0:3], P, RADD).then_inc(q.w_m, 1)
            hold(q.w_m, 4 * n + 1)
            tt(wsum[:, 4:5], wsum[:, 3:4], wsum[:, 4:5], ALU.add).then_inc(q.w_m, 1)
            ts(wsum[:, 5:6], wsum[:, 5:6], 1.0 / (D * I), 1e-5, ALU.mult, ALU.max).then_inc(q.w_m, 1)
            hold(q.w_m, 4 * n + 2)
            ts(wsum[:, 4:5], wsum[:, 4:5], 1.0 / (2 * I * D), 1e-5, ALU.mult, ALU.max).then_inc(q.w_m, 1)

        hold(q.ca_in, 16 * 2)
        a_split(0)
        hold(q.cb_in, 16 * 6)
        hold(q.gw_in, 32)
        for k in range(KD):
            tt(gw[:, k, :], gw[:, k, :], gnorm[:, k:k + 1].broadcast_to([P, E]), ALU.mult).then_inc(q.gwok, 1)

        def c_chain(p):
            n = CC * p
            ssq, amax, var, r, m, rm, a_, v2, am, ra = (cst[:, c, :] for c in range(10))

            def four(c):
                return c.broadcast_to([P, TP])

            hold(q.csq, TP * (p + 1))
            hold(q.camax, TP * (p + 1))
            ts(var, ssq, 1.0 / D, 1e-8, ALU.mult, ALU.add).then_inc(q.cch, 1)
            hold(q.cch, n + 1)
            tt(r, var, four(MHALF), ALU.pow).then_inc(q.cch, 1)
            hold(q.cch, n + 2)
            tt(am, amax, r, ALU.mult).then_inc(q.cch, 1)
            hold(q.cch, n + 3)
            ts(m, am, 1e-5, None, ALU.max).then_inc(q.cch, 1)
            hold(q.cch, n + 4)
            tt(rm, m, four(MONE), ALU.pow).then_inc(q.cch, 1)
            hold(q.cch, n + 5)
            tt(ra, r, rm, ALU.mult).then_inc(q.cch, 1)
            hold(q.cch, n + 6)
            ts(a_, ra, 127.0, None, ALU.mult).then_inc(q.cch, 1)
            tt(q_all[:, ds(TP * p, TP), D:D + 2].bitcast(F32), m.rearrange("p (t a) -> p t a", a=1),
               I127.rearrange("p (t a) -> p t a", a=1).broadcast_to([P, TP, 1]), ALU.mult).then_inc(q.cch, 1)
            ts(v2, ssq, 1.0 / D, 1e-6, ALU.mult, ALU.add).then_inc(q.cch, 1)
            hold(q.cch, n + 9)
            tt(rinv[:, ds(TP * p, TP)], v2, four(MHALF), ALU.pow).then_inc(q.cch, 1)

        def feed(p, prev, pre):
            second_split(p)
            if prev:
                c_chain(p - 1)
            w_mean(2 * p)
            way_split(p)
            if pre:
                a_split(p + 1)
            hold(q.cq1, TP * p)
            w_mean(2 * p + 1)

        feed(0, False, True)
        with g.Fori(1, NP - 1) as p:
            feed(p, True, True)
        feed(NP - 1, True, False)
        c_chain(NP - 1)

        hold(q.h_ps, KF * NP)
        hold(q.l2_ps, NT)
        for t in (q_ta, q_tb, h_ta, h_tb):
            nc.gpsimd.memset(t[:, :, :], 0.0).then_inc(q.built2, 1)
        for t, step, base, cm in ((iota_p[:, :], [[1, P]], 0, 0), (iota_c[:, :], [[1, ST]], 0, 0), (tokid[:, :], [[P, NT]], 0, 1),
                                  (rev8[:, :], [[-1, E]], E, 0), (e_off[:, :], [[CAP, E]], -1 - DUMP, 0)):
            nc.gpsimd.iota(t, pattern=step, base=base, channel_multiplier=cm, allow_small_or_imprecise_dtypes=True).then_inc(q.built2, 1)
        w_mean(E)

        hold(q.w_rec, 2 * (E + 1))
        tt(wscale[:, :, 1], wscale[:, :, 1], I127.broadcast_to([P, E + 1]), ALU.mult).then_inc(q.tsc, 1)
        hold(q.tsc, 1)
        by_pair = wscale[:, 1:E + 1, :].rearrange("p (i h) c -> p i h c", h=2)
        tiles = tscale[:, :, :].rearrange("p (i j) c -> p i j c", j=TE)
        for rows, h, js in ((slice(0, P), 0, slice(0, MID)), (slice(0, P), 1, slice(MID + 1, TE)),
                            (slice(0, HALF), 0, slice(MID, MID + 1)), (slice(HALF, P), 1, slice(MID, MID + 1))):
            n = js.stop - js.start
            if rows.start:
                hold(q.tsc, 4)
            copy(tiles[rows, :, js, :], by_pair[rows, :, h:h + 1, :].broadcast_to([rows.stop - rows.start, E // 2, n, 2])).then_inc(q.tsc, 1)
        hold(q.tsc, 5)

        def gather(first, n):
            for t in range(first, first + n):
                g.indirect_dma_start(xg[:, t, :].bitcast(U32), None, q_d, bass.IndirectOffsetOnAxis(ap=inv[:, t:t + 1], axis=0)).then_inc(g_in[t // TE], 16)

        FIRST = (1, 1, 1, 1, 1, 1, 2, 2, 3, 3, 2, 2)

        def here(k):
            hold(g_in[k], 16 * TE)
            g.sem_inc(q.rows_in, 1)

        def scale_of(kd, jj, g_, c):
            if kd == "shared":
                return wscale[:, 0, c:c + 1]
            return flat(tscale[:, ds(g_ - NT, 1), c:c + 1])

        def mlp_step(kind, i, j, t1=True):
            if isinstance(i, int) and t1:
                n = TP * i + j if kind == "shared" else 2 * TP + j
                if n == 0:
                    hold(q.tsc, 5)
                    hold(q.inv_ok, 1)
                    hold(q.rows_ok, 1)
                if kind == "expert" and j < 2:
                    here(j)
                if n < len(FIRST):
                    gather(sum(FIRST[:n]), FIRST[n])
                else:
                    here(2)
                    here(3)
            if t1:
                kd, ii, jj, t = tile_at(kind, i, j, 0)
                hold(q.hmul, t - 3)
                rows = q_all[:, ds(t, 1), D:D + 2] if kd == "shared" else xg[:, ds(t - NT, 1), D:D + 2]
                tt(mst[:, jj, 2:3], flat(rows).bitcast(F32), scale_of(kd, jj, t, 0), ALU.mult).then_inc(q.msg, 1)
            if t1 or j < 1:
                back = tile_at(kind, i, j, 1)
                if back:
                    kd, ii, jj, t = back
                    ssq, amax, var, r, m, rm, a_, od = (mst[:, jj, c:c + 1] for c in (0, 1, 3, 4, 5, 7, 6, 8))
                    n = 6 * t
                    hold(q.hsq, t + 1)
                    hold(q.hmax, t + 1)
                    ts(var, ssq, 1.0 / I, 1e-8, ALU.mult, ALU.add).then_inc(q.mch, 1)
                    hold(q.mch, n + 1)
                    tt(r, var, MHALF, ALU.pow).then_inc(q.mch, 1)
                    hold(q.mch, n + 2)
                    ts(m, amax, r, 1e-5, ALU.mult, ALU.max).then_inc(q.mch, 1)
                    hold(q.mch, n + 3)
                    tt(rm, m, MONE, ALU.pow).then_inc(q.mch, 1)
                    hold(q.mch, n + 4)
                    hold(q.hq1, t - 3)
                    ts(a_, r, rm, 127.0, ALU.mult, ALU.mult).then_inc(q.mch, 1)
                    hold(q.y_ok, t - 3)
                    tt(od, m, scale_of(kd, jj, t, 1), ALU.mult).then_inc(q.mch, 1)

        steps(g, "shared", mlp_step)
        steps(g, "expert", mlp_step)
        mlp_step("expert", E // 2, 0, t1=False)

        def gather_rows(p):
            hold(q.xt_ps, KD * p)
            copy(gidx[:, :].rearrange("p (j k) -> p k j", k=2), slots[:, :, ds(TP * p, TP)]).then_inc(q.gix, 1)
            hold(q.gix, p + 1)
            for n in range(2 * TP):
                g.indirect_dma_start(gat[:, n, :], None, y_d, bass.IndirectOffsetOnAxis(ap=gidx[:, n:n + 1], axis=0)).then_inc(gath[n // 2], 16)

        def add_bias(p):
            hold(q.comb, 2 * TP * (p + 1))
            even = gat[:, :, :].rearrange("p (j k) d -> p j k d", k=2)[:, :, 0, :]
            tt(xs[:, ds(TP * p, TP), :], even, bias_b[:, :].rearrange("p (a d) -> p a d", a=1).broadcast_to([P, TP, D]),
               ALU.add).then_inc(q.xb, 1)

        def type_split(p):
            for c in range(8):
                hi, lo = (split_dst(tw1, tw2, c // 4, c % 4, k) for k in range(2))
                hold(q.thi, 8 * p + c + 1)
                tt(lo, raw[c % 2][:, :], hi.bitcast(F32), ALU.subtract).then_inc(q.tsp, 1)

        hold(q.y_ok, NT + ST)
        for k in range(TE):
            hold(y_out[k], 16 * (E // 2) + 1)
        gather_rows(0)
        type_split(0)
        hold(q.g1_in, 48)
        add_bias(0)
        gather_rows(1)
        with g.Fori(1, NP - 1) as p:
            type_split(p)
            add_bias(p)
            gather_rows(p + 1)
        type_split(NP - 1)
        add_bias(NP - 1)


def kernel(**inputs):
    import numpy as np
    import concourse.bacc as bacc
    from concourse.bass_utils import run_bass_kernel_spmd

    def x_of(name):
        return np.asarray(inputs[name])

    def rows(w, k):
        return np.swapaxes(w.reshape(*w.shape[:-2], k, P, w.shape[-1]), -3, -2)

    def turn(w):
        return np.swapaxes(w, -1, -2)

    x = x_of("x").reshape(N, D)
    c, t = "L0_cond_", "L0_attn_"
    n = np.arange(D)
    angle = 2.0 * np.pi * (np.outer(n, n) % D) / D
    dft = np.stack([np.cos(angle), np.sin(angle), -np.sin(angle)]).astype(np.float32)
    gates = np.concatenate([x_of(t + "shared_gate_w")[None], x_of(t + "expert_gate_w")])
    downs = np.concatenate([x_of(t + "shared_down_w")[None], x_of(t + "expert_down_w")])
    swi = np.swapaxes(rows(x_of("L0_cond2_swi"), KD), 1, 2)
    swo = np.swapaxes(rows(x_of("L0_cond2_swo"), KF).reshape(2, P, 2, F), 1, 2)
    arrays = {
        "x": x, "xT": rows(x.T, KD),
        "w1T": rows(turn(x_of(c + "wi")), KD), "w2T": rows(turn(x_of(c + "wo")), KF),
        "ca1": rows(turn(x_of(c + "common_wi_a")), KD), "cb1": turn(x_of(c + "common_wi_b")),
        "ca2": rows(turn(x_of(c + "common_wo_a")), KF), "cb2": turn(x_of(c + "common_wo_b")),
        "ea1": rows(turn(x_of(c + "experts_wi_a")), KD), "eb1": turn(x_of(c + "experts_wi_b")),
        "ea2": rows(turn(x_of(c + "experts_wo_a")), KF), "eb2": turn(x_of(c + "experts_wo_b")),
        "gate_wT": rows(turn(x_of(t + "gate_w")), KD), "gnorm": x_of(t + "gate_norm_w").reshape(KD, P).T,
        "gT": rows(turn(gates), KD), "dT": rows(turn(downs), KI),
        "ids": x_of("itok_B_0_7").reshape(1, B), "types": x_of("itok_B_0_2").reshape(1, B),
        "wi": rows(x_of("L0_cond2_wi"), KD), "wo": rows(x_of("L0_cond2_wo"), KF),
        "sw": np.stack([swi, swo], 1).reshape(4, 2, P, F),
        "g1": rows(x_of("L0_cond2_g1"), 3 * KD), "g2": rows(x_of("L0_cond2_g2"), KD),
        "fr": rows(x_of("L0_ffn_w_freq_real"), KD), "fi": rows(x_of("L0_ffn_w_freq_imag"), KD),
        "dft": np.swapaxes(rows(dft, KD), 0, 1), "bias": x_of("L0_ffn_bias").reshape(1, D),
    }
    nc = bacc.Bacc("TRN2", target_bir_lowering=False, num_devices=1)
    data, a = {}, {}
    for name, v in arrays.items():
        v = np.ascontiguousarray(v)
        data["in_" + name] = v
        a[name] = nc.dram_tensor("in_" + name, v.shape, mybir.dt.from_np(v.dtype), kind="ExternalInput").ap()
    a["out"] = nc.dram_tensor("out", (N, D), F32, kind="ExternalOutput").ap()
    build(nc, a)
    r = run_bass_kernel_spmd(nc, [data], core_ids=[0])
    return r.results[0]["out"].reshape(B, S, D)
```
